# Optimizing a Trainium2 kernel written in Bass

```python
import numpy as np
import jax
import jax.numpy as jnp

def _softmax(x, axis=-1):
    return jax.nn.softmax(x, axis=axis)

def _gelu(x):
    return jax.nn.gelu(x, approximate=True)

def _silu(x):
    return jax.nn.silu(x)

def _sigmoid(x):
    return jax.nn.sigmoid(x)

def _layernorm(x, axis=-1, eps=1e-05):
    m = jnp.mean(x, axis=axis, keepdims=True)
    v = jnp.var(x, axis=axis, keepdims=True)
    return (x - m) / jnp.sqrt(v + eps)

def _scatter_add(tgt, idx, src, axis=0):
    return tgt.at[idx].add(src)

def _segment_sum(src, seg, n):
    return jax.ops.segment_sum(src, seg, n)
kernel_name = 'mk_vit_tower_d1_tok_img1024_r4_778d4a'

def setup_inputs(seed: int=0):
    np.random.seed(seed)
    _w = jnp.asarray

    def _rec_inputs():
        import jax
        import jax.numpy as jnp
        _rk = jax.random.key(seed)
        x = -0.000169711 + 1.00022 * jax.random.normal(jax.random.fold_in(_rk, 1), (128, 3, 96, 96), jnp.float32)
        return x
    x = _rec_inputs()

    def _L0_tok_setup():
        import jax, jax.numpy as jnp
        import numpy as np
        C = 256
        H8 = 8
        DH = C // H8
        PS = 14
        CS = 3
        IMG = 168
        B = 4

        def _ln(x, g, b):
            mu = jnp.mean(x, axis=-1, keepdims=True)
            xc = x - mu
            var = jnp.mean(xc * xc, axis=-1, keepdims=True)
            return xc * jax.lax.rsqrt(var + 1e-05) * g + b

        def _forward(pixel_values, conv_w, class_emb, la_ln_q_g, la_ln_q_b, la_wq, la_ln_kv_g, la_ln_kv_b, la_wkv, la_proj_w, la_proj_b, ga_ln_q_g, ga_ln_q_b, ga_wq, ga_ln_kv_g, ga_ln_kv_b, ga_wkv, ga_proj_w, ga_proj_b, mod_w, mod_b):
            b = pixel_values.shape[0]
            pe = jax.lax.conv_general_dilated(pixel_values, conv_w, (PS, PS), 'VALID', dimension_numbers=('NCHW', 'OIHW', 'NCHW'))
            HP = pe.shape[2]
            h = HP // CS
            hw, N = (h * h, CS * CS)
            scale = C ** (-0.5)
            grid = pe.reshape(b, C, h, CS, h, CS)
            red = grid.mean(axis=(3, 5)).reshape(b, C, hw).transpose(0, 2, 1)
            win = grid.transpose(0, 2, 4, 3, 5, 1).reshape(b, hw, N, C)
            q = _ln(red, la_ln_q_g, la_ln_q_b) @ la_wq
            q = q.reshape(b, hw, H8, DH).transpose(0, 2, 1, 3)
            kv = _ln(win, la_ln_kv_g, la_ln_kv_b) @ la_wkv
            kv = kv.reshape(b, hw, N, 2, H8, DH).transpose(3, 0, 4, 1, 2, 5)
            k_, v_ = (kv[0], kv[1])
            attn = jax.nn.softmax(jnp.einsum('bhnd,bhnkd->bhnk', q * scale, k_), axis=-1)
            agg = jnp.einsum('bhnk,bhnkd->bhnd', attn, v_)
            agg = agg.transpose(0, 2, 1, 3).reshape(b, hw, C)
            local_out = red + agg @ la_proj_w + la_proj_b
            cls = jnp.broadcast_to(class_emb, (b, 1, C))
            gq = (_ln(cls, ga_ln_q_g, ga_ln_q_b) @ ga_wq).reshape(b, H8, DH)
            gkv = _ln(local_out, ga_ln_kv_g, ga_ln_kv_b) @ ga_wkv
            gkv = gkv.reshape(b, hw, 2, H8, DH).transpose(2, 0, 3, 1, 4)
            gk, gv = (gkv[0], gkv[1])
            gattn = jax.nn.softmax(jnp.einsum('bhd,bhnd->bhn', gq * scale, gk), axis=-1)
            gagg = jnp.einsum('bhn,bhnd->bhd', gattn, gv).reshape(b, 1, C)
            cls_out = cls + gagg @ ga_proj_w + ga_proj_b
            patch_out = local_out @ mod_w + mod_b
            return jnp.concatenate([patch_out, cls_out], axis=1)
        key = jax.random.key(seed)
        ks = jax.random.split(key, 16)
        nrm = lambda k, shape: jax.random.normal(k, shape, jnp.float32) * 0.02
        return {'pixel_values': jax.random.normal(ks[0], (B, 3, IMG, IMG), jnp.float32), 'pixel_masks': jnp.ones((B, 1, IMG, IMG), jnp.float32), 'conv_w': nrm(ks[1], (C, 3, PS, PS)), 'class_emb': nrm(ks[2], (C,)), 'la_ln_q_g': jnp.ones((C,)), 'la_ln_q_b': jnp.zeros((C,)), 'la_wq': nrm(ks[3], (C, C)), 'la_ln_kv_g': jnp.ones((C,)), 'la_ln_kv_b': jnp.zeros((C,)), 'la_wkv': nrm(ks[4], (C, 2 * C)), 'la_proj_w': nrm(ks[5], (C, C)), 'la_proj_b': jnp.zeros((C,)), 'ga_ln_q_g': jnp.ones((C,)), 'ga_ln_q_b': jnp.zeros((C,)), 'ga_wq': nrm(ks[6], (C, C)), 'ga_ln_kv_g': jnp.ones((C,)), 'ga_ln_kv_b': jnp.zeros((C,)), 'ga_wkv': nrm(ks[7], (C, 2 * C)), 'ga_proj_w': nrm(ks[8], (C, C)), 'ga_proj_b': jnp.zeros((C,)), 'mod_w': nrm(ks[9], (C, C)), 'mod_b': jnp.zeros((C,))}
    _L0_tok_all = _L0_tok_setup()
    _L0_tok_in = {k: v for k, v in _L0_tok_all.items() if k in ('pixel_masks', 'conv_w', 'class_emb', 'la_ln_q_g', 'la_ln_q_b', 'la_wq', 'la_ln_kv_g', 'la_ln_kv_b', 'la_wkv', 'la_proj_w', 'la_proj_b', 'ga_ln_q_g', 'ga_ln_q_b', 'ga_wq', 'ga_ln_kv_g', 'ga_ln_kv_b', 'ga_wkv', 'ga_proj_w', 'ga_proj_b', 'mod_w', 'mod_b')}
    del _L0_tok_all

    def _L0_attn_setup():
        import jax, jax.numpy as jnp
        import numpy as np
        B_SZ, SEQ = (2, 256)
        D_MODEL, D_STATE, D_CONV, EXPAND = (256, 16, 4, 2)
        D_INNER = EXPAND * D_MODEL
        DT_RANK = D_MODEL // 16

        def _layernorm(x, g, b):
            m = x.mean(-1, keepdims=True)
            v = ((x - m) ** 2).mean(-1, keepdims=True)
            return (x - m) * jax.lax.rsqrt(v + 1e-05) * g + b

        def _mamba(x, in_w, conv_w, conv_b, xproj_w, dt_w, dt_b, A_log, D_skip, out_w):
            B, L, _ = x.shape
            xz = x @ in_w.T
            xi, z = jnp.split(xz, 2, axis=-1)
            dc = conv_w.shape[1]
            xp = jnp.pad(xi, ((0, 0), (dc - 1, 0), (0, 0)))
            xc = conv_b + sum((xp[:, k:k + L, :] * conv_w[:, k] for k in range(dc)))
            xc = jax.nn.silu(xc)
            dbl = xc @ xproj_w.T
            n = A_log.shape[1]
            r = xproj_w.shape[0] - 2 * n
            dt, Bm, Cm = (dbl[..., :r], dbl[..., r:r + n], dbl[..., r + n:])
            delta = jax.nn.softplus(dt @ dt_w.T + dt_b)
            A = -jnp.exp(A_log)
            dA = jnp.exp(delta[..., None] * A)
            dBu = delta[..., None] * Bm[:, :, None, :] * xc[..., None]

            def step(h, inp):
                da, dbu, c = inp
                h = da * h + dbu
                return (h, jnp.einsum('bdn,bn->bd', h, c))
            h0 = jnp.zeros((B, delta.shape[-1], n), x.dtype)
            _, ys = jax.lax.scan(step, h0, (dA.swapaxes(0, 1), dBu.swapaxes(0, 1), Cm.swapaxes(0, 1)))
            y = ys.swapaxes(0, 1) + xc * D_skip
            return y * jax.nn.silu(z) @ out_w.T
        key = jax.random.key(seed)
        ks = jax.random.split(key, 16)

        def w(k, shape, s=0.02):
            return jax.random.normal(k, shape, jnp.float32) * s

        def mamba_params(k):
            kk = jax.random.split(k, 6)
            return dict(in_w=w(kk[0], (2 * D_INNER, D_MODEL)), conv_w=w(kk[1], (D_INNER, D_CONV), 0.1), conv_b=jnp.zeros((D_INNER,), jnp.float32), xproj_w=w(kk[2], (DT_RANK + 2 * D_STATE, D_INNER)), dt_w=w(kk[3], (D_INNER, DT_RANK), 0.1), dt_b=w(kk[4], (D_INNER,), 0.1), A_log=jnp.log(jnp.tile(jnp.arange(1, D_STATE + 1, dtype=jnp.float32), (D_INNER, 1))), D_skip=jnp.ones((D_INNER,), jnp.float32), out_w=w(kk[5], (D_MODEL, D_INNER)))
        inp = {'x': jax.random.normal(ks[0], (B_SZ, SEQ, D_MODEL), jnp.float32), 'ln_g': jnp.ones((D_MODEL,), jnp.float32), 'ln_b': jnp.zeros((D_MODEL,), jnp.float32)}
        for name, v in mamba_params(ks[1]).items():
            inp['f_' + name] = v
        for name, v in mamba_params(ks[2]).items():
            inp['b_' + name] = v
        return inp
    _L0_attn_all = _L0_attn_setup()
    _L0_attn_in = {k: v for k, v in _L0_attn_all.items() if k in ('ln_g', 'ln_b', 'f_in_w', 'f_conv_w', 'f_conv_b', 'f_xproj_w', 'f_dt_w', 'f_dt_b', 'f_A_log', 'f_D_skip', 'f_out_w', 'b_in_w', 'b_conv_w', 'b_conv_b', 'b_xproj_w', 'b_dt_w', 'b_dt_b', 'b_A_log', 'b_D_skip', 'b_out_w')}
    del _L0_attn_all

    def _L0_ffn_setup():
        import jax, jax.numpy as jnp
        import numpy as np
        B, S, H, E = (2, 2048, 256, 8)
        SCALE = 0.5
        key = jax.random.key(seed)
        k1, k2 = jax.random.split(key)
        x = jax.random.normal(k1, (B, S, H), dtype=jnp.float32)
        gate_w = jax.random.normal(k2, (E, H), dtype=jnp.float32) * 0.02
        coeff = SCALE * (1.0 + 0.05 * jnp.arange(E, dtype=jnp.float32))
        expert_w = coeff[:, None, None] * jnp.eye(H, dtype=jnp.float32)
        return {'x': x, 'gate_w': gate_w, 'expert_w': expert_w}
    _L0_ffn_all = _L0_ffn_setup()
    _L0_ffn_in = {k: v for k, v in _L0_ffn_all.items() if k in ('gate_w', 'expert_w')}
    del _L0_ffn_all
    return {'x': x, 'L0_tok_pixel_masks': _L0_tok_in['pixel_masks'], 'L0_tok_conv_w': _L0_tok_in['conv_w'], 'L0_tok_class_emb': _L0_tok_in['class_emb'], 'L0_tok_la_ln_q_g': _L0_tok_in['la_ln_q_g'], 'L0_tok_la_ln_q_b': _L0_tok_in['la_ln_q_b'], 'L0_tok_la_wq': _L0_tok_in['la_wq'], 'L0_tok_la_ln_kv_g': _L0_tok_in['la_ln_kv_g'], 'L0_tok_la_ln_kv_b': _L0_tok_in['la_ln_kv_b'], 'L0_tok_la_wkv': _L0_tok_in['la_wkv'], 'L0_tok_la_proj_w': _L0_tok_in['la_proj_w'], 'L0_tok_la_proj_b': _L0_tok_in['la_proj_b'], 'L0_tok_ga_ln_q_g': _L0_tok_in['ga_ln_q_g'], 'L0_tok_ga_ln_q_b': _L0_tok_in['ga_ln_q_b'], 'L0_tok_ga_wq': _L0_tok_in['ga_wq'], 'L0_tok_ga_ln_kv_g': _L0_tok_in['ga_ln_kv_g'], 'L0_tok_ga_ln_kv_b': _L0_tok_in['ga_ln_kv_b'], 'L0_tok_ga_wkv': _L0_tok_in['ga_wkv'], 'L0_tok_ga_proj_w': _L0_tok_in['ga_proj_w'], 'L0_tok_ga_proj_b': _L0_tok_in['ga_proj_b'], 'L0_tok_mod_w': _L0_tok_in['mod_w'], 'L0_tok_mod_b': _L0_tok_in['mod_b'], 'L0_attn_ln_g': _L0_attn_in['ln_g'], 'L0_attn_ln_b': _L0_attn_in['ln_b'], 'L0_attn_f_in_w': _L0_attn_in['f_in_w'], 'L0_attn_f_conv_w': _L0_attn_in['f_conv_w'], 'L0_attn_f_conv_b': _L0_attn_in['f_conv_b'], 'L0_attn_f_xproj_w': _L0_attn_in['f_xproj_w'], 'L0_attn_f_dt_w': _L0_attn_in['f_dt_w'], 'L0_attn_f_dt_b': _L0_attn_in['f_dt_b'], 'L0_attn_f_A_log': _L0_attn_in['f_A_log'], 'L0_attn_f_D_skip': _L0_attn_in['f_D_skip'], 'L0_attn_f_out_w': _L0_attn_in['f_out_w'], 'L0_attn_b_in_w': _L0_attn_in['b_in_w'], 'L0_attn_b_conv_w': _L0_attn_in['b_conv_w'], 'L0_attn_b_conv_b': _L0_attn_in['b_conv_b'], 'L0_attn_b_xproj_w': _L0_attn_in['b_xproj_w'], 'L0_attn_b_dt_w': _L0_attn_in['b_dt_w'], 'L0_attn_b_dt_b': _L0_attn_in['b_dt_b'], 'L0_attn_b_A_log': _L0_attn_in['b_A_log'], 'L0_attn_b_D_skip': _L0_attn_in['b_D_skip'], 'L0_attn_b_out_w': _L0_attn_in['b_out_w'], 'L0_ffn_gate_w': _L0_ffn_in['gate_w'], 'L0_ffn_expert_w': _L0_ffn_in['expert_w']}

def reference(x, L0_tok_pixel_masks, L0_tok_conv_w, L0_tok_class_emb, L0_tok_la_ln_q_g, L0_tok_la_ln_q_b, L0_tok_la_wq, L0_tok_la_ln_kv_g, L0_tok_la_ln_kv_b, L0_tok_la_wkv, L0_tok_la_proj_w, L0_tok_la_proj_b, L0_tok_ga_ln_q_g, L0_tok_ga_ln_q_b, L0_tok_ga_wq, L0_tok_ga_ln_kv_g, L0_tok_ga_ln_kv_b, L0_tok_ga_wkv, L0_tok_ga_proj_w, L0_tok_ga_proj_b, L0_tok_mod_w, L0_tok_mod_b, L0_attn_ln_g, L0_attn_ln_b, L0_attn_f_in_w, L0_attn_f_conv_w, L0_attn_f_conv_b, L0_attn_f_xproj_w, L0_attn_f_dt_w, L0_attn_f_dt_b, L0_attn_f_A_log, L0_attn_f_D_skip, L0_attn_f_out_w, L0_attn_b_in_w, L0_attn_b_conv_w, L0_attn_b_conv_b, L0_attn_b_xproj_w, L0_attn_b_dt_w, L0_attn_b_dt_b, L0_attn_b_A_log, L0_attn_b_D_skip, L0_attn_b_out_w, L0_ffn_gate_w, L0_ffn_expert_w):
    import jax
    import jax.numpy as jnp

    def _L0_tok_ref(pixel_values, pixel_masks, conv_w, class_emb, la_ln_q_g, la_ln_q_b, la_wq, la_ln_kv_g, la_ln_kv_b, la_wkv, la_proj_w, la_proj_b, ga_ln_q_g, ga_ln_q_b, ga_wq, ga_ln_kv_g, ga_ln_kv_b, ga_wkv, ga_proj_w, ga_proj_b, mod_w, mod_b):
        import jax, jax.numpy as jnp
        import numpy as np
        C = 256
        H8 = 8
        DH = C // H8
        PS = 14
        CS = 3
        IMG = 168
        B = 4

        def _ln(x, g, b):
            mu = jnp.mean(x, axis=-1, keepdims=True)
            xc = x - mu
            var = jnp.mean(xc * xc, axis=-1, keepdims=True)
            return xc * jax.lax.rsqrt(var + 1e-05) * g + b

        def _forward(pixel_values, conv_w, class_emb, la_ln_q_g, la_ln_q_b, la_wq, la_ln_kv_g, la_ln_kv_b, la_wkv, la_proj_w, la_proj_b, ga_ln_q_g, ga_ln_q_b, ga_wq, ga_ln_kv_g, ga_ln_kv_b, ga_wkv, ga_proj_w, ga_proj_b, mod_w, mod_b):
            b = pixel_values.shape[0]
            pe = jax.lax.conv_general_dilated(pixel_values, conv_w, (PS, PS), 'VALID', dimension_numbers=('NCHW', 'OIHW', 'NCHW'))
            HP = pe.shape[2]
            h = HP // CS
            hw, N = (h * h, CS * CS)
            scale = C ** (-0.5)
            grid = pe.reshape(b, C, h, CS, h, CS)
            red = grid.mean(axis=(3, 5)).reshape(b, C, hw).transpose(0, 2, 1)
            win = grid.transpose(0, 2, 4, 3, 5, 1).reshape(b, hw, N, C)
            q = _ln(red, la_ln_q_g, la_ln_q_b) @ la_wq
            q = q.reshape(b, hw, H8, DH).transpose(0, 2, 1, 3)
            kv = _ln(win, la_ln_kv_g, la_ln_kv_b) @ la_wkv
            kv = kv.reshape(b, hw, N, 2, H8, DH).transpose(3, 0, 4, 1, 2, 5)
            k_, v_ = (kv[0], kv[1])
            attn = jax.nn.softmax(jnp.einsum('bhnd,bhnkd->bhnk', q * scale, k_), axis=-1)
            agg = jnp.einsum('bhnk,bhnkd->bhnd', attn, v_)
            agg = agg.transpose(0, 2, 1, 3).reshape(b, hw, C)
            local_out = red + agg @ la_proj_w + la_proj_b
            cls = jnp.broadcast_to(class_emb, (b, 1, C))
            gq = (_ln(cls, ga_ln_q_g, ga_ln_q_b) @ ga_wq).reshape(b, H8, DH)
            gkv = _ln(local_out, ga_ln_kv_g, ga_ln_kv_b) @ ga_wkv
            gkv = gkv.reshape(b, hw, 2, H8, DH).transpose(2, 0, 3, 1, 4)
            gk, gv = (gkv[0], gkv[1])
            gattn = jax.nn.softmax(jnp.einsum('bhd,bhnd->bhn', gq * scale, gk), axis=-1)
            gagg = jnp.einsum('bhn,bhnd->bhd', gattn, gv).reshape(b, 1, C)
            cls_out = cls + gagg @ ga_proj_w + ga_proj_b
            patch_out = local_out @ mod_w + mod_b
            return jnp.concatenate([patch_out, cls_out], axis=1)
        del pixel_masks
        return _forward(pixel_values, conv_w, class_emb, la_ln_q_g, la_ln_q_b, la_wq, la_ln_kv_g, la_ln_kv_b, la_wkv, la_proj_w, la_proj_b, ga_ln_q_g, ga_ln_q_b, ga_wq, ga_ln_kv_g, ga_ln_kv_b, ga_wkv, ga_proj_w, ga_proj_b, mod_w, mod_b)

    def _L0_attn_ref(x, ln_g, ln_b, f_in_w, f_conv_w, f_conv_b, f_xproj_w, f_dt_w, f_dt_b, f_A_log, f_D_skip, f_out_w, b_in_w, b_conv_w, b_conv_b, b_xproj_w, b_dt_w, b_dt_b, b_A_log, b_D_skip, b_out_w):
        import jax, jax.numpy as jnp
        import numpy as np
        B_SZ, SEQ = (2, 256)
        D_MODEL, D_STATE, D_CONV, EXPAND = (256, 16, 4, 2)
        D_INNER = EXPAND * D_MODEL
        DT_RANK = D_MODEL // 16

        def _layernorm(x, g, b):
            m = x.mean(-1, keepdims=True)
            v = ((x - m) ** 2).mean(-1, keepdims=True)
            return (x - m) * jax.lax.rsqrt(v + 1e-05) * g + b

        def _mamba(x, in_w, conv_w, conv_b, xproj_w, dt_w, dt_b, A_log, D_skip, out_w):
            B, L, _ = x.shape
            xz = x @ in_w.T
            xi, z = jnp.split(xz, 2, axis=-1)
            dc = conv_w.shape[1]
            xp = jnp.pad(xi, ((0, 0), (dc - 1, 0), (0, 0)))
            xc = conv_b + sum((xp[:, k:k + L, :] * conv_w[:, k] for k in range(dc)))
            xc = jax.nn.silu(xc)
            dbl = xc @ xproj_w.T
            n = A_log.shape[1]
            r = xproj_w.shape[0] - 2 * n
            dt, Bm, Cm = (dbl[..., :r], dbl[..., r:r + n], dbl[..., r + n:])
            delta = jax.nn.softplus(dt @ dt_w.T + dt_b)
            A = -jnp.exp(A_log)
            dA = jnp.exp(delta[..., None] * A)
            dBu = delta[..., None] * Bm[:, :, None, :] * xc[..., None]

            def step(h, inp):
                da, dbu, c = inp
                h = da * h + dbu
                return (h, jnp.einsum('bdn,bn->bd', h, c))
            h0 = jnp.zeros((B, delta.shape[-1], n), x.dtype)
            _, ys = jax.lax.scan(step, h0, (dA.swapaxes(0, 1), dBu.swapaxes(0, 1), Cm.swapaxes(0, 1)))
            y = ys.swapaxes(0, 1) + xc * D_skip
            return y * jax.nn.silu(z) @ out_w.T
        xn = _layernorm(x, ln_g, ln_b)
        y_fwd = _mamba(xn, f_in_w, f_conv_w, f_conv_b, f_xproj_w, f_dt_w, f_dt_b, f_A_log, f_D_skip, f_out_w)
        y_bwd = jnp.flip(_mamba(jnp.flip(xn, 1), b_in_w, b_conv_w, b_conv_b, b_xproj_w, b_dt_w, b_dt_b, b_A_log, b_D_skip, b_out_w), 1)
        return 0.5 * (y_fwd + y_bwd)

    def _L0_ffn_ref(x, gate_w, expert_w):
        import jax, jax.numpy as jnp
        import numpy as np
        B, S, H, E = (2, 2048, 256, 8)
        SCALE = 0.5
        scores = jnp.einsum('bsh,eh->bse', x, gate_w)
        chosen = jnp.argmax(scores, axis=-1)
        onehot = jax.nn.one_hot(chosen, gate_w.shape[0], dtype=x.dtype)
        expert_out = jnp.einsum('bsh,efh->bsef', x, expert_w)
        return x + jnp.einsum('bsef,bse->bsf', expert_out, onehot)
    h = _L0_tok_ref(x, L0_tok_pixel_masks, L0_tok_conv_w, L0_tok_class_emb, L0_tok_la_ln_q_g, L0_tok_la_ln_q_b, L0_tok_la_wq, L0_tok_la_ln_kv_g, L0_tok_la_ln_kv_b, L0_tok_la_wkv, L0_tok_la_proj_w, L0_tok_la_proj_b, L0_tok_ga_ln_q_g, L0_tok_ga_ln_q_b, L0_tok_ga_wq, L0_tok_ga_ln_kv_g, L0_tok_ga_ln_kv_b, L0_tok_ga_wkv, L0_tok_ga_proj_w, L0_tok_ga_proj_b, L0_tok_mod_w, L0_tok_mod_b)
    h = h + _L0_attn_ref(_layernorm(h, axis=-1), L0_attn_ln_g, L0_attn_ln_b, L0_attn_f_in_w, L0_attn_f_conv_w, L0_attn_f_conv_b, L0_attn_f_xproj_w, L0_attn_f_dt_w, L0_attn_f_dt_b, L0_attn_f_A_log, L0_attn_f_D_skip, L0_attn_f_out_w, L0_attn_b_in_w, L0_attn_b_conv_w, L0_attn_b_conv_b, L0_attn_b_xproj_w, L0_attn_b_dt_w, L0_attn_b_dt_b, L0_attn_b_A_log, L0_attn_b_D_skip, L0_attn_b_out_w)
    h = h + _L0_ffn_ref(_layernorm(h, axis=-1), L0_ffn_gate_w, L0_ffn_expert_w)
    return h

_drawn_inputs = setup_inputs


def setup_inputs(seed=0):
    import zlib

    import numpy as np

    out = dict(_drawn_inputs(seed))
    spreads = {'L0_tok_pixel_masks': (1.0, 0.2),
     'L0_tok_la_ln_q_g': (1.0, 0.6),
     'L0_tok_la_ln_q_b': (0.0, 0.8),
     'L0_tok_la_ln_kv_g': (1.0, 0.6),
     'L0_tok_la_ln_kv_b': (0.0, 0.1),
     'L0_tok_la_proj_b': (0.0, 0.1),
     'L0_tok_ga_ln_q_g': (1.0, 0.6),
     'L0_tok_ga_ln_q_b': (0.0, 0.8),
     'L0_tok_ga_ln_kv_g': (1.0, 0.2),
     'L0_tok_ga_ln_kv_b': (0.0, 0.1),
     'L0_tok_ga_proj_b': (0.0, 0.1),
     'L0_tok_mod_b': (0.0, 0.1),
     'L0_attn_ln_g': (1.0, 0.6),
     'L0_attn_ln_b': (0.0, 0.8),
     'L0_attn_f_conv_b': (0.0, 0.432),
     'L0_attn_f_D_skip': (1.0, 0.6),
     'L0_attn_b_conv_b': (0.0, 0.45),
     'L0_attn_b_D_skip': (1.0, 0.6)}
    factors = {'L0_tok_la_wq': 8.0,
     'L0_tok_ga_wq': 8.0,
     'L0_attn_f_in_w': 2.878,
     'L0_attn_f_conv_w': 5.317,
     'L0_attn_f_xproj_w': 8.0,
     'L0_attn_f_dt_w': 8.0,
     'L0_attn_f_dt_b': 8.0,
     'L0_attn_f_A_log': 8.0,
     'L0_attn_b_in_w': 2.815,
     'L0_attn_b_conv_w': 5.119,
     'L0_attn_b_xproj_w': 8.0,
     'L0_attn_b_dt_w': 8.0,
     'L0_attn_b_dt_b': 8.0,
     'L0_attn_b_A_log': 8.0,
     'L0_ffn_gate_w': 64.0,
     'L0_ffn_expert_w': 26.682}
    for name, (base, spread) in spreads.items():
        noise = np.random.default_rng([zlib.crc32(name.encode()), seed]).standard_normal(out[name].shape)
        drawn = base * np.exp(spread * noise) if base else spread * noise
        out[name] = jnp.asarray(drawn.astype(out[name].dtype))
    for name, factor in factors.items():
        out[name] = (out[name] * factor).astype(out[name].dtype)
    return out
```

```python
from contextlib import ExitStack

import concourse.bass as bass
from concourse import mybir

ALU = mybir.AluOpType
ACT = mybir.ActivationFunctionType
AX = mybir.AxisListType
F32 = mybir.dt.float32
BF16 = mybir.dt.bfloat16

B, C, H, DH = 128, 256, 8, 32
P = 128
CH = C // P
W4, K9 = 4, 9
KP = 3 * 14 * 14
KC = -(-KP // P)
KL = KP - (KC - 1) * P
WT = K9 * B
EC = 3
EN = WT // EC
L, DI, NS, R = 5, 512, 16, 16
DC = DI // P
NX = R + 2 * NS
GB = P // NS
NG = B // GB
E8 = 8
EPS = 1e-5
QSCALE = C ** -0.5

VC = {}
_n = 0
for _name, _w in [("q_g", 2), ("q_b", 2), ("gq_g", 2), ("gq_b", 2), ("kv_g", 2), ("kv_b", 2), ("gkv_g", 2),
                  ("gkv_b", 2), ("ln_g", 2), ("ln_b", 2), ("cls", 2), ("cb0", 4), ("cb1", 4), ("cw0", 16),
                  ("cw1", 16)]:
    VC[_name] = _n
    _n += _w
NVC = _n
VR = {"proj_b": 0, "mod_b": 256, "gproj_b": 512, "cls": 768, "D0": 1024, "D1": 1536}
NVR = 2048
KS = 12 * GB
SEG = {"q": (0, 256), "gq": (256, 256), "kv": (512, 512), "gkv": (1024, 512)}


class Chain:

    def __init__(self, eng, sem, base=0):
        self.eng, self.sem, self.base, self.n = eng, sem, base, 0

    def link(self, ins):
        ins.then_inc(self.sem, 1)
        self.n += 1
        self.eng.wait_ge(self.sem, self.base + self.n)


def tower(nc, a, out):
    top = ExitStack()
    with top:
        def sb(name, shape, dt=F32, ctx=top):
            return ctx.enter_context(nc.sbuf_tensor(name, shape, dt))

        def sem(name):
            return top.enter_context(nc.semaphore(name))

        ps = top.enter_context(nc.psum_tensor("ps", [P, 8 * 512], F32))

        def bank(n, lo=0, hi=512, p=P):
            return ps[0:p, n * 512 + lo:n * 512 + hi]

        ident = sb("ident", [P, P])
        mhalf = sb("mhalf", [P, 16])
        cols = sb("cols", [P, NVC])
        rows = sb("rows", [P, NVR])
        inw = sb("inw", [P, 2, CH, 2 * DI])
        xpw = sb("xpw", [P, 2, DC, NX])
        dtw = sb("dtw", [33, 2, DI])
        outw = sb("outw", [P, 2, DC, C])
        expA = sb("expA", [P, 2, DI])
        gatew = sb("gatew", [P, CH, E8])
        hbuf = sb("hbuf", [P, L, C])
        maskb = sb("maskb", [P, GB, NS])
        sel = sb("sel", [KS, 2, P])
        selb = sb("selb", [KS, 2, P], BF16)

        def col(name, j=0, n=1):
            return cols[:, VC[name] + j:VC[name] + j + n]

        def row(name, n):
            return rows[:, VR[name]:VR[name] + n]

        dparts = nc.dram_tensor("dparts", (6, B, L * DI), BF16, kind="Internal").ap()
        uparts = nc.dram_tensor("uparts", (6, B, L * DI), BF16, kind="Internal").ap()
        bparts = nc.dram_tensor("bparts", (12, B, 2 * L * P), BF16, kind="Internal").ap()
        NY = 3 * 32 + GB
        yscr = nc.dram_tensor("yscr", (NG, 2, NY, DI), F32, kind="Internal").ap()

        tok = ExitStack()
        win = ExitStack()
        redT = sb("redT", [P, W4, CH, P], ctx=tok)
        agg = sb("agg", [P, W4, C], ctx=tok)
        wall = sb("wall", [P, CH, 1536], ctx=tok)
        brow = sb("brow", [P, 1536], ctx=tok)
        projw = sb("projw", [P, 3, CH, C], ctx=tok)
        convw = sb("convw", [P, KC, C], ctx=win)
        onesc = sb("onesc", [P, P], ctx=win)
        xbuf = sb("xbuf", [P, 2, KC, WT], ctx=win)
        peT = sb("peT", [P, 2, CH, WT], ctx=win)
        kvs = sb("kvs", [P, 2, K9, 2 * C], ctx=win)
        prod = sb("prod", [P, K9, C], ctx=win)
        redw = sb("redw", [P, 2, CH, P], ctx=win)
        st = sb("st", [P, K9 + 1, 6], ctx=win)
        mv = sb("mv", [P, K9 + 1, 2], ctx=win)
        veps = sb("veps", [P, K9 + 1], ctx=win)
        rstd = sb("rstd", [P, K9 + 1], ctx=win)
        qn = sb("qn", [P, C], ctx=win)
        qb = sb("qb", [P, H], ctx=win)
        sc = sb("sc", [P, K9, H], ctx=win)
        mx = sb("mx", [P, H], ctx=win)
        ex = sb("ex", [P, K9, H], ctx=win)
        sm = sb("sm", [P, H], ctx=win)

        s_vec, s_wall, s_conv, s_late = sem("s_vec"), sem("s_wall"), sem("s_conv"), sem("s_late")
        expA_ready = sem("expA_ready")
        s_const, s_bias, s_brow = sem("s_const"), sem("s_bias"), sem("s_brow")
        s_wg, s_wmean, s_wready = sem("s_wg"), sem("s_wmean"), sem("s_wready")
        x_landed = [[sem(f"x_landed{q}{c}") for c in range(EC)] for q in range(2)]
        emb_ready, emb_free, s_dtz = sem("emb_ready"), sem("emb_free"), sem("s_dtz")
        kv_ready, kv_free, kvs_free = sem("kv_ready"), sem("kv_free"), sem("kvs_free")
        tr_ready, tr_free = sem("tr_ready"), sem("tr_free")
        red_ready, red_kept, q_ready, q_free = sem("red_ready"), sem("red_kept"), sem("q_ready"), sem("q_free")
        veps_ready, rstd_ready, sc_ready, ex_ready = sem("veps_ready"), sem("rstd_ready"), sem("sc_ready"), sem("ex_ready")
        d_chain = sem("d_chain")

        T_EMB, T_KV, T_TR, T_Q = 0, 2, 4, 6

        with nc.Block() as block:
            @block.sync
            def _(sp):
                sp.dma_start(cols[:, :], a["vec_cols"]).then_inc(s_vec, 16)
                sp.dma_start(sel[:, :, :], a["sel"].rearrange("k (d m) -> k d m", d=2)).then_inc(s_vec, 16)
                sp.dma_start(wall[:, :, :], a["wall"].rearrange("(h p) n -> p h n", p=P)).then_inc(s_wall, 16)
                sp.dma_start(convw[:, 0:KC - 1, :], a["conv_wT"][0:(KC - 1) * P].rearrange("(k p) n -> p k n", p=P)).then_inc(s_conv, 16)
                sp.dma_start(convw[0:KL, KC - 1, :], a["conv_wT"][(KC - 1) * P:KP]).then_inc(s_conv, 16)

                def load_window(w, q):
                    for c in range(EC):
                        src = a["xT"][:, bass.ds(w * WT + c * EN, EN)]
                        sp.dma_start(xbuf[:, q, 0:KC - 1, c * EN:(c + 1) * EN],
                                     src[0:(KC - 1) * P].rearrange("(k p) n -> p k n", p=P)).then_inc(x_landed[q][c], 16)
                        sp.dma_start(xbuf[0:KL, q, KC - 1, c * EN:(c + 1) * EN],
                                     src[(KC - 1) * P:KP]).then_inc(x_landed[q][c], 16)

                load_window(0, 0)
                load_window(1, 1)
                sp.dma_start(rows[:, :], a["vec_rows"].to_broadcast([P, NVR])).then_inc(s_late, 16)
                for n, name in enumerate(["la_proj_w", "ga_proj_w", "mod_w"]):
                    sp.dma_start(projw[:, n], a[name].rearrange("(h p) n -> p h n", p=P)).then_inc(s_late, 16)
                for w in (2, 3):
                    sp.wait_ge(emb_ready, 6 * (w - 1))
                    load_window(w, w % 2)
                for d in range(2):
                    sp.dma_start(inw[:, d], a["in_wT"][d].rearrange("(h p) n -> p h n", p=P)).then_inc(s_late, 16)
                    sp.dma_start(xpw[:, d], a["xproj_wT"][d].rearrange("(c p) n -> p c n", p=P)).then_inc(s_late, 16)
                    sp.dma_start(outw[:, d], a["out_wT"][d].rearrange("(c p) n -> p c n", p=P)).then_inc(s_late, 16)
                    for g in range(GB):
                        sp.dma_start(expA[g * NS:(g + 1) * NS, d], a["A_logT"][d]).then_inc(s_late, 16)
                sp.dma_start(gatew[:, :, :], a["gate_wT"].rearrange("(h p) n -> p h n", p=P)).then_inc(s_late, 16)
                sp.wait_ge(s_dtz, 1)
                for d in range(2):
                    sp.dma_start(dtw[0:R, d], a["dt_wT"][d]).then_inc(s_late, 16)
                    sp.dma_start(dtw[32:33, d], a["dt_b"][d]).then_inc(s_late, 16)
                sp.wait_ge(s_late, 16 * (4 + 2 * (3 + GB) + 1 + 4))

            @block.gpsimd
            def _(pool):
                pool.memset(dtw[:, :, :], 0.0).then_inc(s_dtz, 1)
                pool.memset(ident[:, :], 0.0).then_inc(s_const, 1)
                pool.memset(maskb[:, :, :], 0.0).then_inc(s_const, 1)
                pool.memset(mhalf[:, :], -0.5).then_inc(s_const, 1)
                pool.wait_ge(s_const, 3)
                pool.affine_select(out=ident[:, :], in_=ident[:, :], compare_op=ALU.not_equal, fill=1.0, base=0,
                                   pattern=[[-1, P]], channel_multiplier=1).then_inc(s_const, 1)
                pool.wait_ge(s_const, 4)
                for j in range(NG):
                    pool.tensor_tensor(maskb[:, :, :], maskb[:, :, :],
                                       ident[:, j * GB:(j + 1) * GB].unsqueeze(2).to_broadcast([P, GB, NS]),
                                       ALU.add).then_inc(s_const, 1)
                    pool.wait_ge(s_const, 5 + j)
                pool.wait_ge(s_vec, 32)
                pool.tensor_copy(selb[:, :, :], sel[:, :, :]).then_inc(s_const, 1)
                for w in range(W4):
                    pool.wait_ge(veps_ready, w + 1)
                    pool.tensor_tensor(rstd[:, :], veps[:, :], mhalf[:, 0:K9 + 1], ALU.pow).then_inc(rstd_ready, 1)

            @block.tensor
            def _(pe):
                pe.wait_ge(s_vec, 32)
                pe.wait_ge(s_wall, 16)
                for s, (o, n) in SEG.items():
                    for h in range(CH):
                        mm = pe.matmul(bank(o // 512, o % 512, o % 512 + n),
                                       col(s + "_b", h).to_broadcast([P, P]), wall[:, h, o:o + n],
                                       start=(h == 0), stop=(h == CH - 1))
                mm.then_inc(s_bias, 1)
                pe.wait_ge(s_wg, 8)
                for s in range(3):
                    for h in range(CH):
                        mm = pe.matmul(bank(3 + s), onesc[:, :], wall[:, h, s * 512:(s + 1) * 512],
                                       start=(h == 0), stop=(h == CH - 1))
                mm.then_inc(s_wmean, 1)
                pe.wait_ge(s_conv, 32)
                pe.wait_ge(s_brow, 1)
                pe.wait_ge(s_wready, 6)
                pe.wait_ge(s_const, 4)

                def window(i, q):
                    w = 2 * i + q
                    for c in range(EC):
                        pe.wait_ge(x_landed[q][c], 32 * i + 32)
                        for h in range(CH):
                            j = c * CH + h
                            pe.wait_ge(emb_free, 6 * w + j + 1)
                            for k in range(KC):
                                n = P if k < KC - 1 else KL
                                mm = pe.matmul(bank(T_EMB + j % 2, 0, EN), convw[0:n, k, h * P:(h + 1) * P],
                                               xbuf[0:n, q, k, c * EN:(c + 1) * EN],
                                               start=(k == 0), stop=(k == KC - 1))
                            mm.then_inc(emb_ready, 1)
                    for t in range(K9):
                        if t % EC == 0:
                            pe.wait_ge(emb_free, 2 + 6 * w + 2 * (t // EC) + 2)
                        pe.wait_ge(tr_free, 10 * w + t + 1)
                        for h in range(CH):
                            mm = pe.transpose(bank(T_TR + t % 2, h * P, (h + 1) * P),
                                              peT[:, q, h, t * B:(t + 1) * B], ident[:, :])
                        mm.then_inc(tr_ready, 1)
                        pe.wait_ge(kv_free, 9 * w + t + 1)
                        for h in range(CH):
                            mm = pe.matmul(bank(T_KV + (q + t) % 2), peT[:, q, h, t * B:(t + 1) * B],
                                           wall[:, h, 512:1024], start=(h == 0), stop=(h == CH - 1))
                        mm.then_inc(kv_ready, 1)
                    pe.wait_ge(red_ready, w + 1)
                    pe.wait_ge(tr_free, 10 * w + K9 + 1)
                    for h in range(CH):
                        mm = pe.transpose(bank(T_TR + 1, h * P, (h + 1) * P), redw[:, q, h, :], ident[:, :])
                    mm.then_inc(tr_ready, 1)
                    pe.wait_ge(q_free, w + 1)
                    for h in range(CH):
                        mm = pe.matmul(bank(T_Q, 0, C), redw[:, q, h, :], wall[:, h, 0:C],
                                       start=(h == 0), stop=(h == CH - 1))
                    mm.then_inc(q_ready, 1)

                with pe.Fori(0, W4 // 2) as i:
                    for q in range(2):
                        window(i, q)

            @block.scalar
            def _(act):
                act.wait_ge(s_bias, 1)
                act.activation(brow[:, :], ps[:, 0:1536], ACT.Copy).then_inc(s_brow, 1)
                act.sem_inc(emb_free, 2)
                act.sem_inc(kv_free, 2)
                act.sem_inc(red_kept, 2)

                def window(i, q):
                    w = 2 * i + q
                    for c in range(EC):
                        for h in range(CH):
                            j = c * CH + h
                            act.wait_ge(emb_ready, 6 * w + j + 1)
                            act.activation(peT[:, q, h, c * EN:(c + 1) * EN], bank(T_EMB + j % 2, 0, EN),
                                           ACT.Copy).then_inc(emb_free, 1)
                    act.wait_ge(kvs_free, w + 1)
                    for t in range(K9):
                        act.wait_ge(kv_ready, 9 * w + t + 1)
                        act.activation(kvs[:, q, t, :], bank(T_KV + (q + t) % 2), ACT.Copy).then_inc(kv_free, 1)
                        if t == 5:
                            act.wait_ge(red_ready, w + 1)
                            act.activation(redT[:, bass.ds(w, 1), :, :].rearrange("p o h b -> p (o h) b"),
                                           redw[:, q, :, :], ACT.Copy).then_inc(red_kept, 1)
                    act.wait_ge(sc_ready, w + 1)
                    act.activation(ex[:, :, :], sc[:, :, :], ACT.Exp, scale=QSCALE).then_inc(ex_ready, 1)

                with act.Fori(0, W4 // 2) as i:
                    for q in range(2):
                        window(i, q)

            @block.vector
            def _(dve):
                dve.memset(onesc[:, :], 1.0 / C)
                dve.wait_ge(s_bias, 1)
                for s, (o, n) in SEG.items():
                    for h in range(CH):
                        dve.tensor_scalar(wall[:, h, o:o + n], wall[:, h, o:o + n], col(s + "_g", h), None,
                                          ALU.mult).then_inc(s_wg, 1)
                dve.wait_ge(s_wg, 8)
                dve.wait_ge(s_wmean, 1)
                for s in range(3):
                    for h in range(CH):
                        dve.tensor_tensor(wall[:, h, s * 512:(s + 1) * 512], wall[:, h, s * 512:(s + 1) * 512],
                                          bank(3 + s), ALU.subtract).then_inc(s_wready, 1)
                dve.sem_inc(tr_free, 2)
                dve.sem_inc(kvs_free, 2)
                dve.sem_inc(q_free, 1)
                dve.wait_ge(s_wready, 6)
                dve.wait_ge(s_brow, 1)
                NCH = 16

                def window(i, q):
                    w = 2 * i + q
                    ch = Chain(dve, d_chain, NCH * w)
                    dve.wait_ge(emb_free, 2 + 6 * w + 6)
                    dve.wait_ge(red_kept, w + 1)
                    ch.link(dve.tensor_reduce(redw[:, q, :, :],
                                              peT[:, q, :, :].rearrange("p h (k b) -> p h b k", k=K9), AX.X, ALU.add))
                    dve.tensor_scalar(redw[:, q, :, :], redw[:, q, :, :], 1.0 / K9, None,
                                      ALU.mult).then_inc(red_ready, 1)
                    for t in range(K9 + 1):
                        dve.wait_ge(tr_ready, 10 * w + t + 1)
                        dve.bn_stats(st[:, t, :], bank(T_TR + t % 2, 0, C)).then_inc(tr_free, 1)
                    dve.wait_ge(tr_free, 2 + 10 * (w + 1))
                    dve.memset(sm[:, :], 0.0)
                    for t in range(K9):
                        dve.bn_aggr(mv[:, t, :], st[:, t, :])
                    ch.link(dve.bn_aggr(mv[:, K9, :], st[:, K9, :]))
                    dve.tensor_scalar(veps[:, :], mv[:, :, 1], EPS, None, ALU.add).then_inc(veps_ready, 1)
                    dve.wait_ge(rstd_ready, w + 1)
                    dve.wait_ge(q_ready, w + 1)
                    dve.scalar_tensor_tensor(out=qn[:, :], in0=bank(T_Q, 0, C), scalar=rstd[:, K9:K9 + 1],
                                             in1=brow[:, 0:C], op0=ALU.mult, op1=ALU.add).then_inc(q_free, 1)
                    dve.wait_ge(q_free, w + 2)
                    dve.wait_ge(kv_free, 2 + 9 * w + 9)
                    ch.link(dve.tensor_tensor(prod[:, 0, :], qn[:, :], brow[:, 512:512 + C], ALU.mult))
                    ch.link(dve.tensor_reduce(qb[:, :], prod[:, 0, :].rearrange("p (h d) -> p h d", h=H), AX.X, ALU.add))
                    ch.link(dve.tensor_tensor(prod[:, :, :], kvs[:, q, :, 0:C],
                                              qn[:, :].unsqueeze(1).to_broadcast([P, K9, C]), ALU.mult))
                    ch.link(dve.tensor_reduce(sc[:, :, :].rearrange("p k h -> p (k h)"),
                                              prod[:, :, :].rearrange("p k (h d) -> p (k h) d", h=H), AX.X, ALU.add))
                    rk = rstd[:, 0:K9].unsqueeze(2).to_broadcast([P, K9, H])
                    ch.link(dve.tensor_tensor(sc[:, :, :], sc[:, :, :], rk, ALU.mult))
                    ch.link(dve.tensor_tensor(sc[:, :, :], sc[:, :, :],
                                              qb[:, :].unsqueeze(1).to_broadcast([P, K9, H]), ALU.add))
                    ch.link(dve.tensor_reduce(mx[:, :], sc[:, :, :].rearrange("p k h -> p h k"), AX.X, ALU.max))
                    dve.tensor_tensor(sc[:, :, :], sc[:, :, :], mx[:, :].unsqueeze(1).to_broadcast([P, K9, H]),
                                      ALU.subtract).then_inc(sc_ready, 1)
                    dve.wait_ge(ex_ready, w + 1)
                    ch.link(dve.tensor_reduce(sm[:, :], ex[:, :, :].rearrange("p k h -> p h k"), AX.X, ALU.add))
                    ch.link(dve.reciprocal(sm[:, :], sm[:, :]))
                    ch.link(dve.tensor_tensor(ex[:, :, :], ex[:, :, :],
                                              sm[:, :].unsqueeze(1).to_broadcast([P, K9, H]), ALU.mult))
                    ch.link(dve.tensor_tensor(ex[:, :, :], ex[:, :, :], rk, ALU.mult))
                    ch.link(dve.tensor_tensor(prod[:, :, :].rearrange("p k (h d) -> p (k h) d", h=H),
                                              kvs[:, q, :, C:2 * C].rearrange("p k (h d) -> p k h d", h=H),
                                              ex[:, :, :].unsqueeze(3).to_broadcast([P, K9, H, DH]), ALU.mult))
                    dve.sem_inc(kvs_free, 1)
                    ch.link(dve.tensor_reduce(qn[:, :], prod[:, :, :].rearrange("p k c -> p c k"), AX.X, ALU.add))
                    ch.link(dve.tensor_tensor(agg[:, bass.ds(w, 1), :].rearrange("p o c -> p (o c)"), qn[:, :],
                                              brow[:, 512 + C:1024], ALU.add))
                    assert ch.n == NCH

                with dve.Fori(0, W4 // 2) as i:
                    for q in range(2):
                        window(i, q)
        win.close()

        glo = ExitStack()
        lo = sb("lo", [P, W4, C], ctx=glo)
        gkvs = sb("gkvs", [P, W4, 2 * C], ctx=glo)
        aggT = sb("aggT", [P, 2, CH, P], ctx=glo)
        loT = sb("loT", [P, 2, CH, P], ctx=glo)
        gaT = sb("gaT", [P, CH, P], ctx=glo)
        gst = sb("gst", [P, W4 + 1, 6], ctx=glo)
        gmv = sb("gmv", [P, W4 + 1, 2], ctx=glo)
        gve = sb("gve", [P, W4 + 1], ctx=glo)
        grs = sb("grs", [P, W4 + 1], ctx=glo)
        gqn = sb("gqn", [P, C], ctx=glo)
        gqraw = sb("gqraw", [P, C], ctx=glo)
        gpr = sb("gpr", [P, W4, C], ctx=glo)
        gqb = sb("gqb", [P, H], ctx=glo)
        gsc = sb("gsc", [P, W4, H], ctx=glo)
        gmx = sb("gmx", [P, H], ctx=glo)
        gex = sb("gex", [P, W4, H], ctx=glo)
        gag = sb("gag", [P, C], ctx=glo)
        aT_ready, aT_copied = sem("aT_ready"), sem("aT_copied")
        lo_summed, lo_ready, lT_ready, lT_copied = sem("lo_summed"), sem("lo_ready"), sem("lT_ready"), sem("lT_copied")
        gkv_ready, gkv_copied, mod_ready, mod_copied = sem("gkv_ready"), sem("gkv_copied"), sem("mod_ready"), sem("mod_copied")
        gq_ready, gq_read, gve_ready, grs_ready = sem("gq_ready"), sem("gq_read"), sem("gve_ready"), sem("grs_ready")
        gsc_ready, gex_ready, gag_ready, gaT_ready = sem("gsc_ready"), sem("gex_ready"), sem("gag_ready"), sem("gaT_ready")
        gaT_copied, cls_ready, g_chain = sem("gaT_copied"), sem("cls_ready"), sem("g_chain")

        with nc.Block() as block:
            @block.tensor
            def _(pe):
                for h in range(CH):
                    mm = pe.matmul(bank(6, 0, C), col("cls", h).to_broadcast([P, P]), wall[:, h, C:2 * C],
                                   start=(h == 0), stop=(h == CH - 1))
                mm.then_inc(gq_ready, 1)

                def agg_turned(w):
                    if w >= 2:
                        pe.wait_ge(aT_copied, w - 1)
                    for h in range(CH):
                        mm = pe.transpose(bank(w % 2, h * P, (h + 1) * P), agg[:, w, h * P:(h + 1) * P], ident[:, :])
                    mm.then_inc(aT_ready, 1)

                def local_out(w):
                    pe.wait_ge(aT_copied, w + 1)
                    if w >= 2:
                        pe.wait_ge(lo_ready, w - 1)
                    for h in range(CH):
                        pe.matmul(bank(2 + w % 2, 0, C), aggT[:, w % 2, h, :], projw[:, 0, h, :],
                                  start=(h == 0), stop=False, skip_group_check=True)
                    for h in range(CH):
                        mm = pe.matmul(bank(2 + w % 2, h * P, (h + 1) * P), redT[:, w, h, :], ident[:, :],
                                       start=False, stop=(h == CH - 1), skip_group_check=True)
                    mm.then_inc(lo_summed, 1)

                def lo_turned(w):
                    pe.wait_ge(lo_ready, w + 1)
                    if w >= 2:
                        pe.wait_ge(lT_copied, w - 1)
                    for h in range(CH):
                        mm = pe.transpose(bank(4 + w % 2, h * P, (h + 1) * P), lo[:, w, h * P:(h + 1) * P], ident[:, :])
                    mm.then_inc(lT_ready, 1)

                def projections(w):
                    pe.wait_ge(lT_copied, w + 1)
                    if w == 0:
                        pe.wait_ge(gq_read, 1)
                    else:
                        pe.wait_ge(gkv_copied, w)
                    for h in range(CH):
                        mm = pe.matmul(bank(6), loT[:, w % 2, h, :], wall[:, h, 1024:1536],
                                       start=(h == 0), stop=(h == CH - 1))
                    mm.then_inc(gkv_ready, 1)
                    if w >= 1:
                        pe.wait_ge(mod_copied, w)
                    for h in range(CH):
                        mm = pe.matmul(bank(7, 0, C), loT[:, w % 2, h, :], projw[:, 2, h, :],
                                       start=(h == 0), stop=(h == CH - 1))
                    mm.then_inc(mod_ready, 1)

                for n in range(W4 + 3):
                    if n < W4:
                        agg_turned(n)
                    if 1 <= n <= W4:
                        local_out(n - 1)
                    if 2 <= n <= W4 + 1:
                        lo_turned(n - 2)
                    if n >= 3:
                        projections(n - 3)
                pe.wait_ge(gag_ready, 1)
                for h in range(CH):
                    mm = pe.transpose(bank(0, h * P, (h + 1) * P), gag[:, h * P:(h + 1) * P], ident[:, :])
                mm.then_inc(gaT_ready, 1)
                pe.wait_ge(gaT_copied, 1)
                for h in range(CH):
                    mm = pe.matmul(bank(2, 0, C), gaT[:, h, :], projw[:, 1, h, :], start=(h == 0), stop=(h == CH - 1))
                mm.then_inc(cls_ready, 1)

            @block.scalar
            def _(act):
                act.wait_ge(gq_ready, 1)
                act.activation(gqraw[:, :], bank(6, 0, C), ACT.Copy).then_inc(gq_read, 1)

                def turned(w):
                    act.wait_ge(aT_ready, w + 1)
                    if w >= 2:
                        act.wait_ge(lo_summed, w - 1)
                    act.activation(aggT[:, w % 2, :, :], bank(w % 2, 0, C), ACT.Copy).then_inc(aT_copied, 1)

                def lo_copied(w):
                    act.wait_ge(lT_ready, w + 1)
                    if w >= 2:
                        act.wait_ge(mod_ready, w - 1)
                    act.activation(loT[:, w % 2, :, :], bank(4 + w % 2, 0, C), ACT.Copy).then_inc(lT_copied, 1)

                def kv_copied(w):
                    act.wait_ge(gkv_ready, w + 1)
                    act.activation(gkvs[:, w, :], bank(6), ACT.Copy).then_inc(gkv_copied, 1)

                for n in range(W4 + 3):
                    if n < W4:
                        turned(n)
                    if 2 <= n <= W4 + 1:
                        lo_copied(n - 2)
                    if n >= 3:
                        kv_copied(n - 3)
                act.wait_ge(gsc_ready, 1)
                act.activation(gex[:, :, :], gsc[:, :, :], ACT.Exp, scale=QSCALE).then_inc(gex_ready, 1)
                act.wait_ge(gaT_ready, 1)
                act.activation(gaT[:, :, :], bank(0, 0, C), ACT.Copy).then_inc(gaT_copied, 1)

            @block.gpsimd
            def _(pool):
                pool.wait_ge(gve_ready, 1)
                pool.tensor_tensor(grs[:, :], gve[:, :], mhalf[:, 0:W4 + 1], ALU.pow).then_inc(grs_ready, 1)

            @block.vector
            def _(dve):
                ch = Chain(dve, g_chain)
                ch.link(dve.bn_stats(gst[:, W4, :], row("cls", C)))
                for w in range(W4 + 1):
                    if w < W4:
                        dve.wait_ge(lo_summed, w + 1)
                        dve.tensor_tensor(lo[:, w, :], bank(2 + w % 2, 0, C), row("proj_b", C), ALU.add).then_inc(lo_ready, 1)
                        dve.wait_ge(lo_ready, w + 1)
                        ch.link(dve.bn_stats(gst[:, w, :], lo[:, w, :]))
                    ch.link(dve.bn_aggr(gmv[:, w, :], gst[:, w, :]))
                dve.tensor_scalar(gve[:, :], gmv[:, :, 1], EPS, None, ALU.add).then_inc(gve_ready, 1)
                for w in range(W4):
                    dve.wait_ge(mod_ready, w + 1)
                    dve.tensor_tensor(hbuf[:, w, :], bank(7, 0, C), row("mod_b", C), ALU.add).then_inc(mod_copied, 1)
                dve.wait_ge(gq_read, 1)
                dve.wait_ge(grs_ready, 1)
                ch.link(dve.scalar_tensor_tensor(out=gqn[:, :], in0=gqraw[:, :], scalar=grs[:, W4:W4 + 1],
                                                 in1=brow[:, C:2 * C], op0=ALU.mult, op1=ALU.add))
                dve.wait_ge(gkv_copied, W4)
                ch.link(dve.tensor_tensor(gpr[:, 0, :], gqn[:, :], brow[:, 1024:1024 + C], ALU.mult))
                ch.link(dve.tensor_reduce(gqb[:, :], gpr[:, 0, :].rearrange("p (h d) -> p h d", h=H), AX.X, ALU.add))
                ch.link(dve.tensor_tensor(gpr[:, :, :], gkvs[:, :, 0:C],
                                          gqn[:, :].unsqueeze(1).to_broadcast([P, W4, C]), ALU.mult))
                ch.link(dve.tensor_reduce(gsc[:, :, :].rearrange("p k h -> p (k h)"),
                                          gpr[:, :, :].rearrange("p k (h d) -> p (k h) d", h=H), AX.X, ALU.add))
                rk = grs[:, 0:W4].unsqueeze(2).to_broadcast([P, W4, H])
                ch.link(dve.tensor_tensor(gsc[:, :, :], gsc[:, :, :], rk, ALU.mult))
                ch.link(dve.tensor_tensor(gsc[:, :, :], gsc[:, :, :], gqb[:, :].unsqueeze(1).to_broadcast([P, W4, H]), ALU.add))
                ch.link(dve.tensor_reduce(gmx[:, :], gsc[:, :, :].rearrange("p k h -> p h k"), AX.X, ALU.max))
                dve.tensor_tensor(gsc[:, :, :], gsc[:, :, :], gmx[:, :].unsqueeze(1).to_broadcast([P, W4, H]),
                                  ALU.subtract).then_inc(gsc_ready, 1)
                dve.wait_ge(gex_ready, 1)
                ch.link(dve.tensor_reduce(gmx[:, :], gex[:, :, :].rearrange("p k h -> p h k"), AX.X, ALU.add))
                ch.link(dve.reciprocal(gmx[:, :], gmx[:, :]))
                ch.link(dve.tensor_tensor(gex[:, :, :], gex[:, :, :], gmx[:, :].unsqueeze(1).to_broadcast([P, W4, H]), ALU.mult))
                ch.link(dve.tensor_tensor(gex[:, :, :], gex[:, :, :], rk, ALU.mult))
                ch.link(dve.tensor_tensor(gpr[:, :, :].rearrange("p k (h d) -> p (k h) d", h=H),
                                          gkvs[:, :, C:2 * C].rearrange("p k (h d) -> p k h d", h=H),
                                          gex[:, :, :].unsqueeze(3).to_broadcast([P, W4, H, DH]), ALU.mult))
                ch.link(dve.tensor_reduce(gqn[:, :], gpr[:, :, :].rearrange("p k c -> p c k"), AX.X, ALU.add))
                dve.tensor_tensor(gag[:, :], gqn[:, :], brow[:, 1024 + C:1536], ALU.add).then_inc(gag_ready, 1)
                ch.link(dve.tensor_tensor(gqraw[:, :], row("gproj_b", C), row("cls", C), ALU.add))
                dve.wait_ge(cls_ready, 1)
                ch.link(dve.tensor_tensor(hbuf[:, W4, :], bank(2, 0, C), gqraw[:, :], ALU.add))
        glo.close()
        tok.close()

        siluz = sb("siluz", [P, 2, L, DI])
        skip = sb("skip", [P, 2, L, DI])
        CT = sb("CT", [P, 2, L, B])
        pre = ExitStack()
        xn = sb("xn", [P, L, C], ctx=pre)
        xnT = sb("xnT", [P, CH, L * B], ctx=pre)
        xcT = sb("xcT", [P, 2, DC, L * B], ctx=pre)
        acc = sb("acc", [P, 2, L * B], ctx=pre)
        dbl = sb("dbl", [NX, 2, L * B], ctx=pre)
        dtT = sb("dtT", [33, 2, L * B], ctx=pre)
        bct = sb("bct", [P, 2, L, NX], ctx=pre)
        cbp = sb("cbp", [P, L, NS], ctx=pre)
        cb = sb("cb", [P, 2, L], ctx=pre)
        bd = sb("bd", [P, L, GB, NS], ctx=pre)
        cd = sb("cd", [P, L, GB, NS], ctx=pre)
        bhi = sb("bhi", [P, L * P], BF16, ctx=pre)
        bmi = sb("bmi", [P, L * P], BF16, ctx=pre)
        blo = sb("blo", [P, L * P], BF16, ctx=pre)
        xst = sb("xst", [P, L, 6], ctx=pre)
        xmv = sb("xmv", [P, L, 2], ctx=pre)
        xv1 = sb("xv1", [P, L], ctx=pre)
        xr1 = sb("xr1", [P, L], ctx=pre)
        xv2 = sb("xv2", [P, L], ctx=pre)
        xr2 = sb("xr2", [P, L], ctx=pre)
        ez = sb("ez", [P, 2, DI], ctx=pre)
        ln1 = sb("ln1", [P, 2, DI], ctx=pre)
        w1 = sb("w1", [P, 2, DI], ctx=pre)
        delta = sb("delta", [P, 2, DI], ctx=pre)
        dres = sb("dres", [P, 2, DI], ctx=pre)
        uu = sb("uu", [P, 2, DI], ctx=pre)
        ures = sb("ures", [P, 2, DI], ctx=pre)
        xD = sb("xD", [P, 2, DI], ctx=pre)
        bz = sb("bz", [P, L * P], BF16, ctx=pre)
        bz_ready = sem("bz_ready")
        dpt = sb("dpt", [P, 2, 3, DI], BF16, ctx=pre)
        upt = sb("upt", [P, 2, 3, DI], BF16, ctx=pre)
        xv1_ready, xr1_ready, xv2_ready, xr2_ready = sem("xv1_ready"), sem("xr1_ready"), sem("xv2_ready"), sem("xr2_ready")
        xn_ready, xnT_ready, xnT_copied, x_chain = sem("xn_ready"), sem("xnT_ready"), sem("xnT_copied"), sem("x_chain")
        xi_ready, acc_begun, acc_ready, xc_ready = sem("xi_ready"), sem("acc_begun"), sem("acc_ready"), sem("xc_ready")
        z_ready, z_copied, dbl_ready, dbl_copied = sem("z_ready"), sem("z_copied"), sem("dbl_ready"), sem("dbl_copied")
        dtT_zero, dtT_ones, bc_ready, bct_ready = sem("dtT_zero"), sem("dtT_ones"), sem("bc_ready"), sem("bct_ready")
        cd_ready, cdT_ready, CT_ready = sem("cd_ready"), sem("cdT_ready"), sem("CT_ready")
        bd_ready, bhi_ready, bres_ready, bmi_ready = sem("bd_ready"), sem("bhi_ready"), sem("bres_ready"), sem("bmi_ready")
        blo_ready, b_stored = sem("blo_ready"), sem("b_stored")
        dp_ready, xt_ready, ab_done, ez_ready, ln_ready = sem("dp_ready"), sem("xt_ready"), sem("ab_done"), sem("ez_ready"), sem("ln_ready")
        delta_ready, u_ready, item_done, dres_ready = sem("delta_ready"), sem("u_ready"), sem("item_done"), sem("dres_ready")
        dhi_ready, dmi_ready, uhi_ready, umi_ready = sem("dhi_ready"), sem("dmi_ready"), sem("uhi_ready"), sem("umi_ready")
        ures_ready, dlo_ready, ulo_ready = sem("ures_ready"), sem("dlo_ready"), sem("ulo_ready")
        p_stored = [sem(f"p_stored{q}") for q in range(2)]
        ITEMS = [(d, t) for d in range(2) for t in range(L)]

        with nc.Block() as block:
            @block.tensor
            def _(pe):
                for t in range(L):
                    pe.wait_ge(xn_ready, t + 1)
                    for h in range(CH):
                        mm = pe.transpose(ps[:, h * 1024 + t * B:h * 1024 + (t + 1) * B], xn[:, t, h * P:(h + 1) * P],
                                          ident[:, :])
                mm.then_inc(xnT_ready, 1)
                pe.wait_ge(xnT_copied, CH)

                def xi(n):
                    d, c = divmod(n, DC)
                    if n >= 2:
                        pe.wait_ge(acc_ready, n - 1)
                    for lo_, hi_ in ((0, 512), (512, L * B)):
                        for h in range(CH):
                            mm = pe.matmul(ps[:, (n % 2) * 1024 + lo_:(n % 2) * 1024 + hi_],
                                           inw[:, d, h, c * P:(c + 1) * P], xnT[:, h, lo_:hi_],
                                           start=(h == 0), stop=(h == CH - 1))
                    mm.then_inc(xi_ready, 1)

                def z(n):
                    d, t = ITEMS[n]
                    if n >= 2:
                        pe.wait_ge(z_copied, n - 1)
                    for h in range(CH):
                        mm = pe.matmul(bank(4 + n % 2), xnT[:, h, t * B:(t + 1) * B], inw[:, d, h, DI:2 * DI],
                                       start=(h == 0), stop=(h == CH - 1))
                    mm.then_inc(z_ready, 1)

                for n in range(len(ITEMS)):
                    if n < 2 * DC:
                        xi(n)
                    z(n)
                pe.wait_ge(acc_ready, 2 * DC)
                for d in range(2):
                    pe.wait_ge(xc_ready, (d + 1) * DC)
                    for lo_, hi_ in ((0, 512), (512, L * B)):
                        for c in range(DC):
                            mm = pe.matmul(ps[0:NX, d * 1024 + lo_:d * 1024 + hi_], xpw[:, d, c, :],
                                           xcT[:, d, c, lo_:hi_], start=(c == 0), stop=(c == DC - 1))
                    mm.then_inc(dbl_ready, 1)
                for d in range(2):
                    pe.wait_ge(dbl_copied, 2 * d + 1)
                    for t in range(L):
                        mm = pe.transpose(bank(6 + d, t * NX, (t + 1) * NX), dbl[:, d, t * B:(t + 1) * B],
                                          ident[0:NX, 0:NX])
                    mm.then_inc(bc_ready, 1)

                def steps(n):
                    d, t = ITEMS[n]
                    if n >= 2:
                        pe.wait_ge(item_done, n - 1)
                    if n == 0:
                        pe.wait_ge(dbl_copied, 4)
                        pe.wait_ge(dtT_ones, 1)
                    mm = pe.matmul(bank(n % 2), dtT[:, d, t * B:(t + 1) * B], dtw[:, d, :], start=True, stop=True)
                    mm.then_inc(dp_ready, 1)
                    for c in range(DC):
                        mm = pe.transpose(bank(2 + n % 2, c * P, (c + 1) * P), xcT[:, d, c, t * B:(t + 1) * B], ident[:, :])
                    mm.then_inc(xt_ready, 1)

                def c_turned(d):
                    pe.wait_ge(cd_ready, d + 1)
                    if d == 1:
                        pe.wait_ge(CT_ready, 1)
                    else:
                        pe.wait_ge(z_copied, len(ITEMS))
                    for t in range(L):
                        mm = pe.transpose(ps[:, 4 * 512 + t * P:4 * 512 + (t + 1) * P],
                                          cd[:, t, :, :].rearrange("p g n -> p (g n)"), ident[:, :])
                    mm.then_inc(cdT_ready, 1)

                for n in range(len(ITEMS)):
                    steps(n)
                    if n == 1:
                        c_turned(0)
                    if n == 4:
                        c_turned(1)

            @block.scalar
            def _(act):
                act.wait_ge(xnT_ready, 1)
                for h in range(CH):
                    act.activation(xnT[:, h, :], ps[:, h * 1024:h * 1024 + L * B], ACT.Identity,
                                   scale=col("ln_g", h), bias=col("ln_b", h)).then_inc(xnT_copied, 1)

                def conv_begin(n):
                    d, c = divmod(n, DC)
                    act.wait_ge(xi_ready, n + 1)
                    if n >= 2:
                        act.wait_ge(xc_ready, n - 1)
                    act.activation(acc[:, n % 2, :], ps[:, (n % 2) * 1024:(n % 2) * 1024 + L * B], ACT.Identity,
                                   scale=col(f"cw{d}", 4 * c + 3), bias=col(f"cb{d}", c)).then_inc(acc_begun, 1)

                def conv_end(n):
                    d, c = divmod(n, DC)
                    act.wait_ge(acc_ready, n + 1)
                    act.activation(xcT[:, d, c, :], acc[:, n % 2, :], ACT.Silu).then_inc(xc_ready, 1)

                for n in range(len(ITEMS)):
                    if n < 2 * DC:
                        conv_begin(n)
                    if 1 <= n <= 2 * DC:
                        conv_end(n - 1)
                    act.wait_ge(z_ready, n + 1)
                    act.activation(siluz[:, ITEMS[n][0], ITEMS[n][1], :], bank(4 + n % 2), ACT.Silu).then_inc(z_copied, 1)
                for d in range(2):
                    act.wait_ge(dbl_ready, d + 1)
                    act.activation(dbl[:, d, :], ps[0:NX, d * 1024:d * 1024 + L * B], ACT.Copy).then_inc(dbl_copied, 1)
                    if d == 0:
                        act.wait_ge(dtT_ones, 1)
                    act.activation(dtT[0:R, d, :], ps[0:R, d * 1024:d * 1024 + L * B], ACT.Copy).then_inc(dbl_copied, 1)

                def parts(d):
                    act.wait_ge(bd_ready, d + 1)
                    if d == 1:
                        act.wait_ge(b_stored, 128)
                    act.activation(bhi[:, :], bd[:, :, :, :].rearrange("p t g n -> p (t g n)"), ACT.Copy).then_inc(bhi_ready, 1)
                    act.wait_ge(bres_ready, d + 1)
                    act.activation(bmi[:, :], bd[:, :, :, :].rearrange("p t g n -> p (t g n)"), ACT.Copy).then_inc(bmi_ready, 1)

                act.activation(expA[:, :, :], expA[:, :, :], ACT.Exp).then_inc(expA_ready, 1)
                for n in range(len(ITEMS) + 1):
                    q, o = n % 2, 1 - n % 2
                    now, then = n < len(ITEMS), n >= 1
                    if now:
                        act.wait_ge(dp_ready, n + 1)
                        if n >= 2:
                            act.wait_ge(delta_ready, n - 1)
                        act.activation(ez[:, q, :], bank(q), ACT.Abs).then_inc(ab_done, 1)
                        act.wait_ge(ab_done, n + 1)
                        act.activation(ez[:, q, :], ez[:, q, :], ACT.Exp, scale=-1.0).then_inc(ez_ready, 1)
                        act.wait_ge(ez_ready, n + 1)
                        act.activation(ln1[:, q, :], ez[:, q, :], ACT.Ln, bias=1.0).then_inc(ln_ready, 1)
                    if then:
                        act.wait_ge(delta_ready, n)
                        if n >= 3:
                            act.wait_ge(p_stored[o], 32 * ((n - 1) // 2))
                        act.activation(dpt[:, o, 0, :], delta[:, o, :], ACT.Copy).then_inc(dhi_ready, 1)
                        act.wait_ge(u_ready, n)
                        act.activation(upt[:, o, 0, :], uu[:, o, :], ACT.Copy).then_inc(uhi_ready, 1)
                        act.wait_ge(dres_ready, n)
                        act.activation(dpt[:, o, 1, :], dres[:, o, :], ACT.Copy).then_inc(dmi_ready, 1)
                        act.wait_ge(ures_ready, n)
                        act.activation(upt[:, o, 1, :], ures[:, o, :], ACT.Copy).then_inc(umi_ready, 1)
                    if n == 1:
                        parts(0)
                    if n == 2:
                        act.wait_ge(cdT_ready, 1)
                        act.activation(CT[:, 0, :, :], ps[:, 2048:2048 + L * B], ACT.Copy).then_inc(CT_ready, 1)
                    if n == 4:
                        parts(1)
                    if n == 6:
                        act.wait_ge(cdT_ready, 2)
                        act.activation(CT[:, 1, :, :], ps[:, 2048:2048 + L * B], ACT.Copy).then_inc(CT_ready, 1)

            @block.gpsimd
            def _(pool):
                pool.memset(bz[:, :], 0.0).then_inc(bz_ready, 1)
                pool.memset(dtT[:, :, :], 0.0).then_inc(dtT_zero, 1)
                pool.wait_ge(dtT_zero, 1)
                pool.memset(dtT[32:33, :, :], 1.0).then_inc(dtT_ones, 1)
                pool.wait_ge(dtT_ones, 1)
                pool.wait_ge(xv1_ready, 1)
                pool.tensor_tensor(xr1[:, :], xv1[:, :], mhalf[:, 0:L], ALU.pow).then_inc(xr1_ready, 1)
                pool.wait_ge(xv2_ready, 1)
                pool.tensor_tensor(xr2[:, :], xv2[:, :], mhalf[:, 0:L], ALU.pow).then_inc(xr2_ready, 1)
                for n in range(len(ITEMS)):
                    q = n % 2
                    pool.wait_ge(uhi_ready, n + 1)
                    if n >= 2:
                        pool.wait_ge(umi_ready, n - 1)
                    pool.tensor_tensor(ures[:, q, :], uu[:, q, :], upt[:, q, 0, :], ALU.subtract).then_inc(ures_ready, 1)
                    pool.wait_ge(dmi_ready, n + 1)
                    pool.tensor_tensor(dpt[:, q, 2, :], dres[:, q, :], dpt[:, q, 1, :], ALU.subtract).then_inc(dlo_ready, 1)
                    pool.wait_ge(umi_ready, n + 1)
                    pool.tensor_tensor(upt[:, q, 2, :], ures[:, q, :], upt[:, q, 1, :], ALU.subtract).then_inc(ulo_ready, 1)

            @block.vector
            def _(dve):
                ch = Chain(dve, x_chain)
                for t in range(L):
                    ch.link(dve.bn_stats(xst[:, t, :], hbuf[:, t, :]))
                    ch.link(dve.bn_aggr(xmv[:, t, :], xst[:, t, :]))
                dve.tensor_scalar(xv1[:, :], xmv[:, :, 1], EPS, None, ALU.add).then_inc(xv1_ready, 1)
                dve.wait_ge(xr1_ready, 1)
                ch.link(dve.tensor_tensor(xv2[:, :], xr1[:, :], xr1[:, :], ALU.mult))
                ch.link(dve.tensor_tensor(xv2[:, :], xv2[:, :], xmv[:, :, 1], ALU.mult))
                dve.tensor_scalar(xv2[:, :], xv2[:, :], EPS, None, ALU.add).then_inc(xv2_ready, 1)
                dve.wait_ge(xr2_ready, 1)
                ch.link(dve.tensor_tensor(xr1[:, :], xr1[:, :], xr2[:, :], ALU.mult))
                for t in range(L):
                    dve.tensor_scalar(xn[:, t, :], hbuf[:, t, :], xmv[:, t, 0:1], xr1[:, t:t + 1], ALU.subtract,
                                      ALU.mult).then_inc(xn_ready, 1)
                for n in range(2 * DC):
                    d, c = divmod(n, DC)
                    dve.wait_ge(acc_begun, n + 1)
                    for back in range(1, 4):
                        m = (L - back) * B
                        o = back * B
                        src = ps[:, (n % 2) * 1024 + (0 if d == 0 else o):(n % 2) * 1024 + (0 if d == 0 else o) + m]
                        dst = acc[:, n % 2, (o if d == 0 else 0):(o if d == 0 else 0) + m]
                        ins = dve.scalar_tensor_tensor(out=dst, in0=src, scalar=col(f"cw{d}", 4 * c + 3 - back),
                                                       in1=dst, op0=ALU.mult, op1=ALU.add)
                        if back < 3:
                            ch.link(ins)
                        else:
                            ins.then_inc(acc_ready, 1)
                mask4 = maskb[:, :, :].unsqueeze(1).to_broadcast([P, L, GB, NS])

                def spread(d):
                    if d == 1:
                        dve.wait_ge(blo_ready, 1)
                        dve.wait_ge(cdT_ready, 1)
                    ch.link(dve.tensor_tensor(bd[:, :, :, :], bct[:, d, :, R:R + NS].unsqueeze(2).to_broadcast([P, L, GB, NS]),
                                              mask4, ALU.mult))
                    dve.sem_inc(bd_ready, 1)
                    dve.tensor_tensor(cd[:, :, :, :], bct[:, d, :, R + NS:NX].unsqueeze(2).to_broadcast([P, L, GB, NS]),
                                      mask4, ALU.mult).then_inc(cd_ready, 1)

                def b_parts(d):
                    flat = bd[:, :, :, :].rearrange("p t g n -> p (t g n)")
                    dve.wait_ge(bhi_ready, d + 1)
                    dve.tensor_tensor(flat, flat, bhi[:, :], ALU.subtract).then_inc(bres_ready, 1)
                    dve.wait_ge(bmi_ready, d + 1)
                    dve.tensor_tensor(blo[:, :], flat, bmi[:, :], ALU.subtract).then_inc(blo_ready, 1)

                for d in range(2):
                    dve.wait_ge(bc_ready, d + 1)
                    ch.link(dve.tensor_copy(bct[:, d, :, :].rearrange("p t n -> p (t n)"), bank(6 + d, 0, L * NX)))
                    ch.link(dve.tensor_tensor(cbp[:, :, :], bct[:, d, :, R:R + NS], bct[:, d, :, R + NS:NX], ALU.mult))
                    ch.link(dve.tensor_reduce(cb[:, d, :], cbp[:, :, :], AX.X, ALU.add))
                spread(0)
                for n, (d, t) in enumerate(ITEMS):
                    q = n % 2
                    dve.wait_ge(ln_ready, n + 1)
                    ch.link(dve.tensor_scalar(w1[:, q, :], ez[:, q, :], 1.0, -1.0, ALU.add, ALU.add))
                    ch.link(dve.scalar_tensor_tensor(out=w1[:, q, :], in0=w1[:, q, :], scalar=-1.0, in1=ez[:, q, :],
                                                     op0=ALU.mult, op1=ALU.add))
                    ch.link(dve.tensor_tensor(ln1[:, q, :], ln1[:, q, :], w1[:, q, :], ALU.add))
                    if n >= 2:
                        dve.wait_ge(dhi_ready, n - 1)
                    dve.scalar_tensor_tensor(out=delta[:, q, :], in0=bank(q), scalar=0.0, in1=ln1[:, q, :],
                                             op0=ALU.max, op1=ALU.add).then_inc(delta_ready, 1)
                    dve.wait_ge(delta_ready, n + 1)
                    dve.wait_ge(xt_ready, n + 1)
                    if n >= 2:
                        dve.wait_ge(ures_ready, n - 1)
                    dve.tensor_tensor(uu[:, q, :], delta[:, q, :], bank(2 + q), ALU.mult).then_inc(u_ready, 1)
                    ch.link(dve.tensor_tensor(xD[:, q, :], bank(2 + q), row(f"D{d}", DI), ALU.mult))
                    dve.sem_inc(item_done, 1)
                    dve.wait_ge(dhi_ready, n + 1)
                    if n >= 2:
                        dve.wait_ge(dlo_ready, n - 1)
                    dve.tensor_tensor(dres[:, q, :], delta[:, q, :], dpt[:, q, 0, :], ALU.subtract).then_inc(dres_ready, 1)
                    dve.wait_ge(u_ready, n + 1)
                    ch.link(dve.scalar_tensor_tensor(out=skip[:, d, t, :], in0=uu[:, q, :], scalar=cb[:, d, t:t + 1],
                                                     in1=xD[:, q, :], op0=ALU.mult, op1=ALU.add))
                    if n == 0:
                        b_parts(0)
                    if n == 2:
                        spread(1)
                    if n == 3:
                        b_parts(1)

            @block.sync
            def _(sp):
                def store_b(d):
                    sp.wait_ge(blo_ready, d + 1)
                    for k, src in enumerate([bhi, bhi, bhi, bmi, bmi, blo]):
                        sp.dma_start(bparts[2 * k + d, :, d * L * P:(d + 1) * L * P], src[:, :]).then_inc(b_stored, 16)

                sp.wait_ge(bz_ready, 1)
                for d in range(2):
                    sp.dma_start(bparts[d:12:2, :, (1 - d) * L * P:(2 - d) * L * P].rearrange("k b n -> b k n"),
                                 bz[:, :].unsqueeze(1).to_broadcast([P, 6, L * P])).then_inc(b_stored, 16)
                for n, (d, t) in enumerate(ITEMS):
                    q = n % 2
                    sp.wait_ge(dlo_ready, n + 1)
                    sp.wait_ge(ulo_ready, n + 1)
                    o = t * DI
                    sp.dma_start(dparts[d:6:2, :, o:o + DI].rearrange("k b n -> b k n"), dpt[:, q]).then_inc(p_stored[q], 16)
                    sp.dma_start(uparts[d:6:2, :, o:o + DI].rearrange("k b n -> b k n"), upt[:, q]).then_inc(p_stored[q], 16)
                    if n == 1:
                        store_b(0)
                    if n == 4:
                        store_b(1)
                sp.wait_ge(b_stored, 224)
                for q in range(2):
                    sp.wait_ge(p_stored[q], 32 * 5)
        pre.close()

        scn = ExitStack()
        drows = sb("drows", [KS, 2, L * DI], BF16, ctx=scn)
        urows = sb("urows", [KS, 2, L * DI], BF16, ctx=scn)
        brows = sb("brows", [KS, 2, 2 * L * P], BF16, ctx=scn)
        da = sb("da", [P, 8, DI], ctx=scn)
        gb = sb("gb", [P, 8, DI], ctx=scn)
        hb = sb("hb", [P, 2, 2, DI], ctx=scn)
        cst = sb("cst", [P, 2, 2, L, GB], ctx=scn)
        yst = sb("yst", [P, 2, DI], ctx=scn)
        rows_landed = [sem(f"rows_landed{q}") for q in range(2)]
        e_ready, e_free, da_ready = sem("e_ready"), sem("e_free"), sem("da_ready")
        bu_ready, bu_used, gp_done = sem("bu_ready"), sem("bu_used"), sem("gp_done")
        c_staged, y_done, y_copied, y_zero = sem("c_staged"), sem("y_done"), sem("y_copied"), sem("y_zero")
        y_stored = [sem(f"y_stored{k}") for k in range(2)]
        d_padded = sem("d_padded")
        NPAIR = NG // 2
        NGP = 6

        def token(s_, d):
            return s_ if d == 0 else L - 1 - s_

        def pairs(eng, body):
            body(0, True, False)
            with eng.Fori(1, NPAIR - 1) as i:
                body(i, False, False)
            body(NPAIR - 1, False, True)

        with nc.Block() as block:
            @block.sync
            def _(sp):
                def load_rows(g, q):
                    im = bass.ds(g * GB, GB)
                    sp.dma_start(drows[0:6 * GB, q], dparts[:, im, :]).then_inc(rows_landed[q], 16)
                    for lo_, n in ((0, 6), (6, 4), (10, 2)):
                        sp.dma_start(urows[lo_ * GB:(lo_ + n) * GB, q], uparts[0:n, im, :]).then_inc(rows_landed[q], 16)
                    sp.dma_start(brows[:, q], bparts[:, im, :]).then_inc(rows_landed[q], 16)

                def store_y(g, k):
                    sp.wait_ge(y_copied, 2 + 2 * g + k + 1)
                    sp.dma_start(yscr[bass.ds(g, 1), k], yst[0:NY, k, :]).then_inc(y_stored[k], 16)

                sp.wait_ge(d_padded, 1)
                load_rows(0, 0)
                load_rows(1, 1)

                def body(i, first, last):
                    for q in range(2):
                        g = 2 * i + q
                        if not (first and q == 0):
                            store_y(g - 1, 1)
                        if not last:
                            sp.wait_ge(e_ready, 8 * g + 8)
                            sp.wait_ge(bu_ready, 8 * g + 8)
                            load_rows(g + 2, q)
                        store_y(g, 0)

                pairs(sp, body)
                store_y(NG - 1, 1)
                for k in range(2):
                    sp.wait_ge(y_stored[k], 16 * NG)

            @block.tensor
            def _(pe):
                def spread_delta(g, q, j):
                    d, t = j % 2, token(1 + j // 2, j % 2)
                    pe.wait_ge(e_free, 8 * g + j + 1)
                    pe.matmul(bank(j % 2), selb[:, d, :], drows[:, q, t * DI:(t + 1) * DI],
                              start=True, stop=True).then_inc(e_ready, 1)

                def b_times_u(g, q, j):
                    t = token(j // 2, j % 2)
                    o = (j % 2) * L + t
                    pe.wait_ge(bu_used, 8 * g + j + 1)
                    pe.matmul(bank(2 + j % 4), brows[:, q, o * P:(o + 1) * P], urows[:, q, t * DI:(t + 1) * DI],
                              start=True, stop=True).then_inc(bu_ready, 1)

                def outputs(g, q, k):
                    pe.wait_ge(y_copied, 2 * g + k + 1)
                    if k == 0:
                        pe.wait_ge(c_staged, g + 1)
                        pe.wait_ge(bu_used, 4 + 8 * g + 2)
                        pe.wait_ge(gp_done, NGP + NGP * g + 2)
                    else:
                        pe.wait_ge(gp_done, NGP + NGP * g + NGP)
                    for j in range(4):
                        d, s_ = j % 2, 2 * k + 1 + j // 2
                        mm = pe.matmul(ps[32 * j:32 * j + GB, (6 + k) * 512:(7 + k) * 512], cst[:, q, d, token(s_, d), :],
                                       gb[:, 4 * k + j, :], start=True, stop=True)
                    mm.then_inc(y_done, 1)

                def begin(g, q, i):
                    pe.wait_ge(rows_landed[q], 80 * i + 80)

                pe.wait_ge(y_zero, 1)
                begin(0, 0, 0)
                for j in range(4):
                    spread_delta(0, 0, j)
                for j in range(4):
                    b_times_u(0, 0, j)
                spread_delta(0, 0, 4)

                def body(i, first, last):
                    for q in range(2):
                        g = 2 * i + q
                        after = not (last and q == 1)
                        spread_delta(g, q, 5)
                        b_times_u(g, q, 4)
                        spread_delta(g, q, 6)
                        b_times_u(g, q, 5)
                        b_times_u(g, q, 6)
                        spread_delta(g, q, 7)
                        b_times_u(g, q, 7)
                        if after:
                            begin(g + 1, 1 - q, i + q)
                            spread_delta(g + 1, 1 - q, 0)
                            spread_delta(g + 1, 1 - q, 1)
                        outputs(g, q, 0)
                        if after:
                            spread_delta(g + 1, 1 - q, 2)
                            b_times_u(g + 1, 1 - q, 0)
                            b_times_u(g + 1, 1 - q, 1)
                            spread_delta(g + 1, 1 - q, 3)
                            b_times_u(g + 1, 1 - q, 2)
                            b_times_u(g + 1, 1 - q, 3)
                            spread_delta(g + 1, 1 - q, 4)
                        outputs(g, q, 1)

                pairs(pe, body)

            @block.scalar
            def _(act):
                act.sem_inc(y_copied, 2)

                def exponential(g, j):
                    act.wait_ge(e_free, 2 + 8 * g + j + 1)
                    act.activation(da[:, j, :], da[:, j, :], ACT.Exp, scale=-1.0).then_inc(da_ready, 1)

                def copy_y(g, k):
                    act.wait_ge(y_done, 2 + 2 * g + k + 1)
                    act.wait_ge(y_stored[k], 16 * g)
                    act.activation(yst[0:NY, k, :], bank(6 + k, p=NY), ACT.Copy).then_inc(y_copied, 1)

                def stage_c(g, q):
                    act.activation(cst[:, q, :, :, :].rearrange("p d t b -> p (d t) b"),
                                   CT[:, :, :, bass.ds(g * GB, GB)].rearrange("p d t b -> p (d t) b"),
                                   ACT.Copy).then_inc(c_staged, 1)

                for j in range(5):
                    exponential(0, j)

                def body(i, first, last):
                    for q in range(2):
                        g = 2 * i + q
                        after = not (last and q == 1)
                        stage_c(g, q)
                        exponential(g, 5)
                        exponential(g, 6)
                        if not (first and q == 0):
                            copy_y(g - 1, 1)
                        exponential(g, 7)
                        if after:
                            exponential(g + 1, 0)
                            exponential(g + 1, 1)
                        copy_y(g, 0)
                        if after:
                            for j in range(2, 5):
                                exponential(g + 1, j)

                pairs(act, body)
                copy_y(NG - 1, 1)

            @block.gpsimd
            def _(pool):
                pool.sem_inc(gp_done, NGP)

                def decayed(g, s_, d):
                    j = 2 * (s_ - 1) + d
                    pool.wait_ge(da_ready, 8 * g + j + 1)
                    pool.wait_ge(bu_used, 4 + 8 * g + 2 * (s_ - 1) + d + 1)
                    if j == 2:
                        pool.wait_ge(y_done, 2 * g + 1)
                    if j == 4:
                        pool.wait_ge(y_done, 2 * g + 2)
                    pool.tensor_tensor(gb[:, j, :], da[:, j, :], hb[:, d, (s_ - 1) % 2, :], ALU.mult).then_inc(gp_done, 1)

                def body(i, first, last):
                    for q in range(2):
                        for s_, d in [(2, 0), (2, 1), (3, 0), (3, 1), (4, 0), (4, 1)]:
                            decayed(2 * i + q, s_, d)

                pairs(pool, body)

            @block.vector
            def _(dve):
                dve.memset(drows[:, :, :], 0.0).then_inc(d_padded, 1)
                dve.memset(ps[:, 6 * 512:8 * 512], 0.0).then_inc(y_zero, 1)
                dve.sem_inc(e_free, 2)
                dve.sem_inc(bu_used, 4)
                dve.sem_inc(y_done, 2)

                def argument(g, j):
                    dve.wait_ge(e_ready, 8 * g + j + 1)
                    dve.tensor_tensor(da[:, j, :], bank(j % 2), expA[:, j % 2, :], ALU.mult).then_inc(e_free, 1)

                def decayed_1(g, d):
                    dve.wait_ge(da_ready, 8 * g + d + 1)
                    if d == 0:
                        dve.wait_ge(y_done, 2 * g + 1)
                    dve.wait_ge(bu_ready, 8 * g + d + 1)
                    dve.tensor_tensor(gb[:, d, :], da[:, d, :], bank(2 + d), ALU.mult).then_inc(bu_used, 1)

                def state(g, s_, d):
                    j = 2 * s_ + d
                    dve.wait_ge(bu_ready, 8 * g + j + 1)
                    if s_ == 1:
                        dve.wait_ge(gp_done, NGP * g + 5 + d)
                        dve.wait_ge(bu_used, 4 + 8 * g + d + 1)
                    else:
                        dve.wait_ge(gp_done, NGP + NGP * g + 2 * (s_ - 2) + d + 1)
                    dve.tensor_tensor(hb[:, d, s_ % 2, :], gb[:, 2 * (s_ - 1) + d, :], bank(2 + j % 4),
                                      ALU.add).then_inc(bu_used, 1)

                for j in range(4):
                    argument(0, j)
                for d in range(2):
                    decayed_1(0, d)
                argument(0, 4)

                def body(i, first, last):
                    for q in range(2):
                        g = 2 * i + q
                        after = not (last and q == 1)
                        state(g, 1, 0)
                        state(g, 1, 1)
                        argument(g, 5)
                        argument(g, 6)
                        state(g, 2, 0)
                        argument(g, 7)
                        state(g, 2, 1)
                        if after:
                            argument(g + 1, 0)
                        state(g, 3, 0)
                        if after:
                            argument(g + 1, 1)
                        state(g, 3, 1)
                        if after:
                            argument(g + 1, 2)
                            argument(g + 1, 3)
                            decayed_1(g + 1, 0)
                            decayed_1(g + 1, 1)
                            argument(g + 1, 4)

                pairs(dve, body)
        scn.close()

        fin = ExitStack()
        expw = sb("expw", [P, CH, E8 * C], ctx=fin)
        yg = sb("yg", [P, 2, 2, DI], ctx=fin)
        ytok = sb("ytok", [P, 2, L, DI], ctx=fin)
        y_landed = [sem(f"y_landed{n}") for n in range(L)]
        ygT = sb("ygT", [P, 2, 2, DC, P], ctx=fin)
        h1 = sb("h1", [P, L, C], ctx=fin)
        xf = sb("xf", [P, L, C], ctx=fin)
        mo = sb("mo", [P, L, C], ctx=fin)
        xfT = sb("xfT", [P, 2, CH, P], ctx=fin)
        fst = sb("fst", [P, L, 6], ctx=fin)
        fmv = sb("fmv", [P, L, 2], ctx=fin)
        fve = sb("fve", [P, L], ctx=fin)
        frs = sb("frs", [P, L], ctx=fin)
        eid = sb("eid", [P, E8], ctx=fin)
        gsco = sb("gsco", [P, L, E8], ctx=fin)
        gtop = sb("gtop", [P, L, E8], ctx=fin)
        gidx = sb("gidx", [P, L, E8], mybir.dt.uint32, ctx=fin)
        gidf = sb("gidf", [P, L], ctx=fin)
        hot = sb("hot", [P, L, E8], ctx=fin)
        w_landed, ysum_done, yg_ready, ygt_ready, ygt_copied = (sem("w_landed"), sem("ysum_done"), sem("yg_ready"),
                                                                sem("ygt_ready"), sem("ygt_copied"))
        o_ready, h1_ready, fve_ready, frs_ready, xf_ready = (sem("o_ready"), sem("h1_ready"), sem("fve_ready"),
                                                             sem("frs_ready"), sem("xf_ready"))
        xt5_ready, xt5_copied, gate_ready, gate_read = sem("xt5_ready"), sem("xt5_copied"), sem("gate_ready"), sem("gate_read")
        ex5_ready, ex5_used, mo_ready, o_stored, f_chain = (sem("ex5_ready"), sem("ex5_used"), sem("mo_ready"),
                                                            sem("o_stored"), sem("f_chain"))
        with nc.Block() as block:
            @block.sync
            def _(sp):
                for n in range(L):
                    for d in range(2):
                        if (n, d) not in ((0, 0), (L - 1, 1)):
                            s_ = token(n, d)
                            j = 2 * ((s_ - 1) % 2) + d
                            sp.dma_start(ytok[:, d, n, :], yscr[:, (s_ - 1) // 2, 32 * j:32 * j + GB, :]).then_inc(y_landed[n], 16)
                sp.dma_start(expw[:, :, :], a["expert_wT"].rearrange("(h p) n -> p h n", p=P)).then_inc(w_landed, 16)
                for t in range(L):
                    sp.wait_ge(mo_ready, t + 1)
                    sp.dma_start(out[:, t, :], mo[:, t, :]).then_inc(o_stored, 16)
                sp.wait_ge(o_stored, 16 * L)

            @block.gpsimd
            def _(pool):
                def total(n):
                    pool.wait_ge(y_landed[n], 16 if n in (0, L - 1) else 32)
                    for d in range(2):
                        if (n, d) not in ((0, 0), (L - 1, 1)):
                            pool.tensor_tensor(skip[:, d, n, :], skip[:, d, n, :], ytok[:, d, n, :], ALU.add).then_inc(ysum_done, 1)

                def root(n):
                    pool.wait_ge(fve_ready, n + 1)
                    pool.tensor_tensor(frs[:, n:n + 1], fve[:, n:n + 1], mhalf[:, 0:1], ALU.pow).then_inc(frs_ready, 1)

                total(0)
                total(1)
                for n in range(L):
                    if n + 2 < L:
                        total(n + 2)
                    root(n)

            @block.tensor
            def _(pe):
                def turned(n):
                    for d in range(2):
                        pe.wait_ge(yg_ready, 2 * n + d + 1)
                        if n >= 1:
                            pe.wait_ge(ygt_copied, 2 * n + d - 1)
                        for c in range(DC):
                            mm = pe.transpose(bank(d, c * P, (c + 1) * P), yg[:, n % 2, d, c * P:(c + 1) * P], ident[:, :])
                        mm.then_inc(ygt_ready, 1)

                def projected(n):
                    if n >= 2:
                        pe.wait_ge(h1_ready, n - 1)
                    for d in range(2):
                        pe.wait_ge(ygt_copied, 2 * n + d + 1)
                        for c in range(DC):
                            mm = pe.matmul(bank(2 + n % 2, 0, C), ygT[:, n % 2, d, c, :], outw[:, d, c, :],
                                           start=(d == 0 and c == 0), stop=(d == 1 and c == DC - 1))
                    mm.then_inc(o_ready, 1)

                def experts(n):
                    pe.wait_ge(xf_ready, n + 1)
                    if n >= 1:
                        pe.wait_ge(gate_read, n)
                    for h in range(CH):
                        mm = pe.transpose(bank(7, h * P, (h + 1) * P), xf[:, n, h * P:(h + 1) * P], ident[:, :])
                    mm.then_inc(xt5_ready, 1)
                    pe.wait_ge(xt5_copied, n + 1)
                    for h in range(CH):
                        mm = pe.matmul(bank(7, C, C + E8), xfT[:, n % 2, h, :], gatew[:, h, :],
                                       start=(h == 0), stop=(h == CH - 1))
                    mm.then_inc(gate_ready, 1)
                    if n == 0:
                        pe.wait_ge(w_landed, 16)
                    for k in range(E8 // 2):
                        m = 4 * n + k
                        if m >= 3:
                            pe.wait_ge(ex5_used, m - 2)
                        for h in range(CH):
                            mm = pe.matmul(bank(4 + m % 3), xfT[:, n % 2, h, :], expw[:, h, k * 512:(k + 1) * 512],
                                           start=(h == 0), stop=(h == CH - 1))
                        mm.then_inc(ex5_ready, 1)

                for n in range(2):
                    turned(n)
                    projected(n)
                for n in range(L):
                    experts(n)
                    if n + 2 < L:
                        turned(n + 2)
                        projected(n + 2)

            @block.scalar
            def _(act):
                def copy_y(n):
                    for d in range(2):
                        act.wait_ge(ygt_ready, 2 * n + d + 1)
                        if n >= 2:
                            act.wait_ge(o_ready, n - 1)
                        act.activation(ygT[:, n % 2, d, :, :], bank(d), ACT.Copy).then_inc(ygt_copied, 1)

                copy_y(0)
                copy_y(1)
                for n in range(L):
                    act.wait_ge(xt5_ready, n + 1)
                    if n >= 2:
                        act.wait_ge(ex5_ready, 4 * (n - 1))
                    act.activation(xfT[:, n % 2, :, :], bank(7, 0, C), ACT.Copy).then_inc(xt5_copied, 1)
                    if n + 2 < L:
                        copy_y(n + 2)

            @block.vector
            def _(dve):
                ch = Chain(dve, f_chain)
                for e in range(E8):
                    ins = dve.memset(eid[:, e:e + 1], float(e))
                ch.link(ins)
                sums = [0]

                def gated(n):
                    for d in range(2):
                        if (n, d) not in ((0, 0), (L - 1, 1)):
                            sums[0] += 1
                            dve.wait_ge(ysum_done, sums[0])
                        if n >= 2:
                            dve.wait_ge(ygt_ready, 2 * (n - 2) + d + 1)
                        dve.tensor_tensor(yg[:, n % 2, d, :], skip[:, d, n, :], siluz[:, d, n, :], ALU.mult).then_inc(yg_ready, 1)

                def mixed(n):
                    dve.wait_ge(o_ready, n + 1)
                    dve.scalar_tensor_tensor(out=h1[:, n, :], in0=bank(2 + n % 2, 0, C), scalar=0.5, in1=hbuf[:, n, :],
                                             op0=ALU.mult, op1=ALU.add).then_inc(h1_ready, 1)
                    dve.wait_ge(h1_ready, n + 1)
                    ch.link(dve.bn_stats(fst[:, n, :], h1[:, n, :]))
                    ch.link(dve.bn_aggr(fmv[:, n, :], fst[:, n, :]))
                    dve.tensor_scalar(fve[:, n:n + 1], fmv[:, n, 1:2], EPS, None, ALU.add).then_inc(fve_ready, 1)
                    dve.wait_ge(frs_ready, n + 1)
                    dve.tensor_scalar(xf[:, n, :], h1[:, n, :], fmv[:, n, 0:1], frs[:, n:n + 1], ALU.subtract,
                                      ALU.mult).then_inc(xf_ready, 1)
                    dve.wait_ge(xf_ready, n + 1)
                    ch.link(dve.tensor_tensor(mo[:, n, :], h1[:, n, :], xf[:, n, :], ALU.add))

                def chosen(n):
                    dve.wait_ge(gate_ready, n + 1)
                    dve.tensor_copy(gsco[:, n, :], bank(7, C, C + E8)).then_inc(gate_read, 1)
                    dve.wait_ge(gate_read, n + 1)
                    ch.link(dve.max(gtop[:, n, :], gsco[:, n, :]))
                    ch.link(dve.max_index(gidx[:, n, :], gtop[:, n, :], gsco[:, n, :]))
                    ch.link(dve.tensor_copy(gidf[:, n:n + 1], gidx[:, n, 0:1]))
                    ch.link(dve.tensor_scalar(hot[:, n, :], eid[:, :], gidf[:, n:n + 1], None, ALU.is_equal))
                    for k in range(E8 // 2):
                        m = 4 * n + k
                        dve.wait_ge(ex5_ready, m + 1)
                        for e in range(2):
                            ins = dve.scalar_tensor_tensor(out=mo[:, n, :], in0=bank(4 + m % 3, e * C, (e + 1) * C),
                                                           scalar=hot[:, n, 2 * k + e:2 * k + e + 1], in1=mo[:, n, :],
                                                           op0=ALU.mult, op1=ALU.add)
                            if e == 0:
                                ch.link(ins)
                            else:
                                ins.then_inc(ex5_used, 1)
                                dve.wait_ge(ex5_used, m + 1)
                    dve.sem_inc(mo_ready, 1)

                gated(0)
                gated(1)
                mixed(0)
                mixed(1)
                for n in range(L):
                    if n + 2 < L:
                        gated(n + 2)
                    chosen(n)
                    if n + 2 < L:
                        mixed(n + 2)
        fin.close()



def lay_out(x):
    import numpy as np
    g = {k: np.asarray(v) for k, v in x.items()}
    im = g["x"][:, :, :84, :84].reshape(B, 3, 2, 3, 14, 2, 3, 14)
    xT = im.transpose(1, 4, 7, 2, 5, 3, 6, 0).reshape(KP, W4 * WT)
    t = "L0_tok_"
    m = ["L0_attn_f_", "L0_attn_b_"]

    def halves(v):
        return v.reshape(-1, P).T

    def taps(v):
        return v.reshape(DC, P, 4).transpose(1, 0, 2).reshape(P, DC * 4)

    vec_cols = np.concatenate(
        [halves(g[t + n]) for n in ["la_ln_q_g", "la_ln_q_b", "ga_ln_q_g", "ga_ln_q_b", "la_ln_kv_g", "la_ln_kv_b",
                                    "ga_ln_kv_g", "ga_ln_kv_b"]]
        + [halves(g["L0_attn_ln_g"]), halves(g["L0_attn_ln_b"]), halves(g[t + "class_emb"])]
        + [halves(g[p + "conv_b"]) for p in m] + [taps(g[p + "conv_w"]) for p in m], axis=1)
    vec_rows = np.concatenate([g[t + "la_proj_b"], g[t + "mod_b"], g[t + "ga_proj_b"], g[t + "class_emb"],
                               g[m[0] + "D_skip"], g[m[1] + "D_skip"]])[None]
    wall = np.concatenate([g[t + n] for n in ["la_wq", "ga_wq", "la_wkv", "ga_wkv"]], axis=1)
    sel = np.zeros((KS // 2 // GB // 2, 2, GB, 2, GB, NS), np.float32)
    for d in range(2):
        for i in range(GB):
            sel[:, d, i, d, i] = 1
    sel = np.concatenate([sel.reshape(KS // 2, 2 * P), np.zeros((KS // 2, 2 * P), np.float32)])
    both = lambda n, f: np.stack([f(g[p + n]) for p in m])
    arrays = {
        "xT": xT, "sel": sel, "conv_wT": g[t + "conv_w"].reshape(C, KP).T, "vec_cols": vec_cols, "vec_rows": vec_rows,
        "wall": wall, "la_proj_w": g[t + "la_proj_w"], "ga_proj_w": g[t + "ga_proj_w"], "mod_w": g[t + "mod_w"],
        "in_wT": both("in_w", lambda v: v.T), "xproj_wT": both("xproj_w", lambda v: v.T),
        "dt_wT": both("dt_w", lambda v: v.T), "dt_b": both("dt_b", lambda v: v[None]),
        "A_logT": both("A_log", lambda v: v.T), "out_wT": both("out_w", lambda v: v.T),
        "gate_wT": g["L0_ffn_gate_w"].T, "expert_wT": g["L0_ffn_expert_w"].transpose(2, 0, 1).reshape(C, E8 * C),
    }
    return {k: np.ascontiguousarray(v) for k, v in arrays.items()}


def kernel(**inputs):
    import numpy as np
    import concourse.bacc as bacc
    from concourse.bass_utils import run_bass_kernel_spmd

    arrays = lay_out(inputs)
    nc = bacc.Bacc("TRN2", target_bir_lowering=False, num_devices=1)
    aps = {n: nc.dram_tensor("in_" + n, v.shape, mybir.dt.from_np(v.dtype), kind="ExternalInput").ap()
           for n, v in arrays.items()}
    out = nc.dram_tensor("out", (B, L, C), F32, kind="ExternalOutput").ap()
    tower(nc, aps, out)
    r = run_bass_kernel_spmd(nc, [{"in_" + n: v for n, v in arrays.items()}], core_ids=[0])
    return r.results[0]["out"]
```

```python
from contextlib import ExitStack

import concourse.bass as bass
from concourse import mybir

ALU = mybir.AluOpType
ACT = mybir.ActivationFunctionType
AX = mybir.AxisListType
F32 = mybir.dt.float32
BF16 = mybir.dt.bfloat16

B, C, H, DH = 128, 256, 8, 32
P = 128
CH = C // P
W4, K9 = 4, 9
KP = 3 * 14 * 14
KC = -(-KP // P)
KL = KP - (KC - 1) * P
WT = K9 * B
EC = 3
EN = WT // EC
L, DI, NS, R = 5, 512, 16, 16
DC = DI // P
NX = R + 2 * NS
GB = P // NS
NG = B // GB
E8 = 8
EPS = 1e-5
QSCALE = C ** -0.5

VC = {}
_n = 0
for _name, _w in [("q_g", 2), ("q_b", 2), ("gq_g", 2), ("gq_b", 2), ("kv_g", 2), ("kv_b", 2), ("gkv_g", 2),
                  ("gkv_b", 2), ("ln_g", 2), ("ln_b", 2), ("cls", 2), ("cb0", 4), ("cb1", 4), ("cw0", 16),
                  ("cw1", 16), ("D0", 4), ("D1", 4)]:
    VC[_name] = _n
    _n += _w
NVC = _n
VR = {"proj_b": 0, "mod_b": 256, "gproj_b": 512, "cls": 768}
NVR = 1024
KS = 12 * GB
SEG = {"q": (0, 256), "gq": (256, 256), "kv": (512, 512), "gkv": (1024, 512)}


class Chain:

    def __init__(self, eng, sem, base=0):
        self.eng, self.sem, self.base, self.n = eng, sem, base, 0

    def link(self, ins):
        ins.then_inc(self.sem, 1)
        self.n += 1
        self.eng.wait_ge(self.sem, self.base + self.n)

    def mark(self, ins):
        ins.then_inc(self.sem, 1)
        self.n += 1
        return self.n

    def upto(self, n):
        self.eng.wait_ge(self.sem, self.base + n)


def tower(nc, a, out):
    top = ExitStack()
    with top:
        def sb(name, shape, dt=F32, ctx=top):
            return ctx.enter_context(nc.sbuf_tensor(name, shape, dt))

        def sem(name):
            return top.enter_context(nc.semaphore(name))

        ps = top.enter_context(nc.psum_tensor("ps", [P, 8 * 512], F32))

        def bank(n, lo=0, hi=512, p=P):
            return ps[0:p, n * 512 + lo:n * 512 + hi]

        ident = sb("ident", [P, P])
        mhalf = sb("mhalf", [P, 16])
        cols = sb("cols", [P, NVC])
        rows = sb("rows", [P, NVR])
        inw = sb("inw", [P, 2, CH, 2 * DI])
        xpw = sb("xpw", [P, 2, DC, NX])
        dtw = sb("dtw", [33, 2, DI])
        expA = sb("expA", [P, 2, DI])
        gatew = sb("gatew", [P, CH, E8])
        hbuf = sb("hbuf", [P, L, C])
        maskb = sb("maskb", [P, GB, NS])
        sel = sb("sel", [KS, 2, P])
        selb = sb("selb", [KS, 2, P], BF16)

        def col(name, j=0, n=1):
            return cols[:, VC[name] + j:VC[name] + j + n]

        def row(name, n):
            return rows[:, VR[name]:VR[name] + n]

        dparts = nc.dram_tensor("dparts", (6, B, L * DI), BF16, kind="Internal").ap()
        uparts = nc.dram_tensor("uparts", (6, B, L * DI), BF16, kind="Internal").ap()
        bparts = nc.dram_tensor("bparts", (12, B, 2 * L * P), BF16, kind="Internal").ap()
        NY = 3 * 32 + GB
        yscr = nc.dram_tensor("yscr", (NG, 2, NY, DI), F32, kind="Internal").ap()

        tok = ExitStack()
        win = ExitStack()
        redT = sb("redT", [P, W4, CH, P], ctx=tok)
        agg = sb("agg", [P, W4, C], ctx=tok)
        wall = sb("wall", [P, CH, 1536], ctx=tok)
        brow = sb("brow", [P, 1536], ctx=tok)
        projw = sb("projw", [P, 3, CH, C], ctx=tok)
        convw = sb("convw", [P, KC, C], ctx=win)
        onesc = sb("onesc", [P, P], ctx=win)
        xbuf = sb("xbuf", [P, 2, KC, WT], ctx=win)
        peT = sb("peT", [P, 2, CH, WT], ctx=win)
        kvs = sb("kvs", [P, 2, K9, 2 * C], ctx=win)
        prod = sb("prod", [P, K9, C], ctx=win)
        redw = sb("redw", [P, 2, CH, P], ctx=win)
        st = sb("st", [P, K9 + 1, 6], ctx=win)
        mv = sb("mv", [P, K9 + 1, 2], ctx=win)
        veps = sb("veps", [P, K9 + 1], ctx=win)
        rstd = sb("rstd", [P, K9 + 1], ctx=win)
        qn = sb("qn", [P, C], ctx=win)
        qb = sb("qb", [P, H], ctx=win)
        sc = sb("sc", [P, K9, H], ctx=win)
        mx = sb("mx", [P, H], ctx=win)
        ex = sb("ex", [P, K9, H], ctx=win)
        sm = sb("sm", [P, H], ctx=win)

        s_vec, s_wall, s_conv, s_late = sem("s_vec"), sem("s_wall"), sem("s_conv"), sem("s_late")
        expA_ready = sem("expA_ready")
        s_const, s_bias, s_brow = sem("s_const"), sem("s_bias"), sem("s_brow")
        s_wg, s_wmean, s_wready = sem("s_wg"), sem("s_wmean"), sem("s_wready")
        x_landed = [[sem(f"x_landed{q}{c}") for c in range(EC)] for q in range(2)]
        emb_ready, emb_free, s_dtz = sem("emb_ready"), sem("emb_free"), sem("s_dtz")
        kv_ready, kv_free, kvs_free = sem("kv_ready"), sem("kv_free"), sem("kvs_free")
        tr_ready, tr_free = sem("tr_ready"), sem("tr_free")
        red_ready, red_kept, q_ready, q_free = sem("red_ready"), sem("red_kept"), sem("q_ready"), sem("q_free")
        veps_ready, rstd_ready, sc_ready, ex_ready = sem("veps_ready"), sem("rstd_ready"), sem("sc_ready"), sem("ex_ready")
        d_chain = sem("d_chain")

        T_EMB, T_KV, T_TR, T_Q = 0, 2, 4, 6

        with nc.Block() as block:
            @block.sync
            def _(sp):
                sp.dma_start(cols[:, :], a["vec_cols"]).then_inc(s_vec, 16)
                sp.dma_start(sel[:, :, :], a["sel"].rearrange("k (d m) -> k d m", d=2)).then_inc(s_vec, 16)
                sp.dma_start(wall[:, :, :], a["wall"].rearrange("(h p) n -> p h n", p=P)).then_inc(s_wall, 16)
                sp.dma_start(convw[:, 0:KC - 1, :], a["conv_wT"][0:(KC - 1) * P].rearrange("(k p) n -> p k n", p=P)).then_inc(s_conv, 16)
                sp.dma_start(convw[0:KL, KC - 1, :], a["conv_wT"][(KC - 1) * P:KP]).then_inc(s_conv, 16)

                def load_window(w, q):
                    for c in range(EC):
                        src = a["xT"][:, bass.ds(w * WT + c * EN, EN)]
                        sp.dma_start(xbuf[:, q, 0:KC - 1, c * EN:(c + 1) * EN],
                                     src[0:(KC - 1) * P].rearrange("(k p) n -> p k n", p=P)).then_inc(x_landed[q][c], 16)
                        sp.dma_start(xbuf[0:KL, q, KC - 1, c * EN:(c + 1) * EN],
                                     src[(KC - 1) * P:KP]).then_inc(x_landed[q][c], 16)

                load_window(0, 0)
                load_window(1, 1)
                sp.dma_start(rows[:, :], a["vec_rows"].to_broadcast([P, NVR])).then_inc(s_late, 16)
                for n, name in enumerate(["la_proj_w", "ga_proj_w", "mod_w"]):
                    sp.dma_start(projw[:, n], a[name].rearrange("(h p) n -> p h n", p=P)).then_inc(s_late, 16)
                for w in (2, 3):
                    sp.wait_ge(emb_ready, 6 * (w - 1))
                    load_window(w, w % 2)
                for d in range(2):
                    sp.dma_start(inw[:, d], a["in_wT"][d].rearrange("(h p) n -> p h n", p=P)).then_inc(s_late, 16)
                    sp.dma_start(xpw[:, d], a["xproj_wT"][d].rearrange("(c p) n -> p c n", p=P)).then_inc(s_late, 16)
                    for g in range(GB):
                        sp.dma_start(expA[g * NS:(g + 1) * NS, d], a["A_logT"][d]).then_inc(s_late, 16)
                sp.dma_start(gatew[:, :, :], a["gate_wT"].rearrange("(h p) n -> p h n", p=P)).then_inc(s_late, 16)
                sp.wait_ge(s_dtz, 1)
                for d in range(2):
                    sp.dma_start(dtw[0:R, d], a["dt_wT"][d]).then_inc(s_late, 16)
                    sp.dma_start(dtw[32:33, d], a["dt_b"][d]).then_inc(s_late, 16)
                sp.wait_ge(s_late, 16 * (4 + 2 * (2 + GB) + 1 + 4))

            @block.gpsimd
            def _(pool):
                pool.memset(dtw[:, :, :], 0.0).then_inc(s_dtz, 1)
                pool.memset(ident[:, :], 0.0).then_inc(s_const, 1)
                pool.memset(maskb[:, :, :], 0.0).then_inc(s_const, 1)
                pool.memset(mhalf[:, :], -0.5).then_inc(s_const, 1)
                pool.wait_ge(s_const, 3)
                pool.affine_select(out=ident[:, :], in_=ident[:, :], compare_op=ALU.not_equal, fill=1.0, base=0,
                                   pattern=[[-1, P]], channel_multiplier=1).then_inc(s_const, 1)
                pool.wait_ge(s_const, 4)
                for j in range(NG):
                    pool.tensor_tensor(maskb[:, :, :], maskb[:, :, :],
                                       ident[:, j * GB:(j + 1) * GB].unsqueeze(2).to_broadcast([P, GB, NS]),
                                       ALU.add).then_inc(s_const, 1)
                    pool.wait_ge(s_const, 5 + j)
                pool.wait_ge(s_vec, 32)
                pool.tensor_copy(selb[:, :, :], sel[:, :, :]).then_inc(s_const, 1)
                for w in range(W4):
                    pool.wait_ge(veps_ready, w + 1)
                    pool.tensor_tensor(rstd[:, :], veps[:, :], mhalf[:, 0:K9 + 1], ALU.pow).then_inc(rstd_ready, 1)

            @block.tensor
            def _(pe):
                pe.wait_ge(s_vec, 32)
                pe.wait_ge(s_wall, 16)
                for s, (o, n) in SEG.items():
                    for h in range(CH):
                        mm = pe.matmul(bank(o // 512, o % 512, o % 512 + n),
                                       col(s + "_b", h).to_broadcast([P, P]), wall[:, h, o:o + n],
                                       start=(h == 0), stop=(h == CH - 1))
                mm.then_inc(s_bias, 1)
                pe.wait_ge(s_wg, 8)
                for s in range(3):
                    for h in range(CH):
                        mm = pe.matmul(bank(3 + s), onesc[:, :], wall[:, h, s * 512:(s + 1) * 512],
                                       start=(h == 0), stop=(h == CH - 1))
                mm.then_inc(s_wmean, 1)
                pe.wait_ge(s_conv, 32)
                pe.wait_ge(s_brow, 1)
                pe.wait_ge(s_wready, 6)
                pe.wait_ge(s_const, 4)

                def window(i, q):
                    w = 2 * i + q
                    for c in range(EC):
                        pe.wait_ge(x_landed[q][c], 32 * i + 32)
                        for h in range(CH):
                            j = c * CH + h
                            pe.wait_ge(emb_free, 6 * w + j + 1)
                            for k in range(KC):
                                n = P if k < KC - 1 else KL
                                mm = pe.matmul(bank(T_EMB + j % 2, 0, EN), convw[0:n, k, h * P:(h + 1) * P],
                                               xbuf[0:n, q, k, c * EN:(c + 1) * EN],
                                               start=(k == 0), stop=(k == KC - 1))
                            mm.then_inc(emb_ready, 1)
                    for t in range(K9):
                        if t % EC == 0:
                            pe.wait_ge(emb_free, 2 + 6 * w + 2 * (t // EC) + 2)
                        pe.wait_ge(tr_free, 10 * w + t + 1)
                        for h in range(CH):
                            mm = pe.transpose(bank(T_TR + t % 2, h * P, (h + 1) * P),
                                              peT[:, q, h, t * B:(t + 1) * B], ident[:, :])
                        mm.then_inc(tr_ready, 1)
                        pe.wait_ge(kv_free, 9 * w + t + 1)
                        for h in range(CH):
                            mm = pe.matmul(bank(T_KV + (q + t) % 2), peT[:, q, h, t * B:(t + 1) * B],
                                           wall[:, h, 512:1024], start=(h == 0), stop=(h == CH - 1))
                        mm.then_inc(kv_ready, 1)
                    pe.wait_ge(red_ready, w + 1)
                    pe.wait_ge(tr_free, 10 * w + K9 + 1)
                    for h in range(CH):
                        mm = pe.transpose(bank(T_TR + 1, h * P, (h + 1) * P), redw[:, q, h, :], ident[:, :])
                    mm.then_inc(tr_ready, 1)
                    pe.wait_ge(q_free, w + 1)
                    for h in range(CH):
                        mm = pe.matmul(bank(T_Q, 0, C), redw[:, q, h, :], wall[:, h, 0:C],
                                       start=(h == 0), stop=(h == CH - 1))
                    mm.then_inc(q_ready, 1)

                with pe.Fori(0, W4 // 2) as i:
                    for q in range(2):
                        window(i, q)

            @block.scalar
            def _(act):
                act.wait_ge(s_bias, 1)
                act.activation(brow[:, :], ps[:, 0:1536], ACT.Copy).then_inc(s_brow, 1)
                act.sem_inc(emb_free, 2)
                act.sem_inc(kv_free, 2)
                act.sem_inc(red_kept, 2)

                def window(i, q):
                    w = 2 * i + q
                    for c in range(EC):
                        for h in range(CH):
                            j = c * CH + h
                            act.wait_ge(emb_ready, 6 * w + j + 1)
                            act.activation(peT[:, q, h, c * EN:(c + 1) * EN], bank(T_EMB + j % 2, 0, EN),
                                           ACT.Copy).then_inc(emb_free, 1)
                    act.wait_ge(kvs_free, w + 1)
                    for t in range(K9):
                        act.wait_ge(kv_ready, 9 * w + t + 1)
                        act.activation(kvs[:, q, t, :], bank(T_KV + (q + t) % 2), ACT.Copy).then_inc(kv_free, 1)
                        if t == 5:
                            act.wait_ge(red_ready, w + 1)
                            act.activation(redT[:, bass.ds(w, 1), :, :].rearrange("p o h b -> p (o h) b"),
                                           redw[:, q, :, :], ACT.Copy).then_inc(red_kept, 1)
                    act.wait_ge(sc_ready, w + 1)
                    act.activation(ex[:, :, :], sc[:, :, :], ACT.Exp, scale=QSCALE).then_inc(ex_ready, 1)

                with act.Fori(0, W4 // 2) as i:
                    for q in range(2):
                        window(i, q)

            @block.vector
            def _(dve):
                dve.memset(onesc[:, :], 1.0 / C)
                dve.wait_ge(s_bias, 1)
                for s, (o, n) in SEG.items():
                    for h in range(CH):
                        dve.tensor_scalar(wall[:, h, o:o + n], wall[:, h, o:o + n], col(s + "_g", h), None,
                                          ALU.mult).then_inc(s_wg, 1)
                dve.wait_ge(s_wg, 8)
                dve.wait_ge(s_wmean, 1)
                for s in range(3):
                    for h in range(CH):
                        dve.tensor_tensor(wall[:, h, s * 512:(s + 1) * 512], wall[:, h, s * 512:(s + 1) * 512],
                                          bank(3 + s), ALU.subtract).then_inc(s_wready, 1)
                dve.sem_inc(tr_free, 2)
                dve.sem_inc(kvs_free, 2)
                dve.sem_inc(q_free, 1)
                dve.wait_ge(s_wready, 6)
                dve.wait_ge(s_brow, 1)
                NCH = 16

                def window(i, q):
                    w = 2 * i + q
                    ch = Chain(dve, d_chain, NCH * w)
                    dve.wait_ge(emb_free, 2 + 6 * w + 6)
                    dve.wait_ge(red_kept, w + 1)
                    ch.link(dve.tensor_reduce(redw[:, q, :, :],
                                              peT[:, q, :, :].rearrange("p h (k b) -> p h b k", k=K9), AX.X, ALU.add))
                    dve.tensor_scalar(redw[:, q, :, :], redw[:, q, :, :], 1.0 / K9, None,
                                      ALU.mult).then_inc(red_ready, 1)
                    for t in range(K9 + 1):
                        dve.wait_ge(tr_ready, 10 * w + t + 1)
                        dve.bn_stats(st[:, t, :], bank(T_TR + t % 2, 0, C)).then_inc(tr_free, 1)
                    dve.wait_ge(tr_free, 2 + 10 * (w + 1))
                    dve.memset(sm[:, :], 0.0)
                    for t in range(K9):
                        dve.bn_aggr(mv[:, t, :], st[:, t, :])
                    ch.link(dve.bn_aggr(mv[:, K9, :], st[:, K9, :]))
                    dve.tensor_scalar(veps[:, :], mv[:, :, 1], EPS, None, ALU.add).then_inc(veps_ready, 1)
                    dve.wait_ge(rstd_ready, w + 1)
                    dve.wait_ge(q_ready, w + 1)
                    dve.scalar_tensor_tensor(out=qn[:, :], in0=bank(T_Q, 0, C), scalar=rstd[:, K9:K9 + 1],
                                             in1=brow[:, 0:C], op0=ALU.mult, op1=ALU.add).then_inc(q_free, 1)
                    dve.wait_ge(q_free, w + 2)
                    dve.wait_ge(kv_free, 2 + 9 * w + 9)
                    ch.link(dve.tensor_tensor(prod[:, 0, :], qn[:, :], brow[:, 512:512 + C], ALU.mult))
                    ch.link(dve.tensor_reduce(qb[:, :], prod[:, 0, :].rearrange("p (h d) -> p h d", h=H), AX.X, ALU.add))
                    ch.link(dve.tensor_tensor(prod[:, :, :], kvs[:, q, :, 0:C],
                                              qn[:, :].unsqueeze(1).to_broadcast([P, K9, C]), ALU.mult))
                    ch.link(dve.tensor_reduce(sc[:, :, :].rearrange("p k h -> p (k h)"),
                                              prod[:, :, :].rearrange("p k (h d) -> p (k h) d", h=H), AX.X, ALU.add))
                    rk = rstd[:, 0:K9].unsqueeze(2).to_broadcast([P, K9, H])
                    ch.link(dve.tensor_tensor(sc[:, :, :], sc[:, :, :], rk, ALU.mult))
                    ch.link(dve.tensor_tensor(sc[:, :, :], sc[:, :, :],
                                              qb[:, :].unsqueeze(1).to_broadcast([P, K9, H]), ALU.add))
                    ch.link(dve.tensor_reduce(mx[:, :], sc[:, :, :].rearrange("p k h -> p h k"), AX.X, ALU.max))
                    dve.tensor_tensor(sc[:, :, :], sc[:, :, :], mx[:, :].unsqueeze(1).to_broadcast([P, K9, H]),
                                      ALU.subtract).then_inc(sc_ready, 1)
                    dve.wait_ge(ex_ready, w + 1)
                    ch.link(dve.tensor_reduce(sm[:, :], ex[:, :, :].rearrange("p k h -> p h k"), AX.X, ALU.add))
                    ch.link(dve.reciprocal(sm[:, :], sm[:, :]))
                    ch.link(dve.tensor_tensor(ex[:, :, :], ex[:, :, :],
                                              sm[:, :].unsqueeze(1).to_broadcast([P, K9, H]), ALU.mult))
                    ch.link(dve.tensor_tensor(ex[:, :, :], ex[:, :, :], rk, ALU.mult))
                    ch.link(dve.tensor_tensor(prod[:, :, :].rearrange("p k (h d) -> p (k h) d", h=H),
                                              kvs[:, q, :, C:2 * C].rearrange("p k (h d) -> p k h d", h=H),
                                              ex[:, :, :].unsqueeze(3).to_broadcast([P, K9, H, DH]), ALU.mult))
                    dve.sem_inc(kvs_free, 1)
                    ch.link(dve.tensor_reduce(qn[:, :], prod[:, :, :].rearrange("p k c -> p c k"), AX.X, ALU.add))
                    ch.link(dve.tensor_tensor(agg[:, bass.ds(w, 1), :].rearrange("p o c -> p (o c)"), qn[:, :],
                                              brow[:, 512 + C:1024], ALU.add))
                    assert ch.n == NCH

                with dve.Fori(0, W4 // 2) as i:
                    for q in range(2):
                        window(i, q)
        win.close()

        glo = ExitStack()
        lo = sb("lo", [P, W4, C], ctx=glo)
        gkvs = sb("gkvs", [P, W4, 2 * C], ctx=glo)
        aggT = sb("aggT", [P, 2, CH, P], ctx=glo)
        loT = sb("loT", [P, 2, CH, P], ctx=glo)
        gaT = sb("gaT", [P, CH, P], ctx=glo)
        gst = sb("gst", [P, W4 + 1, 6], ctx=glo)
        gmv = sb("gmv", [P, W4 + 1, 2], ctx=glo)
        gve = sb("gve", [P, W4 + 1], ctx=glo)
        grs = sb("grs", [P, W4 + 1], ctx=glo)
        gqn = sb("gqn", [P, C], ctx=glo)
        gqraw = sb("gqraw", [P, C], ctx=glo)
        gpr = sb("gpr", [P, W4, C], ctx=glo)
        gqb = sb("gqb", [P, H], ctx=glo)
        gsc = sb("gsc", [P, W4, H], ctx=glo)
        gmx = sb("gmx", [P, H], ctx=glo)
        gex = sb("gex", [P, W4, H], ctx=glo)
        gag = sb("gag", [P, C], ctx=glo)
        aT_ready, aT_copied = sem("aT_ready"), sem("aT_copied")
        lo_summed, lo_ready, lT_ready, lT_copied = sem("lo_summed"), sem("lo_ready"), sem("lT_ready"), sem("lT_copied")
        gkv_ready, gkv_copied, mod_ready, mod_copied = sem("gkv_ready"), sem("gkv_copied"), sem("mod_ready"), sem("mod_copied")
        gq_ready, gq_read, gve_ready, grs_ready = sem("gq_ready"), sem("gq_read"), sem("gve_ready"), sem("grs_ready")
        gsc_ready, gex_ready, gag_ready, gaT_ready = sem("gsc_ready"), sem("gex_ready"), sem("gag_ready"), sem("gaT_ready")
        gaT_copied, cls_ready, g_chain = sem("gaT_copied"), sem("cls_ready"), sem("g_chain")

        with nc.Block() as block:
            @block.tensor
            def _(pe):
                for h in range(CH):
                    mm = pe.matmul(bank(6, 0, C), col("cls", h).to_broadcast([P, P]), wall[:, h, C:2 * C],
                                   start=(h == 0), stop=(h == CH - 1))
                mm.then_inc(gq_ready, 1)

                def agg_turned(w):
                    if w >= 2:
                        pe.wait_ge(aT_copied, w - 1)
                    for h in range(CH):
                        mm = pe.transpose(bank(w % 2, h * P, (h + 1) * P), agg[:, w, h * P:(h + 1) * P], ident[:, :])
                    mm.then_inc(aT_ready, 1)

                def local_out(w):
                    pe.wait_ge(aT_copied, w + 1)
                    if w >= 2:
                        pe.wait_ge(lo_ready, w - 1)
                    for h in range(CH):
                        pe.matmul(bank(2 + w % 2, 0, C), aggT[:, w % 2, h, :], projw[:, 0, h, :],
                                  start=(h == 0), stop=False, skip_group_check=True)
                    for h in range(CH):
                        mm = pe.matmul(bank(2 + w % 2, h * P, (h + 1) * P), redT[:, w, h, :], ident[:, :],
                                       start=False, stop=(h == CH - 1), skip_group_check=True)
                    mm.then_inc(lo_summed, 1)

                def lo_turned(w):
                    pe.wait_ge(lo_ready, w + 1)
                    if w >= 2:
                        pe.wait_ge(lT_copied, w - 1)
                    for h in range(CH):
                        mm = pe.transpose(bank(4 + w % 2, h * P, (h + 1) * P), lo[:, w, h * P:(h + 1) * P], ident[:, :])
                    mm.then_inc(lT_ready, 1)

                def projections(w):
                    pe.wait_ge(lT_copied, w + 1)
                    if w == 0:
                        pe.wait_ge(gq_read, 1)
                    else:
                        pe.wait_ge(gkv_copied, w)
                    for h in range(CH):
                        mm = pe.matmul(bank(6), loT[:, w % 2, h, :], wall[:, h, 1024:1536],
                                       start=(h == 0), stop=(h == CH - 1))
                    mm.then_inc(gkv_ready, 1)
                    if w >= 1:
                        pe.wait_ge(mod_copied, w)
                    for h in range(CH):
                        mm = pe.matmul(bank(7, 0, C), loT[:, w % 2, h, :], projw[:, 2, h, :],
                                       start=(h == 0), stop=(h == CH - 1))
                    mm.then_inc(mod_ready, 1)

                for n in range(W4 + 3):
                    if n < W4:
                        agg_turned(n)
                    if 1 <= n <= W4:
                        local_out(n - 1)
                    if 2 <= n <= W4 + 1:
                        lo_turned(n - 2)
                    if n >= 3:
                        projections(n - 3)
                pe.wait_ge(gag_ready, 1)
                for h in range(CH):
                    mm = pe.transpose(bank(0, h * P, (h + 1) * P), gag[:, h * P:(h + 1) * P], ident[:, :])
                mm.then_inc(gaT_ready, 1)
                pe.wait_ge(gaT_copied, 1)
                for h in range(CH):
                    mm = pe.matmul(bank(2, 0, C), gaT[:, h, :], projw[:, 1, h, :], start=(h == 0), stop=(h == CH - 1))
                mm.then_inc(cls_ready, 1)

            @block.scalar
            def _(act):
                act.wait_ge(gq_ready, 1)
                act.activation(gqraw[:, :], bank(6, 0, C), ACT.Copy).then_inc(gq_read, 1)

                def turned(w):
                    act.wait_ge(aT_ready, w + 1)
                    if w >= 2:
                        act.wait_ge(lo_summed, w - 1)
                    act.activation(aggT[:, w % 2, :, :], bank(w % 2, 0, C), ACT.Copy).then_inc(aT_copied, 1)

                def lo_copied(w):
                    act.wait_ge(lT_ready, w + 1)
                    if w >= 2:
                        act.wait_ge(mod_ready, w - 1)
                    act.activation(loT[:, w % 2, :, :], bank(4 + w % 2, 0, C), ACT.Copy).then_inc(lT_copied, 1)

                def kv_copied(w):
                    act.wait_ge(gkv_ready, w + 1)
                    act.activation(gkvs[:, w, :], bank(6), ACT.Copy).then_inc(gkv_copied, 1)

                for n in range(W4 + 3):
                    if n < W4:
                        turned(n)
                    if 2 <= n <= W4 + 1:
                        lo_copied(n - 2)
                    if n >= 3:
                        kv_copied(n - 3)
                act.wait_ge(gsc_ready, 1)
                act.activation(gex[:, :, :], gsc[:, :, :], ACT.Exp, scale=QSCALE).then_inc(gex_ready, 1)
                act.wait_ge(gaT_ready, 1)
                act.activation(gaT[:, :, :], bank(0, 0, C), ACT.Copy).then_inc(gaT_copied, 1)

            @block.gpsimd
            def _(pool):
                pool.wait_ge(gve_ready, 1)
                pool.tensor_tensor(grs[:, :], gve[:, :], mhalf[:, 0:W4 + 1], ALU.pow).then_inc(grs_ready, 1)

            @block.vector
            def _(dve):
                ch = Chain(dve, g_chain)
                ch.link(dve.bn_stats(gst[:, W4, :], row("cls", C)))
                for w in range(W4 + 1):
                    if w < W4:
                        dve.wait_ge(lo_summed, w + 1)
                        dve.tensor_tensor(lo[:, w, :], bank(2 + w % 2, 0, C), row("proj_b", C), ALU.add).then_inc(lo_ready, 1)
                        dve.wait_ge(lo_ready, w + 1)
                        ch.link(dve.bn_stats(gst[:, w, :], lo[:, w, :]))
                    ch.link(dve.bn_aggr(gmv[:, w, :], gst[:, w, :]))
                dve.tensor_scalar(gve[:, :], gmv[:, :, 1], EPS, None, ALU.add).then_inc(gve_ready, 1)
                for w in range(W4):
                    dve.wait_ge(mod_ready, w + 1)
                    dve.tensor_tensor(hbuf[:, w, :], bank(7, 0, C), row("mod_b", C), ALU.add).then_inc(mod_copied, 1)
                dve.wait_ge(gq_read, 1)
                dve.wait_ge(grs_ready, 1)
                ch.link(dve.scalar_tensor_tensor(out=gqn[:, :], in0=gqraw[:, :], scalar=grs[:, W4:W4 + 1],
                                                 in1=brow[:, C:2 * C], op0=ALU.mult, op1=ALU.add))
                dve.wait_ge(gkv_copied, W4)
                ch.link(dve.tensor_tensor(gpr[:, 0, :], gqn[:, :], brow[:, 1024:1024 + C], ALU.mult))
                ch.link(dve.tensor_reduce(gqb[:, :], gpr[:, 0, :].rearrange("p (h d) -> p h d", h=H), AX.X, ALU.add))
                ch.link(dve.tensor_tensor(gpr[:, :, :], gkvs[:, :, 0:C],
                                          gqn[:, :].unsqueeze(1).to_broadcast([P, W4, C]), ALU.mult))
                ch.link(dve.tensor_reduce(gsc[:, :, :].rearrange("p k h -> p (k h)"),
                                          gpr[:, :, :].rearrange("p k (h d) -> p (k h) d", h=H), AX.X, ALU.add))
                rk = grs[:, 0:W4].unsqueeze(2).to_broadcast([P, W4, H])
                ch.link(dve.tensor_tensor(gsc[:, :, :], gsc[:, :, :], rk, ALU.mult))
                ch.link(dve.tensor_tensor(gsc[:, :, :], gsc[:, :, :], gqb[:, :].unsqueeze(1).to_broadcast([P, W4, H]), ALU.add))
                ch.link(dve.tensor_reduce(gmx[:, :], gsc[:, :, :].rearrange("p k h -> p h k"), AX.X, ALU.max))
                dve.tensor_tensor(gsc[:, :, :], gsc[:, :, :], gmx[:, :].unsqueeze(1).to_broadcast([P, W4, H]),
                                  ALU.subtract).then_inc(gsc_ready, 1)
                dve.wait_ge(gex_ready, 1)
                ch.link(dve.tensor_reduce(gmx[:, :], gex[:, :, :].rearrange("p k h -> p h k"), AX.X, ALU.add))
                ch.link(dve.reciprocal(gmx[:, :], gmx[:, :]))
                ch.link(dve.tensor_tensor(gex[:, :, :], gex[:, :, :], gmx[:, :].unsqueeze(1).to_broadcast([P, W4, H]), ALU.mult))
                ch.link(dve.tensor_tensor(gex[:, :, :], gex[:, :, :], rk, ALU.mult))
                ch.link(dve.tensor_tensor(gpr[:, :, :].rearrange("p k (h d) -> p (k h) d", h=H),
                                          gkvs[:, :, C:2 * C].rearrange("p k (h d) -> p k h d", h=H),
                                          gex[:, :, :].unsqueeze(3).to_broadcast([P, W4, H, DH]), ALU.mult))
                ch.link(dve.tensor_reduce(gqn[:, :], gpr[:, :, :].rearrange("p k c -> p c k"), AX.X, ALU.add))
                dve.tensor_tensor(gag[:, :], gqn[:, :], brow[:, 1024 + C:1536], ALU.add).then_inc(gag_ready, 1)
                ch.link(dve.tensor_tensor(gqraw[:, :], row("gproj_b", C), row("cls", C), ALU.add))
                dve.wait_ge(cls_ready, 1)
                ch.link(dve.tensor_tensor(hbuf[:, W4, :], bank(2, 0, C), gqraw[:, :], ALU.add))
        glo.close()
        tok.close()

        siluz = sb("siluz", [P, 2, L, DI])
        skip = sb("skip", [P, 2, L, DI])
        CT = sb("CT", [P, 2, L, B])
        pre = ExitStack()
        xn = sb("xn", [P, L, C], ctx=pre)
        xnT = sb("xnT", [P, CH, L * B], ctx=pre)
        xcT = sb("xcT", [P, 2, DC, L * B], ctx=pre)
        acc = sb("acc", [P, 2, L * B], ctx=pre)
        dbl = sb("dbl", [NX, 2, L * B], ctx=pre)
        dtT = sb("dtT", [33, 2, L * B], ctx=pre)
        bct = sb("bct", [P, 2, L, NX], ctx=pre)
        cbp = sb("cbp", [P, L, NS], ctx=pre)
        cb = sb("cb", [P, 2, L], ctx=pre)
        bd = sb("bd", [P, L, GB, NS], ctx=pre)
        cd = sb("cd", [P, L, GB, NS], ctx=pre)
        bhi = sb("bhi", [P, L * P], BF16, ctx=pre)
        bmi = sb("bmi", [P, L * P], BF16, ctx=pre)
        blo = sb("blo", [P, L * P], BF16, ctx=pre)
        xst = sb("xst", [P, L, 6], ctx=pre)
        xmv = sb("xmv", [P, L, 2], ctx=pre)
        xv = sb("xv", [P, L], ctx=pre)
        xr = sb("xr", [P, L], ctx=pre)
        diagD = sb("diagD", [P, 2, DC, P], ctx=pre)
        NDV = 5
        NR = 3
        NZ = 7
        ez = sb("ez", [P, NZ, DI], ctx=pre)
        rc = sb("rc", [P, NZ, DI], ctx=pre)
        delta = sb("delta", [P, 2, DI], ctx=pre)
        dres = sb("dres", [P, 2, DI], ctx=pre)
        uu = sb("uu", [P, 2, DI], ctx=pre)
        ures = sb("ures", [P, 2, DI], ctx=pre)
        dpt = sb("dpt", [P, NR, 3, DI], BF16, ctx=pre)
        upt = sb("upt", [P, NR, 3, DI], BF16, ctx=pre)
        bz = sb("bz", [P, L * P], BF16, ctx=pre)
        bz_ready = sem("bz_ready")
        xv_ready, xr_ready, diag_ready = sem("xv_ready"), sem("xr_ready"), sem("diag_ready")
        xn_ready, xnT_ready, xnT_copied, x_chain = sem("xn_ready"), sem("xnT_ready"), sem("xnT_copied"), sem("x_chain")
        xi_ready, acc_begun, acc_ready, xc_ready = sem("xi_ready"), sem("acc_begun"), sem("acc_ready"), sem("xc_ready")
        z_ready, z_copied, dbl_ready, dbl_copied = sem("z_ready"), sem("z_copied"), sem("dbl_ready"), sem("dbl_copied")
        dtT_zero, dtT_ones, bc_ready, bct_ready = sem("dtT_zero"), sem("dtT_ones"), sem("bc_ready"), sem("bct_ready")
        cd_ready, cdT_ready, CT_ready = sem("cd_ready"), sem("cdT_ready"), sem("CT_ready")
        bd_ready, bhi_ready, bres_ready, bmi_ready = sem("bd_ready"), sem("bhi_ready"), sem("bres_ready"), sem("bmi_ready")
        blo_ready, b_stored = sem("blo_ready"), sem("b_stored")
        dp_ready, xt_ready, ab_done, ez_ready, ln_ready = sem("dp_ready"), sem("xt_ready"), sem("ab_done"), sem("ez_ready"), sem("ln_ready")
        rc_ready, delta_ready, u_ready, skip_ready = sem("rc_ready"), sem("delta_ready"), sem("u_ready"), sem("skip_ready")
        dres_ready, dhi_ready, dmi_ready, uhi_ready = sem("dres_ready"), sem("dhi_ready"), sem("dmi_ready"), sem("uhi_ready")
        umi_ready, ures_ready, dlo_ready, ulo_ready = sem("umi_ready"), sem("ures_ready"), sem("dlo_ready"), sem("ulo_ready")
        p_stored = [sem(f"p_stored{r}") for r in range(NR)]
        ITEMS = [(d, t) for d in range(2) for t in range(L)]
        NI = len(ITEMS)
        WIDE = [("xi", 0, 0), ("xi", 1, 1), ("xi", 2, 2), ("xi", 3, 0), ("xi", 4, 1), ("xi", 5, 0), ("xp", 0, 2),
                ("xi", 6, 1), ("xi", 7, 2), ("bc", 0, 0), ("z", 0, 1), ("z", 1, 0), ("z", 2, 1), ("xp", 1, 1),
                ("cd", 0, 0), ("bc", 1, 1), ("xt", 0, 0), ("xt", 1, 1), ("xt", 2, 0), ("xt", 3, 1), ("xt", 4, 0),
                ("dp", 9, 2), ("dp", 9, 3), ("xt", 5, 2), ("cd", 1, 1), ("xt", 6, 0), ("z", 3, 3), ("xt", 7, 2),
                ("z", 4, 1), ("xt", 8, 0), ("z", 5, 3), ("xt", 9, 2), ("z", 6, 1), ("z", 7, 3), ("z", 8, 1), ("z", 9, 3)]

        def place(kind, n):
            return [w[:2] for w in WIDE].index((kind, n))

        def slot(kind, n):
            return 1024 * WIDE[place(kind, n)][2]

        with nc.Block() as block:
            @block.tensor
            def _(pe):
                for t in range(L):
                    pe.wait_ge(xn_ready, t + 1)
                    for h in range(CH):
                        mm = pe.transpose(ps[:, h * 1024 + t * B:h * 1024 + (t + 1) * B], xn[:, t, h * P:(h + 1) * P],
                                          ident[:, :])
                mm.then_inc(xnT_ready, 1)
                pe.wait_ge(xnT_copied, CH)

                def xi(n, o):
                    d, c = divmod(n, DC)
                    for lo_, hi_ in ((0, 512), (512, L * B)):
                        for h in range(CH):
                            mm = pe.matmul(ps[:, o + lo_:o + hi_], inw[:, d, h, c * P:(c + 1) * P],
                                           xnT[:, h, lo_:hi_], start=(h == 0), stop=(h == CH - 1))
                    mm.then_inc(xi_ready, 1)

                def z(n, o):
                    d, t = ITEMS[n]
                    for h in range(CH):
                        mm = pe.matmul(ps[:, o:o + DI], xnT[:, h, t * B:(t + 1) * B], inw[:, d, h, DI:2 * DI],
                                       start=(h == 0), stop=(h == CH - 1))
                    mm.then_inc(z_ready, 1)

                def xp(d, o):
                    pe.wait_ge(xc_ready, (d + 1) * DC)
                    for lo_, hi_ in ((0, 512), (512, L * B)):
                        for c in range(DC):
                            mm = pe.matmul(ps[0:NX, o + lo_:o + hi_], xpw[:, d, c, :], xcT[:, d, c, lo_:hi_],
                                           start=(c == 0), stop=(c == DC - 1))
                    mm.then_inc(dbl_ready, 1)

                def bc(d, o):
                    pe.wait_ge(dbl_copied, 2 * d + 1)
                    for t in range(L):
                        mm = pe.transpose(ps[:, o + t * NX:o + (t + 1) * NX], dbl[:, d, t * B:(t + 1) * B],
                                          ident[0:NX, 0:NX])
                    mm.then_inc(bc_ready, 1)

                def cd_(d, o):
                    pe.wait_ge(cd_ready, d + 1)
                    for t in range(L):
                        mm = pe.transpose(ps[:, o + t * P:o + (t + 1) * P], cd[:, t, :, :].rearrange("p g n -> p (g n)"),
                                          ident[:, :])
                    mm.then_inc(cdT_ready, 1)

                def xt(n, o):
                    d, t = ITEMS[n]
                    if n == 0:
                        pe.wait_ge(diag_ready, 2 * DC)
                    for c in range(DC):
                        pe.transpose(ps[:, o + c * P:o + (c + 1) * P], xcT[:, d, c, t * B:(t + 1) * B], ident[:, :])
                    for c in range(DC):
                        mm = pe.matmul(ps[:, o + DI + c * P:o + DI + (c + 1) * P], xcT[:, d, c, t * B:(t + 1) * B],
                                       diagD[:, d, c, :], start=True, stop=True)
                    mm.then_inc(xt_ready, 1)

                make = {"xi": xi, "z": z, "xp": xp, "bc": bc, "cd": cd_, "xt": xt}
                read = {"xi": (acc_ready, 1), "z": (z_copied, 1), "xp": (dbl_copied, 2), "bc": (bct_ready, 1),
                        "cd": (CT_ready, 1), "xt": (skip_ready, 1), "dp": (rc_ready, 1)}

                def tenant_read(s_, k):
                    before = [w for w in WIDE[:k] if w[2] == s_]
                    if before:
                        kind, m, _ = before[-1]
                        pe.wait_ge(read[kind][0], read[kind][1] * (m + 1))

                def wide(kind, n):
                    k = place(kind, n)
                    tenant_read(WIDE[k][2], k)
                    make[kind](n, slot(kind, n))

                def dt_product(n):
                    d, t = ITEMS[n]
                    if n == 0:
                        pe.wait_ge(dtT_ones, 1)
                        tenant_read(2, place("xp", 1))
                    pe.wait_ge(dbl_copied, 2 * d + 2)
                    if n >= 4:
                        pe.wait_ge(rc_ready, n - 3)
                    mm = pe.matmul(bank(4 + n % 4), dtT[:, d, t * B:(t + 1) * B], dtw[:, d, :], start=True, stop=True)
                    mm.then_inc(dp_ready, 1)

                for w in WIDE[:place("xp", 1)]:
                    wide(*w[:2])
                for n in range(4):
                    dt_product(n)
                wide("xp", 1)
                wide("cd", 0)
                dt_product(4)
                wide("bc", 1)
                wide("xt", 0)
                for n in range(5, 9):
                    dt_product(n)
                wide("xt", 1)
                wide("xt", 2)
                dt_product(9)
                for w in WIDE[place("xt", 3):]:
                    if w[0] != "dp":
                        wide(*w[:2])

            @block.scalar
            def _(act):
                for d in range(2):
                    for c in range(DC):
                        act.activation(diagD[:, d, c, :], ident[:, :], ACT.Identity, scale=col(f"D{d}", c)).then_inc(diag_ready, 1)
                act.wait_ge(xnT_ready, 1)
                for h in range(CH):
                    act.activation(xnT[:, h, :], ps[:, h * 1024:h * 1024 + L * B], ACT.Identity,
                                   scale=col("ln_g", h), bias=col("ln_b", h)).then_inc(xnT_copied, 1)

                def conv_begin(n):
                    d, c = divmod(n, DC)
                    o = slot("xi", n)
                    act.wait_ge(xi_ready, n + 1)
                    if n >= 2:
                        act.wait_ge(xc_ready, n - 1)
                    act.activation(acc[:, n % 2, :], ps[:, o:o + L * B], ACT.Identity,
                                   scale=col(f"cw{d}", 4 * c + 3), bias=col(f"cb{d}", c)).then_inc(acc_begun, 1)

                def conv_end(n):
                    d, c = divmod(n, DC)
                    act.wait_ge(acc_ready, n + 1)
                    act.activation(xcT[:, d, c, :], acc[:, n % 2, :], ACT.Silu).then_inc(xc_ready, 1)

                def silu_z(n):
                    act.wait_ge(z_ready, n + 1)
                    o = slot("z", n)
                    act.activation(siluz[:, ITEMS[n][0], ITEMS[n][1], :], ps[:, o:o + DI], ACT.Silu).then_inc(z_copied, 1)

                def copy_xp(d):
                    act.wait_ge(dbl_ready, d + 1)
                    o = slot("xp", d)
                    act.activation(dbl[:, d, :], ps[0:NX, o:o + L * B], ACT.Copy).then_inc(dbl_copied, 1)
                    if d == 0:
                        act.wait_ge(dtT_ones, 1)
                    act.activation(dtT[0:R, d, :], ps[0:R, o:o + L * B], ACT.Copy).then_inc(dbl_copied, 1)

                def copy_bc(d):
                    act.wait_ge(bc_ready, d + 1)
                    o = slot("bc", d)
                    act.activation(bct[:, d, :, :].rearrange("p t n -> p (t n)"), ps[:, o:o + L * NX],
                                   ACT.Copy).then_inc(bct_ready, 1)

                def copy_cd(d):
                    act.wait_ge(cdT_ready, d + 1)
                    o = slot("cd", d)
                    act.activation(CT[:, d, :, :], ps[:, o:o + L * B], ACT.Copy).then_inc(CT_ready, 1)

                flat = bd[:, :, :, :].rearrange("p t g n -> p (t g n)")

                def b_high(d):
                    act.wait_ge(bd_ready, d + 1)
                    if d == 1:
                        act.wait_ge(b_stored, 128)
                    act.activation(bhi[:, :], flat, ACT.Copy).then_inc(bhi_ready, 1)

                def b_middle(d):
                    act.wait_ge(bres_ready, d + 1)
                    act.activation(bmi[:, :], flat, ACT.Copy).then_inc(bmi_ready, 1)

                def absolute(n):
                    act.wait_ge(dp_ready, n + 1)
                    if n >= NZ:
                        act.wait_ge(delta_ready, n - NZ + 1)
                    act.activation(ez[:, n % NZ, :], bank(4 + n % 4), ACT.Abs).then_inc(ab_done, 1)

                def exponential(n):
                    act.wait_ge(ab_done, n + 1)
                    act.activation(ez[:, n % NZ, :], ez[:, n % NZ, :], ACT.Exp, scale=-1.0).then_inc(ez_ready, 1)

                def logarithm(n):
                    act.wait_ge(rc_ready, n + 1)
                    act.activation(ez[:, n % NZ, :], ez[:, n % NZ, :], ACT.Ln, bias=1.0).then_inc(ln_ready, 1)

                def delta_high(n):
                    act.wait_ge(delta_ready, n + 1)
                    if n >= NR:
                        act.wait_ge(p_stored[n % NR], 32 * (n // NR))
                    act.activation(dpt[:, n % NR, 0, :], delta[:, n % 2, :], ACT.Copy).then_inc(dhi_ready, 1)

                def u_high(n):
                    act.wait_ge(u_ready, n + 1)
                    act.activation(upt[:, n % NR, 0, :], uu[:, n % 2, :], ACT.Copy).then_inc(uhi_ready, 1)

                def middle(n):
                    q, r = n % 2, n % NR
                    act.wait_ge(dres_ready, n + 1)
                    act.activation(dpt[:, r, 1, :], dres[:, q, :], ACT.Copy).then_inc(dmi_ready, 1)
                    act.wait_ge(ures_ready, n + 1)
                    act.activation(upt[:, r, 1, :], ures[:, q, :], ACT.Copy).then_inc(umi_ready, 1)

                conv_begin(0)
                conv_begin(1)
                conv_end(0)
                conv_begin(2)
                conv_end(1)
                conv_begin(3)
                conv_end(2)
                conv_begin(4)
                conv_end(3)
                conv_begin(5)
                copy_xp(0)
                conv_end(4)
                conv_begin(6)
                conv_end(5)
                conv_begin(7)
                conv_end(6)
                copy_bc(0)
                silu_z(0)
                conv_end(7)
                silu_z(1)
                silu_z(2)
                act.activation(expA[:, :, :], expA[:, :, :], ACT.Exp).then_inc(expA_ready, 1)
                for n in range(4):
                    absolute(n)
                    exponential(n)
                b_high(0)
                copy_cd(0)
                copy_xp(1)
                absolute(4)
                exponential(4)
                copy_bc(1)
                for n in range(5):
                    logarithm(n)
                delta_high(0)
                for n in range(5):
                    absolute(n + 5)
                    u_high(n)
                    exponential(n + 5)
                    if n < 4:
                        delta_high(n + 1)
                    middle(n)
                    if n == 0:
                        b_middle(0)
                    if n == 3:
                        b_high(1)
                for n in range(5, NI):
                    logarithm(n)
                delta_high(5)
                copy_cd(1)
                b_middle(1)
                for n in range(5, NI):
                    u_high(n)
                    if n < NI - 1:
                        delta_high(n + 1)
                    if n > 5:
                        silu_z(n - 3)
                    middle(n)
                for n in range(7, NI):
                    silu_z(n)

            @block.gpsimd
            def _(pool):
                pool.memset(bz[:, :], 0.0).then_inc(bz_ready, 1)
                pool.memset(dtT[:, :, :], 0.0).then_inc(dtT_zero, 1)
                pool.wait_ge(dtT_zero, 1)
                pool.memset(dtT[32:33, :, :], 1.0).then_inc(dtT_ones, 1)
                pool.wait_ge(dtT_ones, 1)
                pool.wait_ge(xv_ready, 1)
                pool.tensor_tensor(xr[:, :], xv[:, :], mhalf[:, 0:L], ALU.pow).then_inc(xr_ready, 1)
                mask4 = maskb[:, :, :].unsqueeze(1).to_broadcast([P, L, GB, NS])
                flat = bd[:, :, :, :].rearrange("p t g n -> p (t g n)")

                def spread(d):
                    pool.wait_ge(bct_ready, d + 1)
                    if d == 1:
                        pool.wait_ge(blo_ready, 1)
                        pool.wait_ge(cdT_ready, 1)
                    pool.tensor_tensor(bd[:, :, :, :], bct[:, d, :, R:R + NS].unsqueeze(2).to_broadcast([P, L, GB, NS]),
                                       mask4, ALU.mult).then_inc(bd_ready, 1)
                    pool.tensor_tensor(cd[:, :, :, :], bct[:, d, :, R + NS:NX].unsqueeze(2).to_broadcast([P, L, GB, NS]),
                                       mask4, ALU.mult).then_inc(cd_ready, 1)

                def b_rest(d):
                    pool.wait_ge(bhi_ready, d + 1)
                    pool.wait_ge(bd_ready, d + 1)
                    pool.tensor_tensor(flat, flat, bhi[:, :], ALU.subtract).then_inc(bres_ready, 1)

                def b_low(d):
                    pool.wait_ge(bmi_ready, d + 1)
                    pool.wait_ge(bres_ready, d + 1)
                    pool.tensor_tensor(blo[:, :], flat, bmi[:, :], ALU.subtract).then_inc(blo_ready, 1)

                def rest(n):
                    q, r = n % 2, n % NR
                    pool.wait_ge(uhi_ready, n + 1)
                    if n >= 2:
                        pool.wait_ge(umi_ready, n - 1)
                        pool.wait_ge(ulo_ready, n - 1)
                    pool.tensor_tensor(ures[:, q, :], uu[:, q, :], upt[:, r, 0, :], ALU.subtract).then_inc(ures_ready, 1)

                def low(n):
                    q, r = n % 2, n % NR
                    pool.wait_ge(dmi_ready, n + 1)
                    pool.tensor_tensor(dpt[:, r, 2, :], dres[:, q, :], dpt[:, r, 1, :], ALU.subtract).then_inc(dlo_ready, 1)
                    if n < NDV:
                        pool.wait_ge(umi_ready, n + 1)
                        pool.wait_ge(ures_ready, n + 1)
                        pool.tensor_tensor(upt[:, r, 2, :], ures[:, q, :], upt[:, r, 1, :], ALU.subtract).then_inc(ulo_ready, 1)

                spread(0)
                b_rest(0)
                for n in range(NI):
                    rest(n)
                    low(n)
                    if n == 1:
                        b_low(0)
                    if n == 2:
                        spread(1)
                    if n == 4:
                        b_rest(1)
                    if n == 5:
                        b_low(1)

            @block.vector
            def _(dve):
                ch = Chain(dve, x_chain)
                marks = [ch.mark(dve.bn_stats(xst[:, t, :], hbuf[:, t, :])) for t in range(L)]
                for t in range(L):
                    ch.upto(marks[t])
                    last = ch.mark(dve.bn_aggr(xmv[:, t, :], xst[:, t, :]))
                ch.upto(last)
                dve.tensor_scalar(xv[:, :], xmv[:, :, 1], 1.0 + EPS, EPS * EPS, ALU.mult, ALU.add).then_inc(xv_ready, 1)
                dve.wait_ge(xr_ready, 1)
                for t in range(L):
                    dve.tensor_scalar(xn[:, t, :], hbuf[:, t, :], xmv[:, t, 0:1], xr[:, t:t + 1], ALU.subtract,
                                      ALU.mult).then_inc(xn_ready, 1)
                for n in range(2 * DC):
                    d, c = divmod(n, DC)
                    dve.wait_ge(acc_begun, n + 1)
                    for back in range(1, 4):
                        m = (L - back) * B
                        o = back * B
                        at = slot("xi", n) + (0 if d == 0 else o)
                        dst = acc[:, n % 2, (o if d == 0 else 0):(o if d == 0 else 0) + m]
                        ins = dve.scalar_tensor_tensor(out=dst, in0=ps[:, at:at + m], scalar=col(f"cw{d}", 4 * c + 3 - back),
                                                       in1=dst, op0=ALU.mult, op1=ALU.add)
                        if back < 3:
                            ch.link(ins)
                        else:
                            ins.then_inc(acc_ready, 1)

                def c_dot_b(d):
                    dve.wait_ge(bct_ready, d + 1)
                    ch.link(dve.tensor_tensor(cbp[:, :, :], bct[:, d, :, R:R + NS], bct[:, d, :, R + NS:NX], ALU.mult))
                    return ch.mark(dve.tensor_reduce(cb[:, d, :], cbp[:, :, :], AX.X, ALU.add))

                def lost_1(n):
                    dve.wait_ge(ez_ready, n + 1)
                    return ch.mark(dve.tensor_scalar(rc[:, n % NZ, :], ez[:, n % NZ, :], 1.0, -1.0, ALU.add, ALU.add))

                def lost_2(n, mark):
                    ch.upto(mark)
                    return ch.mark(dve.tensor_tensor(rc[:, n % NZ, :], ez[:, n % NZ, :], rc[:, n % NZ, :], ALU.subtract))

                def lost_3(n, mark):
                    ch.upto(mark)
                    dve.scalar_tensor_tensor(out=rc[:, n % NZ, :], in0=bank(4 + n % 4), scalar=0.0, in1=rc[:, n % NZ, :],
                                             op0=ALU.max, op1=ALU.add).then_inc(rc_ready, 1)

                def delta_(n):
                    q = n % 2
                    dve.wait_ge(ln_ready, n + 1)
                    dve.wait_ge(rc_ready, n + 1)
                    if n >= 2:
                        dve.wait_ge(dhi_ready, n - 1)
                        dve.wait_ge(dres_ready, n - 1)
                    dve.tensor_tensor(delta[:, q, :], rc[:, n % NZ, :], ez[:, n % NZ, :], ALU.add).then_inc(delta_ready, 1)

                def u_(n):
                    q = n % 2
                    dve.wait_ge(delta_ready, n + 1)
                    dve.wait_ge(xt_ready, n + 1)
                    o = slot("xt", n)
                    if n >= 2:
                        dve.wait_ge(ures_ready, n - 1)
                    dve.tensor_tensor(uu[:, q, :], delta[:, q, :], ps[:, o:o + DI], ALU.mult).then_inc(u_ready, 1)

                def rest(n):
                    q = n % 2
                    dve.wait_ge(dhi_ready, n + 1)
                    if n >= 2:
                        dve.wait_ge(dlo_ready, n - 1)
                    dve.tensor_tensor(dres[:, q, :], delta[:, q, :], dpt[:, n % NR, 0, :], ALU.subtract).then_inc(dres_ready, 1)

                def skip_(n):
                    d, t = ITEMS[n]
                    o = slot("xt", n) + DI
                    dve.wait_ge(u_ready, n + 1)
                    dve.scalar_tensor_tensor(out=skip[:, d, t, :], in0=uu[:, n % 2, :], scalar=cb[:, d, t:t + 1],
                                             in1=ps[:, o:o + DI], op0=ALU.mult, op1=ALU.add).then_inc(skip_ready, 1)

                def low(n):
                    q, r = n % 2, n % NR
                    dve.wait_ge(umi_ready, n + 1)
                    dve.tensor_tensor(upt[:, r, 2, :], ures[:, q, :], upt[:, r, 1, :], ALU.subtract).then_inc(ulo_ready, 1)

                cb_done = c_dot_b(0)
                for some in ((0, 1), (2, 3), (4,)):
                    marks = [lost_1(n) for n in some]
                    marks = [lost_2(n, k) for n, k in zip(some, marks)]
                    for n, k in zip(some, marks):
                        lost_3(n, k)
                ch.upto(cb_done)
                delta_(0)
                for n in range(NI):
                    more = n + 5 < NI
                    u_(n)
                    if n not in (4, NI - 1):
                        delta_(n + 1)
                    rest(n)
                    if more:
                        mark = lost_1(n + 5)
                    if n - 1 >= NDV:
                        low(n - 1)
                    if n == 5:
                        ch.upto(cb_done)
                    skip_(n)
                    if more:
                        lost_3(n + 5, lost_2(n + 5, mark))
                    if n == 4:
                        delta_(5)
                    if n == 3:
                        cb_done = c_dot_b(1)
                low(NI - 1)

            @block.sync
            def _(sp):
                def store_b(d):
                    sp.wait_ge(blo_ready, d + 1)
                    for k, src in enumerate([bhi, bhi, bhi, bmi, bmi, blo]):
                        sp.dma_start(bparts[2 * k + d, :, d * L * P:(d + 1) * L * P], src[:, :]).then_inc(b_stored, 16)

                sp.wait_ge(bz_ready, 1)
                for d in range(2):
                    sp.dma_start(bparts[d:12:2, :, (1 - d) * L * P:(2 - d) * L * P].rearrange("k b n -> b k n"),
                                 bz[:, :].unsqueeze(1).to_broadcast([P, 6, L * P])).then_inc(b_stored, 16)
                for n, (d, t) in enumerate(ITEMS):
                    r = n % NR
                    o = t * DI
                    sp.wait_ge(dlo_ready, n + 1)
                    sp.dma_start(dparts[d:6:2, :, o:o + DI].rearrange("k b n -> b k n"), dpt[:, r]).then_inc(p_stored[r], 16)
                    sp.wait_ge(ulo_ready, n + 1)
                    sp.dma_start(uparts[d:6:2, :, o:o + DI].rearrange("k b n -> b k n"), upt[:, r]).then_inc(p_stored[r], 16)
                    if n == 1:
                        store_b(0)
                    if n == 5:
                        store_b(1)
                sp.wait_ge(b_stored, 224)
                for r in range(NR):
                    sp.wait_ge(p_stored[r], 32 * len(range(r, NI, NR)))
        pre.close()

        outw = sb("outw", [P, 2, DC, C])
        expw = sb("expw", [P, CH, E8 * C])
        w_landed = sem("w_landed")
        scn = ExitStack()
        drows = sb("drows", [KS, 2, L * DI], BF16, ctx=scn)
        urows = sb("urows", [KS, 2, L * DI], BF16, ctx=scn)
        brows = sb("brows", [KS, 2, 2 * L * P], BF16, ctx=scn)
        da = sb("da", [P, 8, DI], ctx=scn)
        gb = sb("gb", [P, 8, DI], ctx=scn)
        hb = sb("hb", [P, 2, 2, DI], ctx=scn)
        cst = sb("cst", [P, 2, 2, L, GB], ctx=scn)
        yst = sb("yst", [P, 2, DI], ctx=scn)
        rows_landed = [sem(f"rows_landed{q}") for q in range(2)]
        e_ready, e_free, da_ready = sem("e_ready"), sem("e_free"), sem("da_ready")
        bu_ready, bu_used, gp_done = sem("bu_ready"), sem("bu_used"), sem("gp_done")
        c_staged, y_done, y_copied, y_zero = sem("c_staged"), sem("y_done"), sem("y_copied"), sem("y_zero")
        y_stored = [sem(f"y_stored{k}") for k in range(2)]
        d_padded = sem("d_padded")
        NPAIR = NG // 2
        NGP = 6

        def token(s_, d):
            return s_ if d == 0 else L - 1 - s_

        def pairs(eng, body):
            body(0, True, False)
            with eng.Fori(1, NPAIR - 1) as i:
                body(i, False, False)
            body(NPAIR - 1, False, True)

        with nc.Block() as block:
            @block.sync
            def _(sp):
                def load_rows(g, q):
                    im = bass.ds(g * GB, GB)
                    sp.dma_start(drows[KS // 2:KS, q], dparts[:, im, :]).then_inc(rows_landed[q], 16)
                    for lo_, n in ((0, 6), (6, 4), (10, 2)):
                        sp.dma_start(urows[lo_ * GB:(lo_ + n) * GB, q], uparts[0:n, im, :]).then_inc(rows_landed[q], 16)
                    sp.dma_start(brows[:, q], bparts[:, im, :]).then_inc(rows_landed[q], 16)

                def store_y(g, k):
                    sp.wait_ge(y_copied, 2 + 2 * g + k + 1)
                    sp.dma_start(yscr[bass.ds(g, 1), k], yst[0:NY, k, :]).then_inc(y_stored[k], 16)

                load_rows(0, 0)
                load_rows(1, 1)
                for d in range(2):
                    sp.dma_start(outw[:, d], a["out_wT"][d].rearrange("(c p) n -> p c n", p=P)).then_inc(w_landed, 16)
                sp.dma_start(expw[:, :, :], a["expert_wT"].rearrange("(h p) n -> p h n", p=P)).then_inc(w_landed, 16)

                def body(i, first, last):
                    for q in range(2):
                        g = 2 * i + q
                        if not (first and q == 0):
                            store_y(g - 1, 1)
                        if not last:
                            sp.wait_ge(e_ready, 8 * g + 8)
                            sp.wait_ge(bu_ready, 8 * g + 8)
                            load_rows(g + 2, q)
                        store_y(g, 0)

                pairs(sp, body)
                store_y(NG - 1, 1)
                sp.wait_ge(w_landed, 48)
                for k in range(2):
                    sp.wait_ge(y_stored[k], 16 * NG)

            @block.tensor
            def _(pe):
                def spread_delta(g, q, j):
                    d, t = j % 2, token(1 + j // 2, j % 2)
                    pe.wait_ge(e_free, 8 * g + j + 1)
                    pe.matmul(bank(j % 2), selb[:, d, :], drows[:, q, t * DI:(t + 1) * DI],
                              start=True, stop=True).then_inc(e_ready, 1)

                def b_times_u(g, q, j):
                    t = token(j // 2, j % 2)
                    o = (j % 2) * L + t
                    pe.wait_ge(bu_used, 8 * g + j + 1)
                    pe.matmul(bank(2 + j % 4), brows[:, q, o * P:(o + 1) * P], urows[:, q, t * DI:(t + 1) * DI],
                              start=True, stop=True).then_inc(bu_ready, 1)

                def outputs(g, q, k):
                    pe.wait_ge(y_copied, 2 * g + k + 1)
                    if k == 0:
                        pe.wait_ge(c_staged, g + 1)
                        pe.wait_ge(bu_used, 4 + 8 * g + 2)
                        pe.wait_ge(gp_done, NGP + NGP * g + 2)
                    else:
                        pe.wait_ge(gp_done, NGP + NGP * g + NGP)
                    for j in range(4):
                        d, s_ = j % 2, 2 * k + 1 + j // 2
                        mm = pe.matmul(ps[32 * j:32 * j + GB, (6 + k) * 512:(7 + k) * 512], cst[:, q, d, token(s_, d), :],
                                       gb[:, 4 * k + j, :], start=True, stop=True)
                    mm.then_inc(y_done, 1)

                def begin(g, q, i):
                    pe.wait_ge(rows_landed[q], 80 * i + 80)

                pe.wait_ge(d_padded, 1)
                pe.wait_ge(y_zero, 1)
                begin(0, 0, 0)
                for j in range(4):
                    spread_delta(0, 0, j)
                for j in range(4):
                    b_times_u(0, 0, j)
                spread_delta(0, 0, 4)

                def body(i, first, last):
                    for q in range(2):
                        g = 2 * i + q
                        after = not (last and q == 1)
                        spread_delta(g, q, 5)
                        b_times_u(g, q, 4)
                        spread_delta(g, q, 6)
                        b_times_u(g, q, 5)
                        b_times_u(g, q, 6)
                        spread_delta(g, q, 7)
                        b_times_u(g, q, 7)
                        if after:
                            begin(g + 1, 1 - q, i + q)
                            spread_delta(g + 1, 1 - q, 0)
                            spread_delta(g + 1, 1 - q, 1)
                        outputs(g, q, 0)
                        if after:
                            spread_delta(g + 1, 1 - q, 2)
                            b_times_u(g + 1, 1 - q, 0)
                            b_times_u(g + 1, 1 - q, 1)
                            spread_delta(g + 1, 1 - q, 3)
                            b_times_u(g + 1, 1 - q, 2)
                            b_times_u(g + 1, 1 - q, 3)
                            spread_delta(g + 1, 1 - q, 4)
                        outputs(g, q, 1)

                pairs(pe, body)

            @block.scalar
            def _(act):
                act.sem_inc(y_copied, 2)

                def exponential(g, j):
                    act.wait_ge(e_free, 2 + 8 * g + j + 1)
                    act.activation(da[:, j, :], da[:, j, :], ACT.Exp, scale=-1.0).then_inc(da_ready, 1)

                def copy_y(g, k):
                    act.wait_ge(y_done, 2 + 2 * g + k + 1)
                    act.wait_ge(y_stored[k], 16 * g)
                    act.activation(yst[0:NY, k, :], bank(6 + k, p=NY), ACT.Copy).then_inc(y_copied, 1)

                def stage_c(g, q):
                    act.activation(cst[:, q, :, :, :].rearrange("p d t b -> p (d t) b"),
                                   CT[:, :, :, bass.ds(g * GB, GB)].rearrange("p d t b -> p (d t) b"),
                                   ACT.Copy).then_inc(c_staged, 1)

                for j in range(5):
                    exponential(0, j)

                def body(i, first, last):
                    for q in range(2):
                        g = 2 * i + q
                        after = not (last and q == 1)
                        stage_c(g, q)
                        exponential(g, 5)
                        exponential(g, 6)
                        if not (first and q == 0):
                            copy_y(g - 1, 1)
                        exponential(g, 7)
                        if after:
                            exponential(g + 1, 0)
                            exponential(g + 1, 1)
                        copy_y(g, 0)
                        if after:
                            for j in range(2, 5):
                                exponential(g + 1, j)

                pairs(act, body)
                copy_y(NG - 1, 1)

            @block.gpsimd
            def _(pool):
                pool.sem_inc(gp_done, NGP)

                def decayed(g, s_, d):
                    j = 2 * (s_ - 1) + d
                    pool.wait_ge(da_ready, 8 * g + j + 1)
                    pool.wait_ge(bu_used, 4 + 8 * g + 2 * (s_ - 1) + d + 1)
                    if j == 2:
                        pool.wait_ge(y_done, 2 * g + 1)
                    if j == 4:
                        pool.wait_ge(y_done, 2 * g + 2)
                    pool.tensor_tensor(gb[:, j, :], da[:, j, :], hb[:, d, (s_ - 1) % 2, :], ALU.mult).then_inc(gp_done, 1)

                def body(i, first, last):
                    for q in range(2):
                        for s_, d in [(2, 0), (2, 1), (3, 0), (3, 1), (4, 0), (4, 1)]:
                            decayed(2 * i + q, s_, d)

                pairs(pool, body)

            @block.vector
            def _(dve):
                dve.memset(drows[0:KS // 2, :, :], 0.0).then_inc(d_padded, 1)
                dve.memset(ps[:, 6 * 512:8 * 512], 0.0).then_inc(y_zero, 1)
                dve.sem_inc(e_free, 2)
                dve.sem_inc(bu_used, 4)
                dve.sem_inc(y_done, 2)

                def argument(g, j):
                    dve.wait_ge(e_ready, 8 * g + j + 1)
                    dve.tensor_tensor(da[:, j, :], bank(j % 2), expA[:, j % 2, :], ALU.mult).then_inc(e_free, 1)

                def decayed_1(g, d):
                    dve.wait_ge(da_ready, 8 * g + d + 1)
                    if d == 0:
                        dve.wait_ge(y_done, 2 * g + 1)
                    dve.wait_ge(bu_ready, 8 * g + d + 1)
                    dve.tensor_tensor(gb[:, d, :], da[:, d, :], bank(2 + d), ALU.mult).then_inc(bu_used, 1)

                def state(g, s_, d):
                    j = 2 * s_ + d
                    dve.wait_ge(bu_ready, 8 * g + j + 1)
                    if s_ == 1:
                        dve.wait_ge(gp_done, NGP * g + 5 + d)
                        dve.wait_ge(bu_used, 4 + 8 * g + d + 1)
                    else:
                        dve.wait_ge(gp_done, NGP + NGP * g + 2 * (s_ - 2) + d + 1)
                    dve.tensor_tensor(hb[:, d, s_ % 2, :], gb[:, 2 * (s_ - 1) + d, :], bank(2 + j % 4),
                                      ALU.add).then_inc(bu_used, 1)

                for j in range(4):
                    argument(0, j)
                for d in range(2):
                    decayed_1(0, d)
                argument(0, 4)

                def body(i, first, last):
                    for q in range(2):
                        g = 2 * i + q
                        after = not (last and q == 1)
                        state(g, 1, 0)
                        state(g, 1, 1)
                        argument(g, 5)
                        argument(g, 6)
                        state(g, 2, 0)
                        argument(g, 7)
                        state(g, 2, 1)
                        if after:
                            argument(g + 1, 0)
                        state(g, 3, 0)
                        if after:
                            argument(g + 1, 1)
                        state(g, 3, 1)
                        if after:
                            argument(g + 1, 2)
                            argument(g + 1, 3)
                            decayed_1(g + 1, 0)
                            decayed_1(g + 1, 1)
                            argument(g + 1, 4)

                pairs(dve, body)
        scn.close()

        fin = ExitStack()
        yg = sb("yg", [P, 2, 2, DI], ctx=fin)
        ytok = sb("ytok", [P, 2, L, DI], ctx=fin)
        y_landed = [sem(f"y_landed{n}") for n in range(L)]
        ygT = sb("ygT", [P, 2, 2, DC, P], ctx=fin)
        h1 = sb("h1", [P, L, C], ctx=fin)
        xf = sb("xf", [P, L, C], ctx=fin)
        mo = sb("mo", [P, L, C], ctx=fin)
        xfT = sb("xfT", [P, 2, CH, P], ctx=fin)
        fst = sb("fst", [P, L, 6], ctx=fin)
        fmv = sb("fmv", [P, L, 2], ctx=fin)
        fve = sb("fve", [P, L], ctx=fin)
        frs = sb("frs", [P, L], ctx=fin)
        eid = sb("eid", [P, E8], ctx=fin)
        gsco = sb("gsco", [P, L, E8], ctx=fin)
        gtop = sb("gtop", [P, L, E8], ctx=fin)
        gidx = sb("gidx", [P, L, E8], mybir.dt.uint32, ctx=fin)
        gidf = sb("gidf", [P, L], ctx=fin)
        hot = sb("hot", [P, L, E8], ctx=fin)
        ysum_done, yg_ready, ygt_ready, ygt_copied = (sem("ysum_done"), sem("yg_ready"),
                                                                sem("ygt_ready"), sem("ygt_copied"))
        o_ready, h1_ready, fve_ready, frs_ready, xf_ready = (sem("o_ready"), sem("h1_ready"), sem("fve_ready"),
                                                             sem("frs_ready"), sem("xf_ready"))
        xt5_ready, xt5_copied, gate_ready, gate_read = sem("xt5_ready"), sem("xt5_copied"), sem("gate_ready"), sem("gate_read")
        ex5_ready, ex5_used, mo_ready, o_stored, f_chain = (sem("ex5_ready"), sem("ex5_used"), sem("mo_ready"),
                                                            sem("o_stored"), sem("f_chain"))
        with nc.Block() as block:
            @block.sync
            def _(sp):
                for n in range(L):
                    for d in range(2):
                        if (n, d) not in ((0, 0), (L - 1, 1)):
                            s_ = token(n, d)
                            j = 2 * ((s_ - 1) % 2) + d
                            sp.dma_start(ytok[:, d, n, :], yscr[:, (s_ - 1) // 2, 32 * j:32 * j + GB, :]).then_inc(y_landed[n], 16)
                for t in range(L):
                    sp.wait_ge(mo_ready, t + 1)
                    sp.dma_start(out[:, t, :], mo[:, t, :]).then_inc(o_stored, 16)
                sp.wait_ge(o_stored, 16 * L)

            @block.gpsimd
            def _(pool):
                def total(n):
                    pool.wait_ge(y_landed[n], 16 if n in (0, L - 1) else 32)
                    for d in range(2):
                        if (n, d) not in ((0, 0), (L - 1, 1)):
                            pool.tensor_tensor(skip[:, d, n, :], skip[:, d, n, :], ytok[:, d, n, :], ALU.add).then_inc(ysum_done, 1)

                def root(n):
                    pool.wait_ge(fve_ready, n + 1)
                    pool.tensor_tensor(frs[:, n:n + 1], fve[:, n:n + 1], mhalf[:, 0:1], ALU.pow).then_inc(frs_ready, 1)

                total(0)
                total(1)
                for n in range(L):
                    if n + 2 < L:
                        total(n + 2)
                    root(n)

            @block.tensor
            def _(pe):
                def turned(n):
                    for d in range(2):
                        pe.wait_ge(yg_ready, 2 * n + d + 1)
                        if n >= 1:
                            pe.wait_ge(ygt_copied, 2 * n + d - 1)
                        for c in range(DC):
                            mm = pe.transpose(bank(d, c * P, (c + 1) * P), yg[:, n % 2, d, c * P:(c + 1) * P], ident[:, :])
                        mm.then_inc(ygt_ready, 1)

                def projected(n):
                    if n >= 2:
                        pe.wait_ge(h1_ready, n - 1)
                    for d in range(2):
                        pe.wait_ge(ygt_copied, 2 * n + d + 1)
                        for c in range(DC):
                            mm = pe.matmul(bank(2 + n % 2, 0, C), ygT[:, n % 2, d, c, :], outw[:, d, c, :],
                                           start=(d == 0 and c == 0), stop=(d == 1 and c == DC - 1))
                    mm.then_inc(o_ready, 1)

                def experts(n):
                    pe.wait_ge(xf_ready, n + 1)
                    if n >= 1:
                        pe.wait_ge(gate_read, n)
                    for h in range(CH):
                        mm = pe.transpose(bank(7, h * P, (h + 1) * P), xf[:, n, h * P:(h + 1) * P], ident[:, :])
                    mm.then_inc(xt5_ready, 1)
                    pe.wait_ge(xt5_copied, n + 1)
                    for h in range(CH):
                        mm = pe.matmul(bank(7, C, C + E8), xfT[:, n % 2, h, :], gatew[:, h, :],
                                       start=(h == 0), stop=(h == CH - 1))
                    mm.then_inc(gate_ready, 1)
                    for k in range(E8 // 2):
                        m = 4 * n + k
                        if m >= 3:
                            pe.wait_ge(ex5_used, m - 2)
                        for h in range(CH):
                            mm = pe.matmul(bank(4 + m % 3), xfT[:, n % 2, h, :], expw[:, h, k * 512:(k + 1) * 512],
                                           start=(h == 0), stop=(h == CH - 1))
                        mm.then_inc(ex5_ready, 1)

                for n in range(2):
                    turned(n)
                    projected(n)
                for n in range(L):
                    experts(n)
                    if n + 2 < L:
                        turned(n + 2)
                        projected(n + 2)

            @block.scalar
            def _(act):
                def copy_y(n):
                    for d in range(2):
                        act.wait_ge(ygt_ready, 2 * n + d + 1)
                        if n >= 2:
                            act.wait_ge(o_ready, n - 1)
                        act.activation(ygT[:, n % 2, d, :, :], bank(d), ACT.Copy).then_inc(ygt_copied, 1)

                copy_y(0)
                copy_y(1)
                for n in range(L):
                    act.wait_ge(xt5_ready, n + 1)
                    if n >= 2:
                        act.wait_ge(ex5_ready, 4 * (n - 1))
                    act.activation(xfT[:, n % 2, :, :], bank(7, 0, C), ACT.Copy).then_inc(xt5_copied, 1)
                    if n + 2 < L:
                        copy_y(n + 2)

            @block.vector
            def _(dve):
                ch = Chain(dve, f_chain)
                for e in range(E8):
                    ins = dve.memset(eid[:, e:e + 1], float(e))
                ch.link(ins)
                sums = [0]

                def gated(n):
                    for d in range(2):
                        if (n, d) not in ((0, 0), (L - 1, 1)):
                            sums[0] += 1
                            dve.wait_ge(ysum_done, sums[0])
                        if n >= 2:
                            dve.wait_ge(ygt_ready, 2 * (n - 2) + d + 1)
                        dve.tensor_tensor(yg[:, n % 2, d, :], skip[:, d, n, :], siluz[:, d, n, :], ALU.mult).then_inc(yg_ready, 1)

                def mixed(n):
                    dve.wait_ge(o_ready, n + 1)
                    dve.scalar_tensor_tensor(out=h1[:, n, :], in0=bank(2 + n % 2, 0, C), scalar=0.5, in1=hbuf[:, n, :],
                                             op0=ALU.mult, op1=ALU.add).then_inc(h1_ready, 1)
                    dve.wait_ge(h1_ready, n + 1)
                    ch.link(dve.bn_stats(fst[:, n, :], h1[:, n, :]))
                    ch.link(dve.bn_aggr(fmv[:, n, :], fst[:, n, :]))
                    dve.tensor_scalar(fve[:, n:n + 1], fmv[:, n, 1:2], EPS, None, ALU.add).then_inc(fve_ready, 1)
                    dve.wait_ge(frs_ready, n + 1)
                    dve.tensor_scalar(xf[:, n, :], h1[:, n, :], fmv[:, n, 0:1], frs[:, n:n + 1], ALU.subtract,
                                      ALU.mult).then_inc(xf_ready, 1)
                    dve.wait_ge(xf_ready, n + 1)
                    ch.link(dve.tensor_tensor(mo[:, n, :], h1[:, n, :], xf[:, n, :], ALU.add))

                def chosen(n):
                    dve.wait_ge(gate_ready, n + 1)
                    dve.tensor_copy(gsco[:, n, :], bank(7, C, C + E8)).then_inc(gate_read, 1)
                    dve.wait_ge(gate_read, n + 1)
                    ch.link(dve.max(gtop[:, n, :], gsco[:, n, :]))
                    ch.link(dve.max_index(gidx[:, n, :], gtop[:, n, :], gsco[:, n, :]))
                    ch.link(dve.tensor_copy(gidf[:, n:n + 1], gidx[:, n, 0:1]))
                    ch.link(dve.tensor_scalar(hot[:, n, :], eid[:, :], gidf[:, n:n + 1], None, ALU.is_equal))
                    for k in range(E8 // 2):
                        m = 4 * n + k
                        dve.wait_ge(ex5_ready, m + 1)
                        for e in range(2):
                            ins = dve.scalar_tensor_tensor(out=mo[:, n, :], in0=bank(4 + m % 3, e * C, (e + 1) * C),
                                                           scalar=hot[:, n, 2 * k + e:2 * k + e + 1], in1=mo[:, n, :],
                                                           op0=ALU.mult, op1=ALU.add)
                            if e == 0:
                                ch.link(ins)
                            else:
                                ins.then_inc(ex5_used, 1)
                                dve.wait_ge(ex5_used, m + 1)
                    dve.sem_inc(mo_ready, 1)

                gated(0)
                gated(1)
                mixed(0)
                mixed(1)
                for n in range(L):
                    if n + 2 < L:
                        gated(n + 2)
                    chosen(n)
                    if n + 2 < L:
                        mixed(n + 2)
        fin.close()



def lay_out(x):
    import numpy as np
    g = {k: np.asarray(v) for k, v in x.items()}
    im = g["x"][:, :, :84, :84].reshape(B, 3, 2, 3, 14, 2, 3, 14)
    xT = im.transpose(1, 4, 7, 2, 5, 3, 6, 0).reshape(KP, W4 * WT)
    t = "L0_tok_"
    m = ["L0_attn_f_", "L0_attn_b_"]

    def halves(v):
        return v.reshape(-1, P).T

    def taps(v):
        return v.reshape(DC, P, 4).transpose(1, 0, 2).reshape(P, DC * 4)

    vec_cols = np.concatenate(
        [halves(g[t + n]) for n in ["la_ln_q_g", "la_ln_q_b", "ga_ln_q_g", "ga_ln_q_b", "la_ln_kv_g", "la_ln_kv_b",
                                    "ga_ln_kv_g", "ga_ln_kv_b"]]
        + [halves(g["L0_attn_ln_g"]), halves(g["L0_attn_ln_b"]), halves(g[t + "class_emb"])]
        + [halves(g[p + "conv_b"]) for p in m] + [taps(g[p + "conv_w"]) for p in m]
        + [halves(g[p + "D_skip"]) for p in m], axis=1)
    vec_rows = np.concatenate([g[t + "la_proj_b"], g[t + "mod_b"], g[t + "ga_proj_b"], g[t + "class_emb"]])[None]
    wall = np.concatenate([g[t + n] for n in ["la_wq", "ga_wq", "la_wkv", "ga_wkv"]], axis=1)
    sel = np.zeros((KS // 2 // GB // 2, 2, GB, 2, GB, NS), np.float32)
    for d in range(2):
        for i in range(GB):
            sel[:, d, i, d, i] = 1
    sel = np.concatenate([np.zeros((KS // 2, 2 * P), np.float32), sel.reshape(KS // 2, 2 * P)])
    both = lambda n, f: np.stack([f(g[p + n]) for p in m])
    arrays = {
        "xT": xT, "sel": sel, "conv_wT": g[t + "conv_w"].reshape(C, KP).T, "vec_cols": vec_cols, "vec_rows": vec_rows,
        "wall": wall, "la_proj_w": g[t + "la_proj_w"], "ga_proj_w": g[t + "ga_proj_w"], "mod_w": g[t + "mod_w"],
        "in_wT": both("in_w", lambda v: v.T), "xproj_wT": both("xproj_w", lambda v: v.T),
        "dt_wT": both("dt_w", lambda v: v.T), "dt_b": both("dt_b", lambda v: v[None]),
        "A_logT": both("A_log", lambda v: v.T), "out_wT": both("out_w", lambda v: v.T),
        "gate_wT": g["L0_ffn_gate_w"].T, "expert_wT": g["L0_ffn_expert_w"].transpose(2, 0, 1).reshape(C, E8 * C),
    }
    return {k: np.ascontiguousarray(v) for k, v in arrays.items()}


def kernel(**inputs):
    import numpy as np
    import concourse.bacc as bacc
    from concourse.bass_utils import run_bass_kernel_spmd

    arrays = lay_out(inputs)
    nc = bacc.Bacc("TRN2", target_bir_lowering=False, num_devices=1)
    aps = {n: nc.dram_tensor("in_" + n, v.shape, mybir.dt.from_np(v.dtype), kind="ExternalInput").ap()
           for n, v in arrays.items()}
    out = nc.dram_tensor("out", (B, L, C), F32, kind="ExternalOutput").ap()
    tower(nc, aps, out)
    r = run_bass_kernel_spmd(nc, [{"in_" + n: v for n, v in arrays.items()}], core_ids=[0])
    return r.results[0]["out"]
```

```python
from contextlib import ExitStack

import concourse.bass as bass
from concourse import mybir

ALU = mybir.AluOpType
ACT = mybir.ActivationFunctionType
AX = mybir.AxisListType
F32 = mybir.dt.float32
BF16 = mybir.dt.bfloat16

B, C, H, DH = 128, 256, 8, 32
P = 128
CH = C // P
W4, K9 = 4, 9
KP = 3 * 14 * 14
KC = -(-KP // P)
KL = KP - (KC - 1) * P
WT = K9 * B
EC = 3
EN = WT // EC
L, DI, NS, R = 5, 512, 16, 16
DC = DI // P
NX = R + 2 * NS
GB = P // NS
NG = B // GB
E8 = 8
EPS = 1e-5
QSCALE = C ** -0.5

VC = {}
_n = 0
for _name, _w in [("q_g", 2), ("q_b", 2), ("gq_g", 2), ("gq_b", 2), ("kv_g", 2), ("kv_b", 2), ("gkv_g", 2),
                  ("gkv_b", 2), ("ln_g", 2), ("ln_b", 2), ("cls", 2), ("cb0", 4), ("cb1", 4), ("cw0", 16),
                  ("cw1", 16), ("D0", 4), ("D1", 4)]:
    VC[_name] = _n
    _n += _w
NVC = _n
VR = {"proj_b": 0, "mod_b": 256, "gproj_b": 512, "cls": 768}
NVR = 1024
KS = 12 * GB
SEG = {"q": (0, 256), "gq": (256, 256), "kv": (512, 512), "gkv": (1024, 512)}


class Chain:

    def __init__(self, eng, sem, base=0):
        self.eng, self.sem, self.base, self.n = eng, sem, base, 0

    def link(self, ins):
        ins.then_inc(self.sem, 1)
        self.n += 1
        self.eng.wait_ge(self.sem, self.base + self.n)

    def mark(self, ins):
        ins.then_inc(self.sem, 1)
        self.n += 1
        return self.n

    def upto(self, n):
        self.eng.wait_ge(self.sem, self.base + n)


def tower(nc, a, out):
    top = ExitStack()
    with top:
        def sb(name, shape, dt=F32, ctx=top):
            return ctx.enter_context(nc.sbuf_tensor(name, shape, dt))

        def sem(name):
            return top.enter_context(nc.semaphore(name))

        ps = top.enter_context(nc.psum_tensor("ps", [P, 8 * 512], F32))

        def bank(n, lo=0, hi=512, p=P):
            return ps[0:p, n * 512 + lo:n * 512 + hi]

        ident = sb("ident", [P, P])
        mhalf = sb("mhalf", [P, 16])
        cols = sb("cols", [P, NVC])
        rows = sb("rows", [P, NVR])
        inw = sb("inw", [P, 2, CH, 2 * DI])
        xpw = sb("xpw", [P, 2, DC, NX])
        dtw = sb("dtw", [33, 2, DI])
        expA = sb("expA", [P, 2, DI])
        gatew = sb("gatew", [P, CH, E8])
        hbuf = sb("hbuf", [P, L, C])
        maskb = sb("maskb", [P, GB, NS])
        sel = sb("sel", [KS, 2, P])
        selb = sb("selb", [KS, 2, P], BF16)

        def col(name, j=0, n=1):
            return cols[:, VC[name] + j:VC[name] + j + n]

        def row(name, n):
            return rows[:, VR[name]:VR[name] + n]

        dparts = nc.dram_tensor("dparts", (6, B, L * DI), BF16, kind="Internal").ap()
        uparts = nc.dram_tensor("uparts", (6, B, L * DI), BF16, kind="Internal").ap()
        bparts = nc.dram_tensor("bparts", (12, B, 2 * L * P), BF16, kind="Internal").ap()
        NY = 3 * 32 + GB
        yscr = nc.dram_tensor("yscr", (NG, 2, NY, DI), F32, kind="Internal").ap()

        xn = sb("xn", [P, L, C])
        xst = sb("xst", [P, L, 6])
        xmv = sb("xmv", [P, L, 2])
        xv = sb("xv", [P, L])
        xr = sb("xr", [P, L])
        tok = ExitStack()
        redT = sb("redT", [P, W4, CH, P], ctx=tok)
        agg = sb("agg", [P, W4, C], ctx=tok)
        wall = sb("wall", [P, CH, 1536], ctx=tok)
        brow = sb("brow", [P, 1536], ctx=tok)
        projw = sb("projw", [P, 3, CH, C], ctx=tok)
        convw = sb("convw", [P, KC, C], ctx=tok)
        onesc = sb("onesc", [P, P], ctx=tok)
        xbuf = sb("xbuf", [P, 2, KC, WT], ctx=tok)
        peT = sb("peT", [P, 2, CH, WT], ctx=tok)
        kvs = sb("kvs", [P, 2, K9, 2 * C], ctx=tok)
        prod = sb("prod", [P, K9, C], ctx=tok)
        redw = sb("redw", [P, 2, CH, P], ctx=tok)
        st = sb("st", [P, K9 + 1, 6], ctx=tok)
        mv = sb("mv", [P, K9 + 1, 2], ctx=tok)
        veps = sb("veps", [P, K9 + 1], ctx=tok)
        rstd = sb("rstd", [P, K9 + 1], ctx=tok)
        qn = sb("qn", [P, C], ctx=tok)
        qb = sb("qb", [P, H], ctx=tok)
        sc = sb("sc", [P, K9, H], ctx=tok)
        mx = sb("mx", [P, H], ctx=tok)
        ex = sb("ex", [P, K9, H], ctx=tok)
        sm = sb("sm", [P, H], ctx=tok)
        lo = sb("lo", [P, 2, C], ctx=tok)
        gkvs = sb("gkvs", [P, W4, 2 * C], ctx=tok)
        aggT = sb("aggT", [P, CH, P], ctx=tok)
        loT = sb("loT", [P, CH, P], ctx=tok)
        gaT = sb("gaT", [P, CH, P], ctx=tok)
        gst = sb("gst", [P, W4 + 1, 6], ctx=tok)
        gmv = sb("gmv", [P, W4 + 1, 2], ctx=tok)
        gve = sb("gve", [P, W4 + 1], ctx=tok)
        grs = sb("grs", [P, W4 + 1], ctx=tok)
        gqn = sb("gqn", [P, C], ctx=tok)
        gqraw = sb("gqraw", [P, C], ctx=tok)
        gqb = sb("gqb", [P, H], ctx=tok)
        gsc = sb("gsc", [P, W4, H], ctx=tok)
        gmx = sb("gmx", [P, H], ctx=tok)
        gex = sb("gex", [P, W4, H], ctx=tok)

        s_vec, s_wall, s_conv, s_proj, s_late = sem("s_vec"), sem("s_wall"), sem("s_conv"), sem("s_proj"), sem("s_late")
        expA_ready, s_const, s_dtz = sem("expA_ready"), sem("s_const"), sem("s_dtz")
        s_bias, s_brow = sem("s_bias"), sem("s_brow")
        s_wg, s_wmean, s_wready = sem("s_wg"), sem("s_wmean"), sem("s_wready")
        x_landed = [[sem(f"x_landed{q}{c}") for c in range(EC)] for q in range(2)]
        emb_ready, emb_free = sem("emb_ready"), sem("emb_free")
        kv_ready, kv_free, kvs_free = sem("kv_ready"), sem("kv_free"), sem("kvs_free")
        tr_ready, tr_free = sem("tr_ready"), sem("tr_free")
        red_ready, red_kept, q_ready, q_free = sem("red_ready"), sem("red_kept"), sem("q_ready"), sem("q_free")
        veps_ready, rstd_ready, sc_ready, ex_ready = sem("veps_ready"), sem("rstd_ready"), sem("sc_ready"), sem("ex_ready")
        d_chain, agg_ready, prod_ready = sem("d_chain"), sem("agg_ready"), sem("prod_ready")
        aT_ready, aT_copied = sem("aT_ready"), sem("aT_copied")
        lo_summed, lo_ready, lT_ready, lT_copied = sem("lo_summed"), sem("lo_ready"), sem("lT_ready"), sem("lT_copied")
        gkv_ready, gkv_copied, mod_ready, mod_copied = sem("gkv_ready"), sem("gkv_copied"), sem("mod_ready"), sem("mod_copied")
        gq_ready, gq_read, gve_ready, grs_ready = sem("gq_ready"), sem("gq_read"), sem("gve_ready"), sem("grs_ready")
        gsc_ready, gex_ready, gag_ready, gaT_ready = sem("gsc_ready"), sem("gex_ready"), sem("gag_ready"), sem("gaT_ready")
        gaT_copied, cls_ready = sem("gaT_copied"), sem("cls_ready")
        xv_ready, xr_ready, xn_ready, xnT_ready = sem("xv_ready"), sem("xr_ready"), sem("xn_ready"), sem("xnT_ready")

        T_EMB, T_KV, T_TR, T_Q = 0, 2, 4, 6
        LB = [[7] * 5, [7] * 5, [7] * 5, [1, 2, 3, 4, 6]]
        PREP = [("q", 6, 2), ("kv", 7, 3), ("gkv", 7, 7), ("gq", 7, 7)]
        PARTS3 = [(0, 3), (3, 6), (6, 9)]
        def halves(n):
            return ps[:, :].rearrange("p (a n) -> p a n", n=1024)[:, 0:CH, n * 512:n * 512 + P]

        RED_AT = 3

        with nc.Block() as block:
            @block.sync
            def _(sp):
                sp.dma_start(convw[:, 0:KC - 1, :], a["conv_wT"][0:(KC - 1) * P].rearrange("(k p) n -> p k n", p=P)).then_inc(s_conv, 16)
                sp.dma_start(convw[0:KL, KC - 1, :], a["conv_wT"][(KC - 1) * P:KP]).then_inc(s_conv, 16)

                def load_x(w, c):
                    src = a["xT"][:, w * WT + c * EN:w * WT + (c + 1) * EN]
                    sp.dma_start(xbuf[:, w % 2, 0:KC - 1, c * EN:(c + 1) * EN],
                                 src[0:(KC - 1) * P].rearrange("(k p) n -> p k n", p=P)).then_inc(x_landed[w % 2][c], 16)
                    sp.dma_start(xbuf[0:KL, w % 2, KC - 1, c * EN:(c + 1) * EN],
                                 src[(KC - 1) * P:KP]).then_inc(x_landed[w % 2][c], 16)

                load_x(0, 0)
                sp.dma_start(cols[:, :], a["vec_cols"]).then_inc(s_vec, 16)
                sp.dma_start(sel[:, :, :], a["sel"].rearrange("k (d m) -> k d m", d=2)).then_inc(s_vec, 16)
                sp.dma_start(wall[:, :, :], a["wall"].rearrange("(h p) n -> p h n", p=P)).then_inc(s_wall, 16)
                load_x(0, 1)
                load_x(0, 2)
                for c in range(EC):
                    load_x(1, c)
                sp.dma_start(rows[:, :], a["vec_rows"].to_broadcast([P, NVR])).then_inc(s_proj, 16)
                for n, name in enumerate(["la_proj_w", "ga_proj_w", "mod_w"]):
                    sp.dma_start(projw[:, n], a[name].rearrange("(h p) n -> p h n", p=P)).then_inc(s_proj, 16)
                for w in (2, 3):
                    sp.wait_ge(emb_ready, 6 * (w - 1))
                    for c in range(EC):
                        load_x(w, c)
                for d in range(2):
                    sp.dma_start(inw[:, d], a["in_wT"][d].rearrange("(h p) n -> p h n", p=P)).then_inc(s_late, 16)
                    sp.dma_start(xpw[:, d], a["xproj_wT"][d].rearrange("(c p) n -> p c n", p=P)).then_inc(s_late, 16)
                    for g in range(GB):
                        sp.dma_start(expA[g * NS:(g + 1) * NS, d], a["A_logT"][d]).then_inc(s_late, 16)
                sp.dma_start(gatew[:, :, :], a["gate_wT"].rearrange("(h p) n -> p h n", p=P)).then_inc(s_late, 16)
                sp.wait_ge(s_dtz, 1)
                for d in range(2):
                    sp.dma_start(dtw[0:R, d], a["dt_wT"][d]).then_inc(s_late, 16)
                    sp.dma_start(dtw[32:33, d], a["dt_b"][d]).then_inc(s_late, 16)
                sp.wait_ge(s_late, 16 * (2 * (2 + GB) + 1 + 4))

            @block.gpsimd
            def _(pool):
                pool.memset(ident[:, :], 0.0).then_inc(s_const, 1)
                pool.memset(maskb[:, :, :], 0.0).then_inc(s_const, 1)
                pool.memset(mhalf[:, :], -0.5).then_inc(s_const, 1)
                pool.wait_ge(s_const, 3)
                pool.affine_select(out=ident[:, :], in_=ident[:, :], compare_op=ALU.not_equal, fill=1.0, base=0,
                                   pattern=[[-1, P]], channel_multiplier=1).then_inc(s_const, 1)
                pool.memset(dtw[:, :, :], 0.0).then_inc(s_dtz, 1)
                pool.wait_ge(s_const, 4)
                for j in range(NG):
                    pool.tensor_tensor(maskb[:, :, :], maskb[:, :, :],
                                       ident[:, j * GB:(j + 1) * GB].unsqueeze(2).to_broadcast([P, GB, NS]),
                                       ALU.add).then_inc(s_const, 1)
                    pool.wait_ge(s_const, 5 + j)
                pool.wait_ge(s_vec, 32)
                pool.tensor_copy(selb[:, :, :], sel[:, :, :]).then_inc(s_const, 1)
                for w in range(W4):
                    pool.wait_ge(veps_ready, 2 * w + 1)
                    pool.tensor_tensor(rstd[:, K9:K9 + 1], veps[:, K9:K9 + 1], mhalf[:, 0:1], ALU.pow).then_inc(rstd_ready, 1)
                    pool.wait_ge(veps_ready, 2 * w + 2)
                    pool.tensor_tensor(rstd[:, 0:K9], veps[:, 0:K9], mhalf[:, 0:K9], ALU.pow).then_inc(rstd_ready, 1)
                pool.wait_ge(gve_ready, 1)
                pool.tensor_tensor(grs[:, 1:W4 + 1], gve[:, 1:W4 + 1], mhalf[:, 0:W4], ALU.pow).then_inc(grs_ready, 1)
                pool.wait_ge(gve_ready, 2)
                pool.tensor_tensor(grs[:, 0:1], gve[:, 0:1], mhalf[:, 0:1], ALU.pow).then_inc(grs_ready, 1)
                pool.wait_ge(xv_ready, 1)
                pool.tensor_tensor(xr[:, 0:W4 - 1], xv[:, 0:W4 - 1], mhalf[:, 0:W4 - 1], ALU.pow).then_inc(xr_ready, 1)
                for n in range(2):
                    t = W4 - 1 + n
                    pool.wait_ge(xv_ready, 2 + n)
                    pool.tensor_tensor(xr[:, t:t + 1], xv[:, t:t + 1], mhalf[:, 0:1], ALU.pow).then_inc(xr_ready, 1)

            @block.tensor
            def _(pe):
                def embedding(w, between=()):
                    q = w % 2
                    for c in range(EC):
                        for h in range(CH):
                            j = c * CH + h
                            if j < len(between) and between[j]:
                                between[j]()
                            if h == 0:
                                pe.wait_ge(x_landed[q][c], 32 * (w // 2) + 32)
                            pe.wait_ge(emb_free, 6 * w + j + 1)
                            for k in range(KC):
                                n = P if k < KC - 1 else KL
                                mm = pe.matmul(bank(T_EMB + j % 2, 0, EN), convw[0:n, k, h * P:(h + 1) * P],
                                               xbuf[0:n, q, k, c * EN:(c + 1) * EN],
                                               start=(k == 0), stop=(k == KC - 1))
                            mm.then_inc(emb_ready, 1)

                def offset(i):
                    s, b_, _ = PREP[i]
                    o, n = SEG[s]
                    if i == 0:
                        pe.wait_ge(s_vec, 32)
                        pe.wait_ge(s_wall, 16)
                    if i >= 2:
                        pe.wait_ge(s_brow, i)
                        pe.wait_ge(s_wready, 4)
                    for h in range(CH):
                        mm = pe.matmul(bank(b_, 0, n), col(s + "_b", h).to_broadcast([P, P]), wall[:, h, o:o + n],
                                       start=(h == 0), stop=(h == CH - 1))
                    mm.then_inc(s_bias, 1)

                def mean(i):
                    s, _, b_ = PREP[i]
                    o, n = SEG[s]
                    pe.wait_ge(s_wg, 2 * i + 2)
                    if i == 2:
                        pe.wait_ge(s_brow, 4)
                    if i == 3:
                        pe.wait_ge(s_wready, 6)
                    for h in range(CH):
                        mm = pe.matmul(bank(b_, 0, n), onesc[:, :], wall[:, h, o:o + n],
                                       start=(h == 0), stop=(h == CH - 1))
                    mm.then_inc(s_wmean, 1)

                def turn(w, u, src):
                    pe.wait_ge(tr_free, 10 * w + u + 1)
                    for h in range(CH):
                        mm = pe.transpose(bank(T_TR + u % 2, h * P, (h + 1) * P), src(h), ident[:, :])
                    mm.then_inc(tr_ready, 1)

                def tokens(w):
                    q = w % 2
                    for t in range(K9):
                        if t == RED_AT:
                            pe.wait_ge(red_ready, w + 1)
                            turn(w, RED_AT, lambda h: redw[:, q, h, :])
                            pe.wait_ge(q_free, w + 1)
                            for h in range(CH):
                                mm = pe.matmul(bank(T_Q, 0, C), redw[:, q, h, :], wall[:, h, 0:C],
                                               start=(h == 0), stop=(h == CH - 1))
                            mm.then_inc(q_ready, 1)
                        if t % EC == 0:
                            pe.wait_ge(emb_free, 2 + 6 * w + 2 * (t // EC) + 2)
                        turn(w, t if t < RED_AT else t + 1, lambda h: peT[:, q, h, t * B:(t + 1) * B])
                        pe.wait_ge(kv_free, 9 * w + t + 1)
                        for h in range(CH):
                            mm = pe.matmul(bank(T_KV + (q + t) % 2), peT[:, q, h, t * B:(t + 1) * B],
                                           wall[:, h, 512:1024], start=(h == 0), stop=(h == CH - 1))
                        mm.then_inc(kv_ready, 1)

                def agg_turned(w):
                    pe.wait_ge(agg_ready, w + 1)
                    if w == 0:
                        pe.wait_ge(s_wready, 8)
                    elif w < W4 - 1:
                        pe.wait_ge(mod_copied, w)
                    b_ = LB[w][0]
                    for h in range(CH):
                        mm = pe.transpose(bank(b_, h * P, (h + 1) * P), agg[:, w, h * P:(h + 1) * P], ident[:, :])
                    mm.then_inc(aT_ready, 1)

                def turned_sum(b_, offset_at, parts, ready, fill):
                    for h in range(CH):
                        pe.matmul(bank(b_ + 2 * h, 0, P), brow[:, offset_at + h * P:offset_at + (h + 1) * P], ident[:, :],
                                  start=True, stop=False)
                    keep_clock(fill, 1)
                    for n, (lo_, hi_) in enumerate(parts):
                        pe.wait_ge(ready, n + 1)
                        for t in range(lo_, hi_):
                            for h in range(CH):
                                mm = pe.matmul(bank(b_ + 2 * h, 0, P), prod[:, t, h * P:(h + 1) * P], ident[:, :],
                                               start=False, stop=(t == parts[-1][1] - 1))
                    return mm

                def keep_clock(n, b_):
                    for _ in range(n):
                        pe.matmul(bank(b_), ident[:, :], wall[:, 0, 0:512], start=True, stop=True)

                def local_out(w):
                    if w == 0:
                        pe.wait_ge(s_proj, 16 * 4)
                    pe.wait_ge(red_kept, 2 + w + 1)
                    pe.wait_ge(aT_copied, w + 1)
                    b_ = LB[w][1]
                    for h in range(CH):
                        pe.matmul(bank(b_, 0, C), aggT[:, h, :], projw[:, 0, h, :],
                                  start=(h == 0), stop=False, skip_group_check=True)
                    for h in range(CH):
                        mm = pe.matmul(bank(b_, h * P, (h + 1) * P), redT[:, w, h, :], ident[:, :],
                                       start=False, stop=(h == CH - 1), skip_group_check=True)
                    mm.then_inc(lo_summed, 1)

                def lo_turned(w):
                    pe.wait_ge(lo_ready, w + 1)
                    b_ = LB[w][2]
                    for h in range(CH):
                        mm = pe.transpose(bank(b_, h * P, (h + 1) * P), lo[:, w % 2, h * P:(h + 1) * P], ident[:, :])
                    mm.then_inc(lT_ready, 1)

                def keys_values(w):
                    pe.wait_ge(lT_copied, w + 1)
                    if w == W4 - 1:
                        for n in range(2):
                            for h in range(CH):
                                mm = pe.matmul(bank(LB[w][3] + n, 0, C), loT[:, h, :],
                                               wall[:, h, 1024 + n * C:1024 + (n + 1) * C],
                                               start=(h == 0), stop=(h == CH - 1))
                            mm.then_inc(gkv_ready, 1)
                        return
                    for h in range(CH):
                        mm = pe.matmul(bank(LB[w][3]), loT[:, h, :], wall[:, h, 1024:1536],
                                       start=(h == 0), stop=(h == CH - 1))
                    mm.then_inc(gkv_ready, 1)

                def out_token(w):
                    if w < W4 - 1:
                        pe.wait_ge(gkv_copied, w + 1)
                    for h in range(CH):
                        mm = pe.matmul(bank(LB[w][4], 0, C), loT[:, h, :], projw[:, 2, h, :],
                                       start=(h == 0), stop=(h == CH - 1))
                    mm.then_inc(mod_ready, 1)

                def local_steps(w):
                    return [lambda: agg_turned(w), lambda: local_out(w), None, lambda: lo_turned(w),
                            lambda: keys_values(w), lambda: out_token(w)]

                pe.wait_ge(s_conv, 32)
                embedding(0)
                for i in range(2):
                    offset(i)
                for i in range(2):
                    mean(i)
                pe.wait_ge(s_brow, 2)
                pe.wait_ge(s_wready, 4)
                pe.wait_ge(s_const, 4)
                tokens(0)
                embedding(1, [lambda: offset(2), None, lambda: offset(3), None, lambda: mean(2), lambda: mean(3)])
                tokens(1)
                embedding(2, local_steps(0))
                tokens(2)
                embedding(3, local_steps(1))
                tokens(3)
                pe.wait_ge(emb_free, 2 + 6 * W4)
                for h in range(CH):
                    mm = pe.matmul(bank(0, 0, C), col("cls", h).to_broadcast([P, P]), wall[:, h, C:2 * C],
                                   start=(h == 0), stop=(h == CH - 1))
                mm.then_inc(gq_ready, 1)
                agg_turned(2)
                local_out(2)
                keep_clock(2, 1)
                lo_turned(2)
                keys_values(2)
                pe.wait_ge(kv_free, 2 + K9 * W4)
                pe.wait_ge(tr_free, 2 + 10 * W4)
                turned_sum(1, 512 + C, PARTS3, prod_ready, 0).then_inc(aT_ready, 1)
                out_token(2)
                local_out(3)
                keep_clock(3, 1)
                lo_turned(3)
                keys_values(3)
                out_token(3)
                pe.wait_ge(gq_read, 1)
                turned_sum(0, 1024 + C, [(0, 2), (2, W4)], gag_ready, 3).then_inc(gaT_ready, 1)
                pe.wait_ge(gaT_copied, 1)
                pe.wait_ge(mod_copied, W4 - 1)
                for h in range(CH):
                    mm = pe.matmul(bank(7, 0, C), gaT[:, h, :], projw[:, 1, h, :], start=(h == 0), stop=(h == CH - 1))
                mm.then_inc(cls_ready, 1)
                for t in range(L):
                    if t == L - 1:
                        keep_clock(2, 5)
                    pe.wait_ge(xn_ready, t + 1)
                    for h in range(CH):
                        mm = pe.transpose(ps[:, h * 1024 + t * B:h * 1024 + (t + 1) * B], xn[:, t, h * P:(h + 1) * P],
                                          ident[:, :])
                mm.then_inc(xnT_ready, 1)

            @block.scalar
            def _(act):
                act.sem_inc(emb_free, 2)
                act.sem_inc(kv_free, 2)
                act.sem_inc(red_kept, 2)

                def copy_offset(i):
                    s, b_, _ = PREP[i]
                    o, n = SEG[s]
                    act.wait_ge(s_bias, i + 1)
                    act.activation(brow[:, o:o + n], bank(b_, 0, n), ACT.Copy).then_inc(s_brow, 1)

                def embedded(w, between=()):
                    q = w % 2
                    for c in range(EC):
                        for h in range(CH):
                            j = c * CH + h
                            for f in (between[j] if j < len(between) else ()):
                                f()
                            act.wait_ge(emb_ready, 6 * w + j + 1)
                            act.activation(peT[:, q, h, c * EN:(c + 1) * EN], bank(T_EMB + j % 2, 0, EN),
                                           ACT.Copy).then_inc(emb_free, 1)

                def keys_values(w):
                    q = w % 2
                    act.wait_ge(kvs_free, w + 1)
                    for t in range(K9):
                        act.wait_ge(kv_ready, 9 * w + t + 1)
                        act.activation(kvs[:, q, t, :], bank(T_KV + (q + t) % 2), ACT.Copy).then_inc(kv_free, 1)
                        if t == 5:
                            act.wait_ge(red_ready, w + 1)
                            act.activation(redT[:, w, :, :], redw[:, q, :, :], ACT.Copy).then_inc(red_kept, 1)

                def exponential(w):
                    act.wait_ge(sc_ready, w + 1)
                    act.activation(ex[:, :, :], sc[:, :, :], ACT.Exp, scale=QSCALE).then_inc(ex_ready, 1)

                def agg_copied(w):
                    act.wait_ge(aT_ready, w + 1)
                    act.activation(aggT[:, :, :], bank(LB[w][0], 0, C), ACT.Copy).then_inc(aT_copied, 1)

                def lo_copied(w):
                    act.wait_ge(lT_ready, w + 1)
                    act.activation(loT[:, :, :], bank(LB[w][2], 0, C), ACT.Copy).then_inc(lT_copied, 1)

                def kv_copied(w):
                    act.wait_ge(gkv_ready, w + 1)
                    act.activation(gkvs[:, w, :], bank(LB[w][3]), ACT.Copy).then_inc(gkv_copied, 1)

                embedded(0)
                copy_offset(0)
                copy_offset(1)
                keys_values(0)
                embedded(1, [[lambda: copy_offset(2)], [], [lambda: exponential(0), lambda: copy_offset(3)]])
                keys_values(1)
                for w in (2, 3):
                    embedded(w, [[lambda: agg_copied(w - 2)], [], [lambda: exponential(w - 1)], [lambda: lo_copied(w - 2)],
                                 [lambda: kv_copied(w - 2)]])
                    keys_values(w)
                act.wait_ge(gq_ready, 1)
                act.activation(gqraw[:, :], bank(0, 0, C), ACT.Copy).then_inc(gq_read, 1)
                agg_copied(2)
                exponential(3)
                lo_copied(2)
                kv_copied(2)
                act.wait_ge(aT_ready, W4)
                act.activation(aggT[:, :, :], halves(1), ACT.Copy).then_inc(aT_copied, 1)
                lo_copied(3)
                act.wait_ge(gkv_ready, W4 + 1)
                act.activation(gkvs[:, W4 - 1, C:2 * C], bank(LB[3][3] + 1, 0, C), ACT.Copy).then_inc(gkv_copied, 1)
                act.wait_ge(gsc_ready, 1)
                act.activation(gex[:, :, :], gsc[:, :, :], ACT.Exp, scale=QSCALE).then_inc(gex_ready, 1)
                act.wait_ge(gaT_ready, 1)
                act.activation(gaT[:, :, :], halves(0), ACT.Copy).then_inc(gaT_copied, 1)

            @block.vector
            def _(dve):
                ch = Chain(dve, d_chain)
                dve.memset(onesc[:, :], 1.0 / C)
                dve.sem_inc(tr_free, 2)
                dve.sem_inc(kvs_free, 2)
                dve.sem_inc(q_free, 1)

                def gain(i):
                    s = PREP[i][0]
                    o, n = SEG[s]
                    dve.wait_ge(s_bias, i + 1)
                    for h in range(CH):
                        dve.tensor_scalar(wall[:, h, o:o + n], wall[:, h, o:o + n], col(s + "_g", h), None,
                                          ALU.mult).then_inc(s_wg, 1)

                def centre(i):
                    s, _, b_ = PREP[i]
                    o, n = SEG[s]
                    dve.wait_ge(s_wg, 2 * i + 2)
                    dve.wait_ge(s_wmean, i + 1)
                    for h in range(CH):
                        dve.tensor_tensor(wall[:, h, o:o + n], wall[:, h, o:o + n], bank(b_, 0, n),
                                          ALU.subtract).then_inc(s_wready, 1)

                def window_mean(w):
                    q = w % 2
                    dve.wait_ge(emb_free, 2 + 6 * w + 6)
                    dve.wait_ge(red_kept, w + 1)
                    ch.link(dve.tensor_reduce(redw[:, q, :, :],
                                              peT[:, q, :, :].rearrange("p h (k b) -> p h b k", k=K9), AX.X, ALU.add))
                    dve.tensor_scalar(redw[:, q, :, :], redw[:, q, :, :], 1.0 / K9, None,
                                      ALU.mult).then_inc(red_ready, 1)

                def stats(w, u):
                    dve.wait_ge(tr_ready, 10 * w + u + 1)
                    t = K9 if u == RED_AT else u - (u > RED_AT)
                    dve.bn_stats(st[:, t, :], bank(T_TR + u % 2, 0, C)).then_inc(tr_free, 1)

                def query(w):
                    dve.wait_ge(rstd_ready, 2 * w + 1)
                    dve.wait_ge(q_ready, w + 1)
                    dve.wait_ge(s_brow, 2)
                    dve.scalar_tensor_tensor(out=qn[:, :], in0=bank(T_Q, 0, C), scalar=rstd[:, K9:K9 + 1],
                                             in1=brow[:, 0:C], op0=ALU.mult, op1=ALU.add).then_inc(q_free, 1)
                    dve.wait_ge(q_free, w + 2)

                def multiplied(w, lo_, hi_):
                    dve.wait_ge(kv_free, 2 + 9 * w + hi_)
                    return ch.mark(dve.tensor_tensor(prod[:, lo_:hi_, :], kvs[:, w % 2, lo_:hi_, 0:C],
                                                     qn[:, :].unsqueeze(1).to_broadcast([P, hi_ - lo_, C]), ALU.mult))

                def scored(w, lo_, hi_, mark):
                    ch.upto(mark)
                    return ch.mark(dve.tensor_reduce(sc[:, lo_:hi_, :].rearrange("p k h -> p (k h)"),
                                                     prod[:, lo_:hi_, :].rearrange("p k (h d) -> p (k h) d", h=H), AX.X, ALU.add))

                def attention_begin(w):
                    window_mean(w)
                    for u in range(RED_AT + 1):
                        stats(w, u)
                    dve.wait_ge(tr_free, 2 + 10 * w + RED_AT + 1)
                    ch.link(dve.bn_aggr(mv[:, K9, :], st[:, K9, :]))
                    dve.tensor_scalar(veps[:, K9:K9 + 1], mv[:, K9:K9 + 1, 1], EPS, None, ALU.add).then_inc(veps_ready, 1)
                    stats(w, 4)
                    query(w)
                    stats(w, 5)
                    m_q = ch.mark(dve.tensor_tensor(prod[:, K9 - 1, :], qn[:, :], brow[:, 512:512 + C], ALU.mult))
                    m_0 = multiplied(w, 0, 3)
                    stats(w, 6)
                    ch.upto(m_q)
                    ch.mark(dve.tensor_reduce(qb[:, :], prod[:, K9 - 1, :].rearrange("p (h d) -> p h d", h=H), AX.X, ALU.add))
                    scored(w, 0, 3, m_0)
                    stats(w, 7)
                    m_1 = multiplied(w, 3, 6)
                    stats(w, 8)
                    scored(w, 3, 6, m_1)
                    stats(w, 9)
                    dve.wait_ge(tr_free, 2 + 10 * (w + 1))
                    for t in range(K9):
                        last = ch.mark(dve.bn_aggr(mv[:, t, :], st[:, t, :]))
                    m_2 = multiplied(w, 6, 9)
                    ch.upto(last)
                    dve.tensor_scalar(veps[:, 0:K9], mv[:, 0:K9, 1], EPS, None, ALU.add).then_inc(veps_ready, 1)
                    ch.upto(scored(w, 6, 9, m_2))

                def softmax(w):
                    rk = rstd[:, 0:K9].unsqueeze(2).to_broadcast([P, K9, H])
                    dve.wait_ge(rstd_ready, 2 * w + 2)
                    ch.link(dve.tensor_tensor(sc[:, :, :], sc[:, :, :], rk, ALU.mult))
                    ch.link(dve.tensor_tensor(sc[:, :, :], sc[:, :, :],
                                              qb[:, :].unsqueeze(1).to_broadcast([P, K9, H]), ALU.add))
                    ch.link(dve.tensor_reduce(mx[:, :], sc[:, :, :].rearrange("p k h -> p h k"), AX.X, ALU.max))
                    dve.tensor_tensor(sc[:, :, :], sc[:, :, :], mx[:, :].unsqueeze(1).to_broadcast([P, K9, H]),
                                      ALU.subtract).then_inc(sc_ready, 1)

                def attention_end(w):
                    q = w % 2
                    rk = rstd[:, 0:K9].unsqueeze(2).to_broadcast([P, K9, H])
                    dve.wait_ge(ex_ready, w + 1)
                    ch.link(dve.tensor_reduce(sm[:, :], ex[:, :, :].rearrange("p k h -> p h k"), AX.X, ALU.add))
                    ch.link(dve.reciprocal(sm[:, :], sm[:, :]))
                    ch.link(dve.tensor_tensor(ex[:, :, :], ex[:, :, :],
                                              sm[:, :].unsqueeze(1).to_broadcast([P, K9, H]), ALU.mult))
                    ch.link(dve.tensor_tensor(ex[:, :, :], ex[:, :, :], rk, ALU.mult))
                    dve.wait_ge(kv_free, 2 + 9 * w + 9)
                    if w == W4 - 1:
                        for lo_, hi_ in PARTS3:
                            dve.tensor_tensor(prod[:, lo_:hi_, :].rearrange("p k (h d) -> p (k h) d", h=H),
                                              kvs[:, q, lo_:hi_, C:2 * C].rearrange("p k (h d) -> p k h d", h=H),
                                              ex[:, lo_:hi_, :].unsqueeze(3).to_broadcast([P, hi_ - lo_, H, DH]),
                                              ALU.mult).then_inc(prod_ready, 1)
                        return
                    ch.link(dve.tensor_tensor(prod[:, :, :].rearrange("p k (h d) -> p (k h) d", h=H),
                                              kvs[:, q, :, C:2 * C].rearrange("p k (h d) -> p k h d", h=H),
                                              ex[:, :, :].unsqueeze(3).to_broadcast([P, K9, H, DH]), ALU.mult))
                    dve.sem_inc(kvs_free, 1)
                    ch.link(dve.tensor_reduce(qn[:, :], prod[:, :, :].rearrange("p k c -> p c k"), AX.X, ALU.add))
                    dve.tensor_tensor(agg[:, w, :], qn[:, :], brow[:, 512 + C:1024], ALU.add).then_inc(agg_ready, 1)

                def local(w):
                    g = W4 - 1 - w
                    dve.wait_ge(lo_summed, w + 1)
                    if w == 0:
                        dve.wait_ge(s_proj, 16 * 4)
                    if w >= 2:
                        dve.wait_ge(lT_ready, w - 1)
                    dve.tensor_tensor(lo[:, w % 2, :], bank(LB[w][1], 0, C), row("proj_b", C), ALU.add).then_inc(lo_ready, 1)
                    dve.wait_ge(lo_ready, w + 1)
                    ch.link(dve.bn_stats(gst[:, g, :], lo[:, w % 2, :]))
                    ch.link(dve.bn_aggr(gmv[:, g, :], gst[:, g, :]))

                def token_out(w):
                    dve.wait_ge(mod_ready, w + 1)
                    dve.tensor_tensor(hbuf[:, w, :], bank(LB[w][4], 0, C), row("mod_b", C), ALU.add).then_inc(mod_copied, 1)

                def token_stats(lo_, hi_):
                    marks = [ch.mark(dve.bn_stats(xst[:, t, :], hbuf[:, t, :])) for t in range(lo_, hi_)]
                    for t, k in zip(range(lo_, hi_), marks):
                        ch.upto(k)
                        last = ch.mark(dve.bn_aggr(xmv[:, t, :], xst[:, t, :]))
                    ch.upto(last)
                    dve.tensor_scalar(xv[:, lo_:hi_], xmv[:, lo_:hi_, 1], 1.0 + EPS, EPS * EPS, ALU.mult,
                                      ALU.add).then_inc(xv_ready, 1)

                def token_normed(lo_, hi_, k):
                    dve.wait_ge(xr_ready, k)
                    for t in range(lo_, hi_):
                        dve.tensor_scalar(xn[:, t, :], hbuf[:, t, :], xmv[:, t, 0:1], xr[:, t:t + 1], ALU.subtract,
                                          ALU.mult).then_inc(xn_ready, 1)

                dve.wait_ge(s_vec, 32)
                gain(0)
                gain(1)
                centre(0)
                centre(1)
                dve.wait_ge(s_wready, 4)
                attention_begin(0)
                softmax(0)
                gain(2)
                gain(3)
                attention_end(0)
                centre(2)
                centre(3)
                for w in (1, 2):
                    attention_begin(w)
                    softmax(w)
                    local(w - 1)
                    attention_end(w)
                    token_out(w - 1)
                attention_begin(3)
                softmax(3)
                local(2)
                ch.link(dve.bn_stats(gst[:, W4, :], row("cls", C)))
                ch.link(dve.bn_aggr(gmv[:, W4, :], gst[:, W4, :]))
                dve.tensor_scalar(gve[:, 1:W4 + 1], gmv[:, 1:W4 + 1, 1], EPS, None, ALU.add).then_inc(gve_ready, 1)
                attention_end(3)
                dve.wait_ge(gq_read, 1)
                dve.wait_ge(grs_ready, 1)
                dve.wait_ge(s_brow, 4)
                ch.link(dve.scalar_tensor_tensor(out=gqn[:, :], in0=gqraw[:, :], scalar=grs[:, W4:W4 + 1],
                                                 in1=brow[:, C:2 * C], op0=ALU.mult, op1=ALU.add))

                def class_scores(lo_, hi_, keys):
                    ch.link(dve.tensor_tensor(prod[:, lo_:hi_, :], keys,
                                              gqn[:, :].unsqueeze(1).to_broadcast([P, hi_ - lo_, C]), ALU.mult))
                    ch.link(dve.tensor_reduce(gsc[:, lo_:hi_, :].rearrange("p k h -> p (k h)"),
                                              prod[:, lo_:hi_, :].rearrange("p k (h d) -> p (k h) d", h=H), AX.X, ALU.add))

                dve.wait_ge(aT_ready, W4)
                m_b = ch.mark(dve.tensor_tensor(prod[:, K9 - 1, :], gqn[:, :], brow[:, 1024:1024 + C], ALU.mult))
                dve.wait_ge(gkv_copied, W4 - 1)
                class_scores(0, W4 - 1, gkvs[:, 0:W4 - 1, 0:C])
                local(3)
                dve.tensor_scalar(gve[:, 0:1], gmv[:, 0:1, 1], EPS, None, ALU.add).then_inc(gve_ready, 1)
                token_out(2)
                ch.upto(m_b)
                ch.mark(dve.tensor_reduce(gqb[:, :], prod[:, K9 - 1, :].rearrange("p (h d) -> p h d", h=H), AX.X, ALU.add))
                ch.mark(dve.tensor_tensor(qn[:, :], row("gproj_b", C), row("cls", C), ALU.add))
                dve.wait_ge(mod_copied, W4 - 1)
                token_stats(0, W4 - 1)
                dve.wait_ge(gkv_ready, W4)
                class_scores(W4 - 1, W4, bank(LB[3][3], 0, C).unsqueeze(1))
                dve.wait_ge(grs_ready, 2)

                def by_rstd(dst, src):
                    for w in range(W4):
                        ins = dve.tensor_scalar(dst[:, w, :], src[:, w, :], grs[:, W4 - 1 - w:W4 - w], None, ALU.mult)
                    ch.link(ins)

                by_rstd(gsc, gsc)
                ch.link(dve.tensor_tensor(gsc[:, :, :], gsc[:, :, :], gqb[:, :].unsqueeze(1).to_broadcast([P, W4, H]), ALU.add))
                ch.link(dve.tensor_reduce(gmx[:, :], gsc[:, :, :].rearrange("p k h -> p h k"), AX.X, ALU.max))
                dve.tensor_tensor(gsc[:, :, :], gsc[:, :, :], gmx[:, :].unsqueeze(1).to_broadcast([P, W4, H]),
                                  ALU.subtract).then_inc(gsc_ready, 1)
                token_normed(0, 1, 1)
                dve.wait_ge(gex_ready, 1)
                ch.link(dve.tensor_reduce(gmx[:, :], gex[:, :, :].rearrange("p k h -> p h k"), AX.X, ALU.add))
                ch.link(dve.reciprocal(gmx[:, :], gmx[:, :]))
                ch.link(dve.tensor_tensor(gex[:, :, :], gex[:, :, :], gmx[:, :].unsqueeze(1).to_broadcast([P, W4, H]), ALU.mult))
                by_rstd(gex, gex)
                dve.wait_ge(gkv_copied, W4)
                for lo_, hi_ in ((0, 2), (2, W4)):
                    dve.tensor_tensor(prod[:, lo_:hi_, :].rearrange("p k (h d) -> p (k h) d", h=H),
                                      gkvs[:, lo_:hi_, C:2 * C].rearrange("p k (h d) -> p k h d", h=H),
                                      gex[:, lo_:hi_, :].unsqueeze(3).to_broadcast([P, hi_ - lo_, H, DH]),
                                      ALU.mult).then_inc(gag_ready, 1)
                token_normed(1, W4 - 1, 1)
                token_out(3)
                dve.wait_ge(mod_copied, W4)
                token_stats(W4 - 1, W4)
                token_normed(W4 - 1, W4, 2)
                dve.wait_ge(cls_ready, 1)
                ch.link(dve.tensor_tensor(hbuf[:, W4, :], bank(7, 0, C), qn[:, :], ALU.add))
                token_stats(W4, L)
                token_normed(W4, L, 3)
        tok.close()

        siluz = sb("siluz", [P, 2, L, DI])
        skip = sb("skip", [P, 2, L, DI])
        CT = sb("CT", [P, 2, L, B])
        pre = ExitStack()
        xnT = sb("xnT", [P, CH, L * B], ctx=pre)
        xcT = sb("xcT", [P, 2, DC, L * B], ctx=pre)
        acc = sb("acc", [P, 2, L * B], ctx=pre)
        dbl = sb("dbl", [NX, 2, L * B], ctx=pre)
        dtT = sb("dtT", [33, 2, L * B], ctx=pre)
        bct = sb("bct", [P, 2, L, NX], ctx=pre)
        cbp = sb("cbp", [P, L, NS], ctx=pre)
        cb = sb("cb", [P, 2, L], ctx=pre)
        bd = sb("bd", [P, L, GB, NS], ctx=pre)
        cd = sb("cd", [P, L, GB, NS], ctx=pre)
        bhi = sb("bhi", [P, L * P], BF16, ctx=pre)
        bmi = sb("bmi", [P, L * P], BF16, ctx=pre)
        blo = sb("blo", [P, L * P], BF16, ctx=pre)
        diagD = sb("diagD", [P, 2, DC, P], ctx=pre)
        NDV = 5
        NR = 3
        NZ = 7
        ez = sb("ez", [P, NZ, DI], ctx=pre)
        rc = sb("rc", [P, NZ, DI], ctx=pre)
        delta = sb("delta", [P, 2, DI], ctx=pre)
        dres = sb("dres", [P, 2, DI], ctx=pre)
        uu = sb("uu", [P, 2, DI], ctx=pre)
        ures = sb("ures", [P, 2, DI], ctx=pre)
        dpt = sb("dpt", [P, NR, 3, DI], BF16, ctx=pre)
        upt = sb("upt", [P, NR, 3, DI], BF16, ctx=pre)
        bz = sb("bz", [P, L * P], BF16, ctx=pre)
        bz_ready = sem("bz_ready")
        diag_ready, xnT_copied, x_chain = sem("diag_ready"), sem("xnT_copied"), sem("x_chain")
        xi_ready, acc_begun, acc_ready, xc_ready = sem("xi_ready"), sem("acc_begun"), sem("acc_ready"), sem("xc_ready")
        z_ready, z_copied, dbl_ready, dbl_copied = sem("z_ready"), sem("z_copied"), sem("dbl_ready"), sem("dbl_copied")
        dtT_zero, dtT_ones, bc_ready, bct_ready = sem("dtT_zero"), sem("dtT_ones"), sem("bc_ready"), sem("bct_ready")
        cd_ready, cdT_ready, CT_ready = sem("cd_ready"), sem("cdT_ready"), sem("CT_ready")
        bd_ready, bhi_ready, bres_ready, bmi_ready = sem("bd_ready"), sem("bhi_ready"), sem("bres_ready"), sem("bmi_ready")
        blo_ready, b_stored = sem("blo_ready"), sem("b_stored")
        dp_ready, xt_ready, ab_done, ez_ready, ln_ready = sem("dp_ready"), sem("xt_ready"), sem("ab_done"), sem("ez_ready"), sem("ln_ready")
        rc_ready, delta_ready, u_ready, skip_ready = sem("rc_ready"), sem("delta_ready"), sem("u_ready"), sem("skip_ready")
        dres_ready, dhi_ready, dmi_ready, uhi_ready = sem("dres_ready"), sem("dhi_ready"), sem("dmi_ready"), sem("uhi_ready")
        umi_ready, ures_ready, dlo_ready, ulo_ready = sem("umi_ready"), sem("ures_ready"), sem("dlo_ready"), sem("ulo_ready")
        p_stored = [sem(f"p_stored{r}") for r in range(NR)]
        ITEMS = [(d, t) for d in range(2) for t in range(L)]
        NI = len(ITEMS)
        WIDE = [("xi", 0, 0), ("xi", 1, 1), ("xi", 2, 2), ("xi", 3, 0), ("z", 0, 3), ("xi", 4, 1), ("xi", 5, 0), ("xp", 0, 2),
                ("xi", 6, 1), ("xi", 7, 2), ("bc", 0, 0), ("z", 1, 1), ("z", 2, 0), ("xp", 1, 1),
                ("cd", 0, 0), ("bc", 1, 1), ("xt", 0, 0), ("xt", 1, 1), ("xt", 2, 0), ("xt", 3, 1), ("xt", 4, 0),
                ("dp", 9, 2), ("dp", 9, 3), ("xt", 5, 2), ("cd", 1, 1), ("xt", 6, 0), ("z", 3, 3), ("xt", 7, 2),
                ("z", 4, 1), ("xt", 8, 0), ("z", 5, 3), ("xt", 9, 2), ("z", 6, 1), ("z", 7, 3), ("z", 8, 1), ("z", 9, 3)]

        def place(kind, n):
            return [w[:2] for w in WIDE].index((kind, n))

        def slot(kind, n):
            return 1024 * WIDE[place(kind, n)][2]

        with nc.Block() as block:
            @block.tensor
            def _(pe):
                pe.wait_ge(xnT_copied, CH)

                def xi(n, o):
                    d, c = divmod(n, DC)
                    for lo_, hi_ in ((0, 512), (512, L * B)):
                        for h in range(CH):
                            mm = pe.matmul(ps[:, o + lo_:o + hi_], inw[:, d, h, c * P:(c + 1) * P],
                                           xnT[:, h, lo_:hi_], start=(h == 0), stop=(h == CH - 1))
                    mm.then_inc(xi_ready, 1)

                def z(n, o):
                    d, t = ITEMS[n]
                    for h in range(CH):
                        mm = pe.matmul(ps[:, o:o + DI], xnT[:, h, t * B:(t + 1) * B], inw[:, d, h, DI:2 * DI],
                                       start=(h == 0), stop=(h == CH - 1))
                    mm.then_inc(z_ready, 1)

                def xp(d, o):
                    pe.wait_ge(xc_ready, (d + 1) * DC)
                    for lo_, hi_ in ((0, 512), (512, L * B)):
                        for c in range(DC):
                            mm = pe.matmul(ps[0:NX, o + lo_:o + hi_], xpw[:, d, c, :], xcT[:, d, c, lo_:hi_],
                                           start=(c == 0), stop=(c == DC - 1))
                    mm.then_inc(dbl_ready, 1)

                def bc(d, o):
                    pe.wait_ge(dbl_copied, 2 * d + 1)
                    for t in range(L):
                        mm = pe.transpose(ps[:, o + t * NX:o + (t + 1) * NX], dbl[:, d, t * B:(t + 1) * B],
                                          ident[0:NX, 0:NX])
                    mm.then_inc(bc_ready, 1)

                def cd_(d, o):
                    pe.wait_ge(cd_ready, d + 1)
                    for t in range(L):
                        mm = pe.transpose(ps[:, o + t * P:o + (t + 1) * P], cd[:, t, :, :].rearrange("p g n -> p (g n)"),
                                          ident[:, :])
                    mm.then_inc(cdT_ready, 1)

                def xt(n, o):
                    d, t = ITEMS[n]
                    if n == 0:
                        pe.wait_ge(diag_ready, 2 * DC)
                    for c in range(DC):
                        pe.transpose(ps[:, o + c * P:o + (c + 1) * P], xcT[:, d, c, t * B:(t + 1) * B], ident[:, :])
                    for c in range(DC):
                        mm = pe.matmul(ps[:, o + DI + c * P:o + DI + (c + 1) * P], xcT[:, d, c, t * B:(t + 1) * B],
                                       diagD[:, d, c, :], start=True, stop=True)
                    mm.then_inc(xt_ready, 1)

                make = {"xi": xi, "z": z, "xp": xp, "bc": bc, "cd": cd_, "xt": xt}
                read = {"xi": (acc_ready, 1), "z": (z_copied, 1), "xp": (dbl_copied, 2), "bc": (bct_ready, 1),
                        "cd": (CT_ready, 1), "xt": (skip_ready, 1), "dp": (rc_ready, 1)}

                def tenant_read(s_, k):
                    before = [w for w in WIDE[:k] if w[2] == s_]
                    if before:
                        kind, m, _ = before[-1]
                        pe.wait_ge(read[kind][0], read[kind][1] * (m + 1))

                def wide(kind, n):
                    k = place(kind, n)
                    tenant_read(WIDE[k][2], k)
                    make[kind](n, slot(kind, n))

                def dt_product(n):
                    d, t = ITEMS[n]
                    if n == 0:
                        pe.wait_ge(dtT_ones, 1)
                        tenant_read(2, place("xp", 1))
                        tenant_read(3, place("xp", 1))
                    pe.wait_ge(dbl_copied, 2 * d + 2)
                    if n >= 4:
                        pe.wait_ge(rc_ready, n - 3)
                    mm = pe.matmul(bank(4 + n % 4), dtT[:, d, t * B:(t + 1) * B], dtw[:, d, :], start=True, stop=True)
                    mm.then_inc(dp_ready, 1)

                for w in WIDE[:place("xp", 1)]:
                    wide(*w[:2])
                for n in range(4):
                    dt_product(n)
                wide("xp", 1)
                wide("cd", 0)
                dt_product(4)
                wide("bc", 1)
                wide("xt", 0)
                for n in range(5, 9):
                    dt_product(n)
                wide("xt", 1)
                wide("xt", 2)
                dt_product(9)
                for w in WIDE[place("xt", 3):]:
                    if w[0] != "dp":
                        wide(*w[:2])

            @block.scalar
            def _(act):
                act.wait_ge(xnT_ready, 1)
                act.activation(xnT[:, 0, :], ps[:, 0:L * B], ACT.Identity,
                               scale=col("ln_g", 0), bias=col("ln_b", 0)).then_inc(xnT_copied, 1)

                def conv_begin(n):
                    d, c = divmod(n, DC)
                    o = slot("xi", n)
                    act.wait_ge(xi_ready, n + 1)
                    if n >= 2:
                        act.wait_ge(xc_ready, n - 1)
                    act.activation(acc[:, n % 2, :], ps[:, o:o + L * B], ACT.Identity,
                                   scale=col(f"cw{d}", 4 * c + 3), bias=col(f"cb{d}", c)).then_inc(acc_begun, 1)

                def conv_end(n):
                    d, c = divmod(n, DC)
                    act.wait_ge(acc_ready, n + 1)
                    act.activation(xcT[:, d, c, :], acc[:, n % 2, :], ACT.Silu).then_inc(xc_ready, 1)

                def silu_z(n):
                    act.wait_ge(z_ready, n + 1)
                    o = slot("z", n)
                    act.activation(siluz[:, ITEMS[n][0], ITEMS[n][1], :], ps[:, o:o + DI], ACT.Silu).then_inc(z_copied, 1)

                def copy_xp(d):
                    act.wait_ge(dbl_ready, d + 1)
                    o = slot("xp", d)
                    act.activation(dbl[:, d, :], ps[0:NX, o:o + L * B], ACT.Copy).then_inc(dbl_copied, 1)
                    if d == 0:
                        act.wait_ge(dtT_ones, 1)
                    act.activation(dtT[0:R, d, :], ps[0:R, o:o + L * B], ACT.Copy).then_inc(dbl_copied, 1)

                def copy_bc(d):
                    act.wait_ge(bc_ready, d + 1)
                    o = slot("bc", d)
                    act.activation(bct[:, d, :, :].rearrange("p t n -> p (t n)"), ps[:, o:o + L * NX],
                                   ACT.Copy).then_inc(bct_ready, 1)

                def copy_cd(d):
                    act.wait_ge(cdT_ready, d + 1)
                    o = slot("cd", d)
                    act.activation(CT[:, d, :, :], ps[:, o:o + L * B], ACT.Copy).then_inc(CT_ready, 1)

                flat = bd[:, :, :, :].rearrange("p t g n -> p (t g n)")

                def b_high(d):
                    act.wait_ge(bd_ready, d + 1)
                    if d == 1:
                        act.wait_ge(b_stored, 128)
                    act.activation(bhi[:, :], flat, ACT.Copy).then_inc(bhi_ready, 1)

                def b_middle(d):
                    act.wait_ge(bres_ready, d + 1)
                    act.activation(bmi[:, :], flat, ACT.Copy).then_inc(bmi_ready, 1)

                def absolute(n):
                    act.wait_ge(dp_ready, n + 1)
                    if n >= NZ:
                        act.wait_ge(delta_ready, n - NZ + 1)
                    act.activation(ez[:, n % NZ, :], bank(4 + n % 4), ACT.Abs).then_inc(ab_done, 1)

                def exponential(n):
                    act.wait_ge(ab_done, n + 1)
                    act.activation(ez[:, n % NZ, :], ez[:, n % NZ, :], ACT.Exp, scale=-1.0).then_inc(ez_ready, 1)

                def logarithm(n):
                    act.wait_ge(rc_ready, n + 1)
                    act.activation(ez[:, n % NZ, :], ez[:, n % NZ, :], ACT.Ln, bias=1.0).then_inc(ln_ready, 1)

                def delta_high(n):
                    act.wait_ge(delta_ready, n + 1)
                    if n >= NR:
                        act.wait_ge(p_stored[n % NR], 32 * (n // NR))
                    act.activation(dpt[:, n % NR, 0, :], delta[:, n % 2, :], ACT.Copy).then_inc(dhi_ready, 1)

                def u_high(n):
                    act.wait_ge(u_ready, n + 1)
                    act.activation(upt[:, n % NR, 0, :], uu[:, n % 2, :], ACT.Copy).then_inc(uhi_ready, 1)

                def middle(n):
                    q, r = n % 2, n % NR
                    act.wait_ge(dres_ready, n + 1)
                    act.activation(dpt[:, r, 1, :], dres[:, q, :], ACT.Copy).then_inc(dmi_ready, 1)
                    act.wait_ge(ures_ready, n + 1)
                    act.activation(upt[:, r, 1, :], ures[:, q, :], ACT.Copy).then_inc(umi_ready, 1)

                conv_begin(0)
                conv_begin(1)
                conv_end(0)
                conv_begin(2)
                conv_end(1)
                conv_begin(3)
                conv_end(2)
                conv_begin(4)
                silu_z(0)
                conv_end(3)
                conv_begin(5)
                for d in range(2):
                    for c in range(DC):
                        act.activation(diagD[:, d, c, :], ident[:, :], ACT.Identity, scale=col(f"D{d}", c)).then_inc(diag_ready, 1)
                copy_xp(0)
                conv_end(4)
                conv_begin(6)
                conv_end(5)
                conv_begin(7)
                conv_end(6)
                copy_bc(0)
                conv_end(7)
                silu_z(1)
                silu_z(2)
                for n in range(4):
                    absolute(n)
                    exponential(n)
                act.activation(expA[:, :, :], expA[:, :, :], ACT.Exp).then_inc(expA_ready, 1)
                b_high(0)
                copy_cd(0)
                copy_xp(1)
                absolute(4)
                exponential(4)
                copy_bc(1)
                for n in range(5):
                    logarithm(n)
                delta_high(0)
                for n in range(5):
                    absolute(n + 5)
                    u_high(n)
                    exponential(n + 5)
                    if n < 4:
                        delta_high(n + 1)
                    middle(n)
                    if n == 0:
                        b_middle(0)
                    if n == 3:
                        b_high(1)
                for n in range(5, NI):
                    logarithm(n)
                delta_high(5)
                copy_cd(1)
                b_middle(1)
                for n in range(5, NI):
                    u_high(n)
                    if n > 5:
                        silu_z(n - 3)
                    if n < NI - 1:
                        delta_high(n + 1)
                    middle(n)
                for n in range(7, NI):
                    silu_z(n)

            @block.gpsimd
            def _(pool):
                pool.memset(bz[:, :], 0.0).then_inc(bz_ready, 1)
                pool.memset(dtT[:, :, :], 0.0).then_inc(dtT_zero, 1)
                pool.wait_ge(dtT_zero, 1)
                pool.memset(dtT[32:33, :, :], 1.0).then_inc(dtT_ones, 1)
                pool.wait_ge(dtT_ones, 1)
                mask4 = maskb[:, :, :].unsqueeze(1).to_broadcast([P, L, GB, NS])
                flat = bd[:, :, :, :].rearrange("p t g n -> p (t g n)")

                def b_spread(d):
                    pool.wait_ge(bct_ready, d + 1)
                    if d == 1:
                        pool.wait_ge(blo_ready, 1)
                    pool.tensor_tensor(bd[:, :, :, :], bct[:, d, :, R:R + NS].unsqueeze(2).to_broadcast([P, L, GB, NS]),
                                       mask4, ALU.mult).then_inc(bd_ready, 1)

                def c_spread(d):
                    pool.wait_ge(bct_ready, d + 1)
                    if d == 1:
                        pool.wait_ge(cdT_ready, 1)
                    pool.tensor_tensor(cd[:, :, :, :], bct[:, d, :, R + NS:NX].unsqueeze(2).to_broadcast([P, L, GB, NS]),
                                       mask4, ALU.mult).then_inc(cd_ready, 1)

                def b_rest(d):
                    pool.wait_ge(bhi_ready, d + 1)
                    pool.wait_ge(bd_ready, d + 1)
                    pool.tensor_tensor(flat, flat, bhi[:, :], ALU.subtract).then_inc(bres_ready, 1)

                def b_low(d):
                    pool.wait_ge(bmi_ready, d + 1)
                    pool.wait_ge(bres_ready, d + 1)
                    pool.tensor_tensor(blo[:, :], flat, bmi[:, :], ALU.subtract).then_inc(blo_ready, 1)

                def rest(n):
                    q, r = n % 2, n % NR
                    pool.wait_ge(uhi_ready, n + 1)
                    if n >= 2:
                        pool.wait_ge(umi_ready, n - 1)
                        pool.wait_ge(ulo_ready, n - 1)
                    pool.tensor_tensor(ures[:, q, :], uu[:, q, :], upt[:, r, 0, :], ALU.subtract).then_inc(ures_ready, 1)

                def low(n):
                    q, r = n % 2, n % NR
                    pool.wait_ge(dmi_ready, n + 1)
                    pool.tensor_tensor(dpt[:, r, 2, :], dres[:, q, :], dpt[:, r, 1, :], ALU.subtract).then_inc(dlo_ready, 1)
                    if n < NDV:
                        pool.wait_ge(umi_ready, n + 1)
                        pool.wait_ge(ures_ready, n + 1)
                        pool.tensor_tensor(upt[:, r, 2, :], ures[:, q, :], upt[:, r, 1, :], ALU.subtract).then_inc(ulo_ready, 1)

                b_spread(0)
                c_spread(0)
                b_rest(0)
                c_spread(1)
                for n in range(NI):
                    rest(n)
                    low(n)
                    if n == 0:
                        b_low(0)
                    if n == 2:
                        b_spread(1)
                    if n == 4:
                        b_rest(1)
                    if n == 5:
                        b_low(1)

            @block.vector
            def _(dve):
                ch = Chain(dve, x_chain)
                dve.wait_ge(xnT_ready, 1)
                dve.tensor_scalar(xnT[:, 1, :], ps[:, 1024:1024 + L * B], col("ln_g", 1), col("ln_b", 1),
                                  ALU.mult, ALU.add).then_inc(xnT_copied, 1)
                for n in range(2 * DC):
                    d, c = divmod(n, DC)
                    dve.wait_ge(acc_begun, n + 1)
                    for back in range(1, 4):
                        m = (L - back) * B
                        o = back * B
                        at = slot("xi", n) + (0 if d == 0 else o)
                        dst = acc[:, n % 2, (o if d == 0 else 0):(o if d == 0 else 0) + m]
                        ins = dve.scalar_tensor_tensor(out=dst, in0=ps[:, at:at + m], scalar=col(f"cw{d}", 4 * c + 3 - back),
                                                       in1=dst, op0=ALU.mult, op1=ALU.add)
                        if back < 3:
                            ch.link(ins)
                        else:
                            ins.then_inc(acc_ready, 1)

                def c_dot_b(d):
                    dve.wait_ge(bct_ready, d + 1)
                    ch.link(dve.tensor_tensor(cbp[:, :, :], bct[:, d, :, R:R + NS], bct[:, d, :, R + NS:NX], ALU.mult))
                    return ch.mark(dve.tensor_reduce(cb[:, d, :], cbp[:, :, :], AX.X, ALU.add))

                def lost_1(n):
                    dve.wait_ge(ez_ready, n + 1)
                    return ch.mark(dve.tensor_scalar(rc[:, n % NZ, :], ez[:, n % NZ, :], 1.0, -1.0, ALU.add, ALU.add))

                def lost_2(n, mark):
                    ch.upto(mark)
                    return ch.mark(dve.tensor_tensor(rc[:, n % NZ, :], ez[:, n % NZ, :], rc[:, n % NZ, :], ALU.subtract))

                def lost_3(n, mark):
                    ch.upto(mark)
                    dve.scalar_tensor_tensor(out=rc[:, n % NZ, :], in0=bank(4 + n % 4), scalar=0.0, in1=rc[:, n % NZ, :],
                                             op0=ALU.max, op1=ALU.add).then_inc(rc_ready, 1)

                def delta_(n):
                    q = n % 2
                    dve.wait_ge(ln_ready, n + 1)
                    dve.wait_ge(rc_ready, n + 1)
                    if n >= 2:
                        dve.wait_ge(dhi_ready, n - 1)
                        dve.wait_ge(dres_ready, n - 1)
                    dve.tensor_tensor(delta[:, q, :], rc[:, n % NZ, :], ez[:, n % NZ, :], ALU.add).then_inc(delta_ready, 1)

                def u_(n):
                    q = n % 2
                    dve.wait_ge(delta_ready, n + 1)
                    dve.wait_ge(xt_ready, n + 1)
                    o = slot("xt", n)
                    if n >= 2:
                        dve.wait_ge(ures_ready, n - 1)
                    dve.tensor_tensor(uu[:, q, :], delta[:, q, :], ps[:, o:o + DI], ALU.mult).then_inc(u_ready, 1)

                def rest(n):
                    q = n % 2
                    dve.wait_ge(dhi_ready, n + 1)
                    if n >= 2:
                        dve.wait_ge(dlo_ready, n - 1)
                    dve.tensor_tensor(dres[:, q, :], delta[:, q, :], dpt[:, n % NR, 0, :], ALU.subtract).then_inc(dres_ready, 1)

                def skip_(n):
                    d, t = ITEMS[n]
                    o = slot("xt", n) + DI
                    dve.wait_ge(u_ready, n + 1)
                    dve.scalar_tensor_tensor(out=skip[:, d, t, :], in0=uu[:, n % 2, :], scalar=cb[:, d, t:t + 1],
                                             in1=ps[:, o:o + DI], op0=ALU.mult, op1=ALU.add).then_inc(skip_ready, 1)

                def low(n):
                    q, r = n % 2, n % NR
                    dve.wait_ge(umi_ready, n + 1)
                    dve.tensor_tensor(upt[:, r, 2, :], ures[:, q, :], upt[:, r, 1, :], ALU.subtract).then_inc(ulo_ready, 1)

                cb_done = c_dot_b(0)
                for some in ((0, 1), (2, 3), (4,)):
                    marks = [lost_1(n) for n in some]
                    marks = [lost_2(n, k) for n, k in zip(some, marks)]
                    for n, k in zip(some, marks):
                        lost_3(n, k)
                ch.upto(cb_done)
                delta_(0)
                for n in range(NI):
                    more = n + 5 < NI
                    u_(n)
                    if n not in (4, NI - 1):
                        delta_(n + 1)
                    rest(n)
                    if more:
                        mark = lost_1(n + 5)
                    if n - 1 >= NDV:
                        low(n - 1)
                    if n == 5:
                        ch.upto(cb_done)
                    skip_(n)
                    if more:
                        lost_3(n + 5, lost_2(n + 5, mark))
                    if n == 4:
                        delta_(5)
                    if n == 3:
                        cb_done = c_dot_b(1)
                low(NI - 1)

            @block.sync
            def _(sp):
                def store_b(d):
                    sp.wait_ge(blo_ready, d + 1)
                    for k, src in enumerate([bhi, bhi, bhi, bmi, bmi, blo]):
                        sp.dma_start(bparts[2 * k + d, :, d * L * P:(d + 1) * L * P], src[:, :]).then_inc(b_stored, 16)

                sp.wait_ge(bz_ready, 1)
                for d in range(2):
                    sp.dma_start(bparts[d:12:2, :, (1 - d) * L * P:(2 - d) * L * P].rearrange("k b n -> b k n"),
                                 bz[:, :].unsqueeze(1).to_broadcast([P, 6, L * P])).then_inc(b_stored, 16)
                for n, (d, t) in enumerate(ITEMS):
                    r = n % NR
                    o = t * DI
                    sp.wait_ge(dlo_ready, n + 1)
                    sp.dma_start(dparts[d:6:2, :, o:o + DI].rearrange("k b n -> b k n"), dpt[:, r]).then_inc(p_stored[r], 16)
                    sp.wait_ge(ulo_ready, n + 1)
                    sp.dma_start(uparts[d:6:2, :, o:o + DI].rearrange("k b n -> b k n"), upt[:, r]).then_inc(p_stored[r], 16)
                    if n == 1:
                        store_b(0)
                    if n == 5:
                        store_b(1)
                sp.wait_ge(b_stored, 224)
                for r in range(NR):
                    sp.wait_ge(p_stored[r], 32 * len(range(r, NI, NR)))
        pre.close()

        outw = sb("outw", [P, 2, DC, C])
        expw = sb("expw", [P, CH, E8 * C])
        ytok = sb("ytok", [P, 2, L, DI])
        w_landed, sum_done, gated_done = sem("w_landed"), sem("sum_done"), sem("gated_done")
        y_landed = [sem(f"y_landed{t}") for t in range(L)]
        ORDER = [2, 0, 4, 1, 3]
        NIL = ((0, 0), (L - 1, 1))

        def y_sum(eng, d, t):
            if (t, d) not in NIL:
                eng.wait_ge(y_landed[t], 32 if t in (0, L - 1) else 64)
                eng.tensor_tensor(skip[:, d, t, :], skip[:, d, t, :], ytok[:, d, t, :], ALU.add).then_inc(sum_done, 1)

        scn = ExitStack()
        drows = sb("drows", [KS, 2, L * DI], BF16, ctx=scn)
        urows = sb("urows", [KS, 2, L * DI], BF16, ctx=scn)
        brows = sb("brows", [KS, 2, 2 * L * P], BF16, ctx=scn)
        da = sb("da", [P, 8, DI], ctx=scn)
        gb = sb("gb", [P, 8, DI], ctx=scn)
        hb = sb("hb", [P, 2, 2, DI], ctx=scn)
        cst = sb("cst", [P, 2, 2, L, GB], ctx=scn)
        yst = sb("yst", [P, 2, DI], ctx=scn)
        bu7 = sb("bu7", [P, DI], ctx=scn)
        bu7_copied = sem("bu7_copied")
        d_landed = [sem(f"d_landed{q}") for q in range(2)]
        u_landed = [sem(f"u_landed{q}") for q in range(2)]
        e_ready, e_free, da_ready = sem("e_ready"), sem("e_free"), sem("da_ready")
        bu_ready, bu_used, gp_done = sem("bu_ready"), sem("bu_used"), sem("gp_done")
        c_staged, y_done, y_copied, y_zero = sem("c_staged"), sem("y_done"), sem("y_copied"), sem("y_zero")
        y_stored = [sem(f"y_stored{k}") for k in range(2)]
        d_padded, d_padded_1 = sem("d_padded"), sem("d_padded_1")
        NPAIR = NG // 2
        NGP = 7

        def token(s_, d):
            return s_ if d == 0 else L - 1 - s_

        def pairs(eng, body):
            body(0, True, False)
            with eng.Fori(1, NPAIR - 1) as i:
                body(i, False, False)
            body(NPAIR - 1, False, True)

        with nc.Block() as block:
            @block.sync
            def _(sp):
                def load_rows(g, q):
                    im = bass.ds(g * GB, GB)
                    sp.dma_start(drows[KS // 2:KS, q], dparts[:, im, :]).then_inc(d_landed[q], 16)
                    for lo_, n in ((0, 6), (6, 4), (10, 2)):
                        sp.dma_start(urows[lo_ * GB:(lo_ + n) * GB, q], uparts[0:n, im, :]).then_inc(u_landed[q], 16)
                    sp.dma_start(brows[:, q], bparts[:, im, :]).then_inc(u_landed[q], 16)

                def store_y(g, k):
                    sp.wait_ge(y_copied, 2 + 2 * g + k + 1)
                    sp.dma_start(yscr[bass.ds(g, 1), k], yst[0:NY, k, :]).then_inc(y_stored[k], 16)

                def gather_y(k):
                    sp.wait_ge(y_stored[k], 16 * (NG - 1))
                    for j in range(4):
                        d, s_ = j % 2, 2 * k + 1 + j // 2
                        t = token(s_, d)
                        sp.dma_start(ytok[0:(NG - 1) * GB, d, t, :],
                                     yscr[0:NG - 1, k, 32 * j:32 * j + GB, :]).then_inc(y_landed[t], 16)

                def last_y(k):
                    sp.wait_ge(y_copied, 2 + 2 * (NG - 1) + k + 1)
                    for j in (2, 3, 0, 1):
                        d, s_ = j % 2, 2 * k + 1 + j // 2
                        t = token(s_, d)
                        sp.dma_start(ytok[(NG - 1) * GB:B, d, t, :],
                                     yst[32 * j:32 * j + GB, k, :]).then_inc(y_landed[t], 16)

                load_rows(0, 0)
                load_rows(1, 1)
                for d in range(2):
                    sp.dma_start(outw[:, d], a["out_wT"][d].rearrange("(c p) n -> p c n", p=P)).then_inc(w_landed, 16)
                sp.dma_start(expw[:, :, :], a["expert_wT"].rearrange("(h p) n -> p h n", p=P)).then_inc(w_landed, 16)

                def body(i, first, last):
                    for q in range(2):
                        g = 2 * i + q
                        if not (first and q == 0):
                            store_y(g - 1, 1)
                        if not last:
                            sp.wait_ge(e_ready, 8 * g + 8)
                            sp.wait_ge(bu_ready, 8 * g + 8)
                            load_rows(g + 2, q)
                        if last and q == 1:
                            last_y(0)
                            gather_y(1)
                        else:
                            store_y(g, 0)
                        if last and q == 0:
                            gather_y(0)

                pairs(sp, body)
                last_y(1)
                sp.wait_ge(w_landed, 48)

            @block.tensor
            def _(pe):
                def spread_delta(g, q, j):
                    d, t = j % 2, token(1 + j // 2, j % 2)
                    pe.wait_ge(e_free, 8 * g + j + 1)
                    pe.matmul(bank(j % 2), selb[:, d, :], drows[:, q, t * DI:(t + 1) * DI],
                              start=True, stop=True).then_inc(e_ready, 1)

                def b_times_u(g, q, j):
                    t = token(j // 2, j % 2)
                    o = (j % 2) * L + t
                    if j == 3:
                        pe.wait_ge(bu7_copied, g + 1)
                    else:
                        pe.wait_ge(bu_used, 7 * g + j + (2 if j < 3 else 1))
                    pe.matmul(bank(2 + j % 4), brows[:, q, o * P:(o + 1) * P], urows[:, q, t * DI:(t + 1) * DI],
                              start=True, stop=True).then_inc(bu_ready, 1)

                def outputs(g, q, k):
                    pe.wait_ge(y_copied, 2 * g + k + 1)
                    if k == 0:
                        pe.wait_ge(c_staged, g + 1)
                        pe.wait_ge(bu_used, 4 + 7 * g + 2)
                        pe.wait_ge(gp_done, NGP + NGP * g + 2)
                    else:
                        pe.wait_ge(gp_done, NGP + NGP * g + NGP)
                    for j in range(4):
                        d, s_ = j % 2, 2 * k + 1 + j // 2
                        mm = pe.matmul(ps[32 * j:32 * j + GB, (6 + k) * 512:(7 + k) * 512], cst[:, q, d, token(s_, d), :],
                                       gb[:, 4 * k + j, :], start=True, stop=True)
                    mm.then_inc(y_done, 1)

                pe.wait_ge(d_padded, 1)
                pe.wait_ge(d_landed[0], 16)
                for j in range(4):
                    spread_delta(0, 0, j)
                pe.wait_ge(u_landed[0], 64)
                for j in range(4):
                    b_times_u(0, 0, j)
                spread_delta(0, 0, 4)

                def body(i, first, last):
                    for q in range(2):
                        g = 2 * i + q
                        after = not (last and q == 1)
                        spread_delta(g, q, 5)
                        b_times_u(g, q, 4)
                        spread_delta(g, q, 6)
                        if not (first and q == 0):
                            outputs(g - 1, 1 - q, 1)
                        spread_delta(g, q, 7)
                        b_times_u(g, q, 5)
                        b_times_u(g, q, 6)
                        b_times_u(g, q, 7)
                        if after:
                            pe.wait_ge(d_landed[1 - q], 16 * (i + q) + 16)
                            spread_delta(g + 1, 1 - q, 0)
                            spread_delta(g + 1, 1 - q, 1)
                        outputs(g, q, 0)
                        if after:
                            spread_delta(g + 1, 1 - q, 2)
                            pe.wait_ge(u_landed[1 - q], 64 * (i + q) + 64)
                            b_times_u(g + 1, 1 - q, 0)
                            b_times_u(g + 1, 1 - q, 1)
                            spread_delta(g + 1, 1 - q, 3)
                            b_times_u(g + 1, 1 - q, 2)
                            b_times_u(g + 1, 1 - q, 3)
                            spread_delta(g + 1, 1 - q, 4)

                pe.wait_ge(y_zero, 1)
                pe.wait_ge(d_padded_1, 1)
                def keep_clock(n):
                    for _ in range(n):
                        pe.matmul(bank(0), ident[:, :], expw[:, 0, 0:512], start=True, stop=True)

                pairs(pe, body)
                pe.wait_ge(w_landed, 48)
                pe.wait_ge(e_free, 2 + 8 * NG)
                keep_clock(6)
                outputs(NG - 1, 1, 1)
                keep_clock(3)

            @block.scalar
            def _(act):
                act.sem_inc(y_copied, 2)

                def exponential(g, j):
                    act.wait_ge(e_free, 2 + 8 * g + j + 1)
                    act.activation(da[:, j, :], da[:, j, :], ACT.Exp, scale=-1.0).then_inc(da_ready, 1)

                def copy_y(g, k):
                    act.wait_ge(y_done, 2 + 2 * g + k + 1)
                    act.wait_ge(y_stored[k], 16 * g)
                    act.activation(yst[0:NY, k, :], bank(6 + k, p=NY), ACT.Copy).then_inc(y_copied, 1)

                def stage_c(g, q):
                    act.activation(cst[:, q, :, :, :].rearrange("p d t b -> p (d t) b"),
                                   CT[:, :, :, bass.ds(g * GB, GB)].rearrange("p d t b -> p (d t) b"),
                                   ACT.Copy).then_inc(c_staged, 1)

                def copy_bu7(g):
                    act.wait_ge(bu_ready, 8 * g + 8)
                    act.wait_ge(gp_done, NGP * g + 6)
                    act.activation(bu7[:, :], bank(2 + 7 % 4), ACT.Copy).then_inc(bu7_copied, 1)

                act.sem_inc(bu7_copied, 1)
                for j in range(5):
                    exponential(0, j)

                def body(i, first, last):
                    for q in range(2):
                        g = 2 * i + q
                        after = not (last and q == 1)
                        stage_c(g, q)
                        exponential(g, 5)
                        exponential(g, 6)
                        if not (first and q == 0):
                            copy_y(g - 1, 1)
                        exponential(g, 7)
                        if after:
                            exponential(g + 1, 0)
                        copy_bu7(g)
                        if after:
                            exponential(g + 1, 1)
                        copy_y(g, 0)
                        if after:
                            for j in range(2, 5):
                                exponential(g + 1, j)

                pairs(act, body)
                copy_y(NG - 1, 1)

            @block.gpsimd
            def _(pool):
                pool.sem_inc(gp_done, NGP)
                pool.memset(drows[0:KS // 2, 1, :], 0.0).then_inc(d_padded_1, 1)

                def decayed(g, s_, d):
                    j = 2 * (s_ - 1) + d
                    pool.wait_ge(da_ready, 8 * g + j + 1)
                    if (s_, d) == (4, 1):
                        pool.wait_ge(gp_done, NGP + NGP * g + 6)
                    else:
                        pool.wait_ge(bu_used, 4 + 7 * g + 2 * (s_ - 1) + d + 1)
                    if j == 2:
                        pool.wait_ge(y_done, 2 * g + 1)
                    if j == 4:
                        pool.wait_ge(y_done, 2 * g + 2)
                    pool.tensor_tensor(gb[:, j, :], da[:, j, :], hb[:, d, (s_ - 1) % 2, :], ALU.mult).then_inc(gp_done, 1)

                def state_3(g):
                    pool.wait_ge(bu7_copied, 1 + g + 1)
                    pool.wait_ge(gp_done, NGP + NGP * g + 4)
                    pool.tensor_tensor(hb[:, 1, 1, :], gb[:, 5, :], bu7[:, :], ALU.add).then_inc(gp_done, 1)

                def body(i, first, last):
                    for q in range(2):
                        g = 2 * i + q
                        for s_, d in [(2, 0), (2, 1), (3, 0), (3, 1), (4, 0)]:
                            decayed(g, s_, d)
                        state_3(g)
                        decayed(g, 4, 1)

                pairs(pool, body)

            @block.vector
            def _(dve):
                dve.sem_inc(e_free, 2)
                dve.sem_inc(bu_used, 4)
                dve.sem_inc(y_done, 2)
                dve.memset(drows[0:KS // 2, 0, :], 0.0).then_inc(d_padded, 1)
                dve.memset(ps[:, 6 * 512:8 * 512], 0.0).then_inc(y_zero, 1)

                def argument(g, j):
                    dve.wait_ge(e_ready, 8 * g + j + 1)
                    dve.tensor_tensor(da[:, j, :], bank(j % 2), expA[:, j % 2, :], ALU.mult).then_inc(e_free, 1)

                def decayed_1(g, d):
                    dve.wait_ge(da_ready, 8 * g + d + 1)
                    if d == 0:
                        dve.wait_ge(y_done, 2 * g + 1)
                    dve.wait_ge(bu_ready, 8 * g + d + 1)
                    dve.tensor_tensor(gb[:, d, :], da[:, d, :], bank(2 + d), ALU.mult).then_inc(bu_used, 1)

                def state(g, s_, d):
                    j = 2 * s_ + d
                    dve.wait_ge(bu_ready, 8 * g + j + 1)
                    if s_ == 1:
                        dve.wait_ge(gp_done, NGP * g + 5 + 2 * d)
                        dve.wait_ge(bu_used, 4 + 7 * g + d + 1)
                    else:
                        dve.wait_ge(gp_done, NGP + NGP * g + 2 * (s_ - 2) + d + 1)
                    dve.tensor_tensor(hb[:, d, s_ % 2, :], gb[:, 2 * (s_ - 1) + d, :], bank(2 + j % 4),
                                      ALU.add).then_inc(bu_used, 1)

                for j in range(4):
                    argument(0, j)
                for d in range(2):
                    decayed_1(0, d)
                argument(0, 4)

                def body(i, first, last):
                    for q in range(2):
                        g = 2 * i + q
                        after = not (last and q == 1)
                        state(g, 1, 0)
                        state(g, 1, 1)
                        argument(g, 5)
                        argument(g, 6)
                        state(g, 2, 0)
                        argument(g, 7)
                        state(g, 2, 1)
                        if after:
                            argument(g + 1, 0)
                        state(g, 3, 0)
                        if after:
                            argument(g + 1, 1)
                            argument(g + 1, 2)
                            argument(g + 1, 3)
                            decayed_1(g + 1, 0)
                            decayed_1(g + 1, 1)
                            argument(g + 1, 4)

                pairs(dve, body)
                for d in range(2):
                    y_sum(dve, d, ORDER[0])
                dve.wait_ge(sum_done, 2)
                for d in range(2):
                    dve.tensor_tensor(skip[:, d, ORDER[0], :], skip[:, d, ORDER[0], :], siluz[:, d, ORDER[0], :],
                                      ALU.mult).then_inc(gated_done, 1)
        scn.close()

        fin = ExitStack()
        ygT = sb("ygT", [P, 2, 2, DC, P], ctx=fin)
        h1 = sb("h1", [P, L, C], ctx=fin)
        xf = sb("xf", [P, L, C], ctx=fin)
        mo = sb("mo", [P, L, C], ctx=fin)
        xfT = sb("xfT", [P, 2, CH, P], ctx=fin)
        fst = sb("fst", [P, L, 6], ctx=fin)
        fmv = sb("fmv", [P, L, 2], ctx=fin)
        fve = sb("fve", [P, L], ctx=fin)
        frs = sb("frs", [P, L], ctx=fin)
        eid = sb("eid", [P, E8], ctx=fin)
        gsco = sb("gsco", [P, L, E8], ctx=fin)
        gtop = sb("gtop", [P, L, E8], ctx=fin)
        gidx = sb("gidx", [P, L, E8], mybir.dt.uint32, ctx=fin)
        gidf = sb("gidf", [P, L], ctx=fin)
        hot = sb("hot", [P, L, E8], ctx=fin)
        ygt_ready, ygt_copied = sem("ygt_ready"), sem("ygt_copied")
        o_ready, h1_ready, fve_ready, frs_ready, xf_ready = (sem("o_ready"), sem("h1_ready"), sem("fve_ready"),
                                                             sem("frs_ready"), sem("xf_ready"))
        xt5_ready, xt5_copied, gate_ready, gate_read = sem("xt5_ready"), sem("xt5_copied"), sem("gate_ready"), sem("gate_read")
        ex5_ready, ex5_used, mo_ready, o_stored, f_chain = (sem("ex5_ready"), sem("ex5_used"), sem("mo_ready"),
                                                            sem("o_stored"), sem("f_chain"))
        with nc.Block() as block:
            @block.sync
            def _(sp):
                for t in range(L):
                    sp.wait_ge(mo_ready, t + 1)
                    sp.dma_start(out[:, ORDER[t], :], mo[:, t, :]).then_inc(o_stored, 16)
                sp.wait_ge(o_stored, 16 * L)

            @block.gpsimd
            def _(pool):
                def root(n):
                    pool.wait_ge(fve_ready, n + 1)
                    pool.tensor_tensor(frs[:, n:n + 1], fve[:, n:n + 1], mhalf[:, 0:1], ALU.pow).then_inc(frs_ready, 1)

                for n in range(1, L):
                    for d in range(2):
                        y_sum(pool, d, ORDER[n])
                    if n == 2:
                        root(0)
                    if n == 3:
                        root(1)
                for n in range(2, L):
                    root(n)

            @block.tensor
            def _(pe):
                def turned(n):
                    for d in range(2):
                        pe.wait_ge(gated_done, 2 * n + d + 1)
                        if n >= 1:
                            pe.wait_ge(ygt_copied, 2 * n + d - 1)
                        for c in range(DC):
                            mm = pe.transpose(bank(d, c * P, (c + 1) * P), skip[:, d, ORDER[n], c * P:(c + 1) * P], ident[:, :])
                        mm.then_inc(ygt_ready, 1)

                def projected(n):
                    if n >= 2:
                        pe.wait_ge(h1_ready, n - 1)
                    for d in range(2):
                        pe.wait_ge(ygt_copied, 2 * n + d + 1)
                        for c in range(DC):
                            mm = pe.matmul(bank(2 + n % 2, 0, C), ygT[:, n % 2, d, c, :], outw[:, d, c, :],
                                           start=(d == 0 and c == 0), stop=(d == 1 and c == DC - 1))
                    mm.then_inc(o_ready, 1)

                def x_turned(n):
                    pe.wait_ge(xf_ready, n + 1)
                    if n >= 1:
                        pe.wait_ge(gate_read, n)
                    for h in range(CH):
                        mm = pe.transpose(bank(7, h * P, (h + 1) * P), xf[:, n, h * P:(h + 1) * P], ident[:, :])
                    mm.then_inc(xt5_ready, 1)

                def experts(n):
                    pe.wait_ge(xt5_copied, n + 1)
                    for h in range(CH):
                        mm = pe.matmul(bank(7, C, C + E8), xfT[:, n % 2, h, :], gatew[:, h, :],
                                       start=(h == 0), stop=(h == CH - 1))
                    mm.then_inc(gate_ready, 1)
                    for k in range(E8 // 2):
                        m = 4 * n + k
                        if m >= 3:
                            pe.wait_ge(ex5_used, m - 2)
                        for h in range(CH):
                            mm = pe.matmul(bank(4 + m % 3), xfT[:, n % 2, h, :], expw[:, h, k * 512:(k + 1) * 512],
                                           start=(h == 0), stop=(h == CH - 1))
                        mm.then_inc(ex5_ready, 1)

                pe.wait_ge(w_landed, 48)
                turned(0)
                projected(0)
                turned(1)
                projected(1)
                turned(2)
                x_turned(0)
                projected(2)
                for n in range(L):
                    if n >= 1:
                        x_turned(n)
                    if n >= 1 and n + 2 < L:
                        turned(n + 2)
                    experts(n)
                    if n >= 1 and n + 2 < L:
                        projected(n + 2)

            @block.scalar
            def _(act):
                def copy_y(n):
                    for d in range(2):
                        act.wait_ge(ygt_ready, 2 * n + d + 1)
                        if n >= 2:
                            act.wait_ge(o_ready, n - 1)
                        act.activation(ygT[:, n % 2, d, :, :], bank(d), ACT.Copy).then_inc(ygt_copied, 1)

                def copy_x(n):
                    act.wait_ge(xt5_ready, n + 1)
                    if n >= 2:
                        act.wait_ge(ex5_ready, 4 * (n - 1))
                    act.activation(xfT[:, n % 2, :, :], bank(7, 0, C), ACT.Copy).then_inc(xt5_copied, 1)

                for n in range(3):
                    copy_y(n)
                copy_x(0)
                for n in range(1, L):
                    copy_x(n)
                    if n + 2 < L:
                        copy_y(n + 2)

            @block.vector
            def _(dve):
                ch = Chain(dve, f_chain)
                for e in range(E8):
                    ins = dve.memset(eid[:, e:e + 1], float(e))
                ch.link(ins)
                sums = [2]

                def gated(n):
                    t = ORDER[n]
                    for d in range(2):
                        if (t, d) not in NIL:
                            sums[0] += 1
                            dve.wait_ge(sum_done, sums[0])
                        dve.tensor_tensor(skip[:, d, t, :], skip[:, d, t, :], siluz[:, d, t, :], ALU.mult).then_inc(gated_done, 1)

                def mixed(n):
                    dve.wait_ge(o_ready, n + 1)
                    dve.scalar_tensor_tensor(out=h1[:, n, :], in0=bank(2 + n % 2, 0, C), scalar=0.5, in1=hbuf[:, ORDER[n], :],
                                             op0=ALU.mult, op1=ALU.add).then_inc(h1_ready, 1)
                    dve.wait_ge(h1_ready, n + 1)
                    ch.link(dve.bn_stats(fst[:, n, :], h1[:, n, :]))
                    ch.link(dve.bn_aggr(fmv[:, n, :], fst[:, n, :]))
                    dve.tensor_scalar(fve[:, n:n + 1], fmv[:, n, 1:2], EPS, None, ALU.add).then_inc(fve_ready, 1)
                    dve.wait_ge(frs_ready, n + 1)
                    dve.tensor_scalar(xf[:, n, :], h1[:, n, :], fmv[:, n, 0:1], frs[:, n:n + 1], ALU.subtract,
                                      ALU.mult).then_inc(xf_ready, 1)
                    dve.wait_ge(xf_ready, n + 1)
                    ch.link(dve.tensor_tensor(mo[:, n, :], h1[:, n, :], xf[:, n, :], ALU.add))

                def chosen(n):
                    dve.wait_ge(gate_ready, n + 1)
                    dve.tensor_copy(gsco[:, n, :], bank(7, C, C + E8)).then_inc(gate_read, 1)
                    dve.wait_ge(gate_read, n + 1)
                    ch.link(dve.max(gtop[:, n, :], gsco[:, n, :]))
                    ch.link(dve.max_index(gidx[:, n, :], gtop[:, n, :], gsco[:, n, :]))
                    ch.link(dve.tensor_copy(gidf[:, n:n + 1], gidx[:, n, 0:1]))
                    ch.link(dve.tensor_scalar(hot[:, n, :], eid[:, :], gidf[:, n:n + 1], None, ALU.is_equal))
                    for k in range(E8 // 2):
                        m = 4 * n + k
                        dve.wait_ge(ex5_ready, m + 1)
                        for e in range(2):
                            ins = dve.scalar_tensor_tensor(out=mo[:, n, :], in0=bank(4 + m % 3, e * C, (e + 1) * C),
                                                           scalar=hot[:, n, 2 * k + e:2 * k + e + 1], in1=mo[:, n, :],
                                                           op0=ALU.mult, op1=ALU.add)
                            if e == 0:
                                ch.link(ins)
                            else:
                                ins.then_inc(ex5_used, 1)
                                dve.wait_ge(ex5_used, m + 1)
                    dve.sem_inc(mo_ready, 1)

                gated(1)
                gated(2)
                mixed(0)
                gated(3)
                mixed(1)
                gated(4)
                for n in range(L):
                    chosen(n)
                    if n + 2 < L:
                        mixed(n + 2)
        fin.close()



def lay_out(x):
    import numpy as np
    g = {k: np.asarray(v) for k, v in x.items()}
    im = g["x"][:, :, :84, :84].reshape(B, 3, 2, 3, 14, 2, 3, 14)
    xT = im.transpose(1, 4, 7, 2, 5, 3, 6, 0).reshape(KP, W4 * WT)
    t = "L0_tok_"
    m = ["L0_attn_f_", "L0_attn_b_"]

    def halves(v):
        return v.reshape(-1, P).T

    def taps(v):
        return v.reshape(DC, P, 4).transpose(1, 0, 2).reshape(P, DC * 4)

    vec_cols = np.concatenate(
        [halves(g[t + n]) for n in ["la_ln_q_g", "la_ln_q_b", "ga_ln_q_g", "ga_ln_q_b", "la_ln_kv_g", "la_ln_kv_b",
                                    "ga_ln_kv_g", "ga_ln_kv_b"]]
        + [halves(g["L0_attn_ln_g"]), halves(g["L0_attn_ln_b"]), halves(g[t + "class_emb"])]
        + [halves(g[p + "conv_b"]) for p in m] + [taps(g[p + "conv_w"]) for p in m]
        + [halves(g[p + "D_skip"]) for p in m], axis=1)
    vec_rows = np.concatenate([g[t + "la_proj_b"], g[t + "mod_b"], g[t + "ga_proj_b"], g[t + "class_emb"]])[None]
    wall = np.concatenate([g[t + n] for n in ["la_wq", "ga_wq", "la_wkv", "ga_wkv"]], axis=1)
    sel = np.zeros((KS // 2 // GB // 2, 2, GB, 2, GB, NS), np.float32)
    for d in range(2):
        for i in range(GB):
            sel[:, d, i, d, i] = 1
    sel = np.concatenate([np.zeros((KS // 2, 2 * P), np.float32), sel.reshape(KS // 2, 2 * P)])
    both = lambda n, f: np.stack([f(g[p + n]) for p in m])
    arrays = {
        "xT": xT, "sel": sel, "conv_wT": g[t + "conv_w"].reshape(C, KP).T, "vec_cols": vec_cols, "vec_rows": vec_rows,
        "wall": wall, "la_proj_w": g[t + "la_proj_w"], "ga_proj_w": g[t + "ga_proj_w"], "mod_w": g[t + "mod_w"],
        "in_wT": both("in_w", lambda v: v.T), "xproj_wT": both("xproj_w", lambda v: v.T),
        "dt_wT": both("dt_w", lambda v: v.T), "dt_b": both("dt_b", lambda v: v[None]),
        "A_logT": both("A_log", lambda v: v.T), "out_wT": both("out_w", lambda v: v.T),
        "gate_wT": g["L0_ffn_gate_w"].T, "expert_wT": g["L0_ffn_expert_w"].transpose(2, 0, 1).reshape(C, E8 * C),
    }
    return {k: np.ascontiguousarray(v) for k, v in arrays.items()}


def kernel(**inputs):
    import numpy as np
    import concourse.bacc as bacc
    from concourse.bass_utils import run_bass_kernel_spmd

    arrays = lay_out(inputs)
    nc = bacc.Bacc("TRN2", target_bir_lowering=False, num_devices=1)
    aps = {n: nc.dram_tensor("in_" + n, v.shape, mybir.dt.from_np(v.dtype), kind="ExternalInput").ap()
           for n, v in arrays.items()}
    out = nc.dram_tensor("out", (B, L, C), F32, kind="ExternalOutput").ap()
    tower(nc, aps, out)
    r = run_bass_kernel_spmd(nc, [{"in_" + n: v for n, v in arrays.items()}], core_ids=[0])
    return r.results[0]["out"]
```
